# Optimizing a Trainium2 kernel written in Bass

```python
import numpy as np
import jax
import jax.numpy as jnp

def _softmax(x, axis=-1):
    return jax.nn.softmax(x, axis=axis)

def _gelu(x):
    return jax.nn.gelu(x, approximate=True)

def _silu(x):
    return jax.nn.silu(x)

def _sigmoid(x):
    return jax.nn.sigmoid(x)

def _layernorm(x, axis=-1, eps=1e-05):
    m = jnp.mean(x, axis=axis, keepdims=True)
    v = jnp.var(x, axis=axis, keepdims=True)
    return (x - m) / jnp.sqrt(v + eps)

def _scatter_add(tgt, idx, src, axis=0):
    return tgt.at[idx].add(src)

def _segment_sum(src, seg, n):
    return jax.ops.segment_sum(src, seg, n)
kernel_name = 'mk_gnn_resnorm_d2_gnn_r64_f4e8ee'

def setup_inputs(seed: int=0):
    np.random.seed(seed)
    _w = jnp.asarray

    def _rec_inputs():
        import jax
        import jax.numpy as jnp
        _gk = jax.random.key(seed)
        x = 0.0001712 + 1 * jax.random.normal(jax.random.fold_in(_gk, 1), (100000, 16), jnp.float32)
        src = jax.random.randint(jax.random.fold_in(_gk, 2), (50000,), 0, 100000, jnp.int32)
        dst = jnp.minimum((100000 * jax.random.uniform(jax.random.fold_in(_gk, 3), (50000,)) ** 2.0).astype(jnp.int32), 99999)
        _o = jnp.argsort(dst, stable=True)
        src = src[_o]
        dst = dst[_o]
        edge_attr_16 = 2.32446e-05 + 1 * jax.random.normal(jax.random.fold_in(_gk, 12), (50000, 16), jnp.float32)
        edge_type_8 = jax.random.randint(jax.random.fold_in(_gk, 14), (50000,), 0, 8, jnp.int32)
        return (x, src, dst, edge_attr_16, edge_type_8)
    x, src, dst, edge_attr_16, edge_type_8 = _rec_inputs()

    def _L0_gnn_setup():
        import jax, jax.numpy as jnp
        import numpy as np
        N_NODES = 50000
        N_EDGES = 500000
        IN_F = 16
        OUT_F = 16
        E_DIM = 16
        key = jax.random.key(seed)
        k1, k2, k3, k4, k5 = jax.random.split(key, 5)
        feat = jax.random.normal(k1, (N_NODES, IN_F), dtype=jnp.float32)
        efeat = jax.random.normal(k2, (N_EDGES, E_DIM), dtype=jnp.float32)
        W_e = jax.random.normal(k3, (E_DIM, IN_F * OUT_F), dtype=jnp.float32) * (1.0 / np.sqrt(E_DIM))
        b_e = jnp.zeros((IN_F * OUT_F,), dtype=jnp.float32)
        bias = jnp.zeros((OUT_F,), dtype=jnp.float32)
        src = jax.random.randint(k4, (N_EDGES,), 0, N_NODES, dtype=jnp.int32)
        dst = jax.random.randint(k5, (N_EDGES,), 0, N_NODES, dtype=jnp.int32)
        return {'feat': feat, 'efeat': efeat, 'W_e': W_e, 'b_e': b_e, 'bias': bias, 'src': src, 'dst': dst}
    _L0_gnn_all = _L0_gnn_setup()
    _L0_gnn_in = {k: v for k, v in _L0_gnn_all.items() if k in ('W_e', 'b_e', 'bias')}
    del _L0_gnn_all

    def _L1_gnn_setup():
        import jax, jax.numpy as jnp
        import numpy as np
        N_NODES = 100000
        N_EDGES = 50000
        NUM_REL = 8

        def _rgcn_layer(x, src, dst, edge_type, W, root, bias):
            out = x @ root + bias
            x_src = x[src]
            for r in range(W.shape[0]):
                mask = (edge_type == r).astype(x.dtype)
                s = jax.ops.segment_sum(x_src * mask[:, None], dst, num_segments=x.shape[0])
                cnt = jax.ops.segment_sum(mask, dst, num_segments=x.shape[0])
                agg = s / jnp.clip(cnt, 1.0)[:, None]
                out = out + agg @ W[r]
            return out
        key = jax.random.key(seed)
        ks = jax.random.split(key, 9)
        x = jax.random.normal(ks[0], (N_NODES, 16), dtype=jnp.float32)
        edge_index = jax.random.randint(ks[1], (2, N_EDGES), 0, N_NODES, dtype=jnp.int32)
        edge_type = jax.random.randint(ks[2], (N_EDGES,), 0, NUM_REL, dtype=jnp.int32)
        s1 = 1.0 / np.sqrt(16.0)
        s2 = 1.0 / np.sqrt(32.0)
        W1 = jax.random.normal(ks[3], (NUM_REL, 16, 32), dtype=jnp.float32) * s1
        root1 = jax.random.normal(ks[4], (16, 32), dtype=jnp.float32) * s1
        b1 = jnp.zeros((32,), dtype=jnp.float32)
        W2 = jax.random.normal(ks[5], (NUM_REL, 32, 16), dtype=jnp.float32) * s2
        root2 = jax.random.normal(ks[6], (32, 16), dtype=jnp.float32) * s2
        b2 = jnp.zeros((16,), dtype=jnp.float32)
        return {'x': x, 'edge_index': edge_index, 'edge_type': edge_type, 'W1': W1, 'root1': root1, 'b1': b1, 'W2': W2, 'root2': root2, 'b2': b2}
    _L1_gnn_all = _L1_gnn_setup()
    _L1_gnn_in = {k: v for k, v in _L1_gnn_all.items() if k in ('W1', 'root1', 'b1', 'W2', 'root2', 'b2')}
    del _L1_gnn_all
    return {'x': x, 'src': src, 'dst': dst, 'edge_attr_16': edge_attr_16, 'edge_type_8': edge_type_8, 'L0_gnn_W_e': _L0_gnn_in['W_e'], 'L0_gnn_b_e': _L0_gnn_in['b_e'], 'L0_gnn_bias': _L0_gnn_in['bias'], 'L1_gnn_W1': _L1_gnn_in['W1'], 'L1_gnn_root1': _L1_gnn_in['root1'], 'L1_gnn_b1': _L1_gnn_in['b1'], 'L1_gnn_W2': _L1_gnn_in['W2'], 'L1_gnn_root2': _L1_gnn_in['root2'], 'L1_gnn_b2': _L1_gnn_in['b2']}

def reference(x, src, dst, edge_attr_16, edge_type_8, L0_gnn_W_e, L0_gnn_b_e, L0_gnn_bias, L1_gnn_W1, L1_gnn_root1, L1_gnn_b1, L1_gnn_W2, L1_gnn_root2, L1_gnn_b2):
    import jax
    import jax.numpy as jnp

    def _L0_gnn_ref(feat, efeat, W_e, b_e, bias, src, dst):
        import jax, jax.numpy as jnp
        import numpy as np
        N_NODES = 50000
        N_EDGES = 500000
        IN_F = 16
        OUT_F = 16
        E_DIM = 16
        E = efeat.shape[0]
        N, in_f = feat.shape
        out_f = bias.shape[0]
        ew = (efeat @ W_e + b_e).reshape(E, in_f, out_f)
        msg = jnp.einsum('ei,eio->eo', feat[src], ew)
        summed = jax.ops.segment_sum(msg, dst, num_segments=N)
        cnt = jax.ops.segment_sum(jnp.ones((E,), feat.dtype), dst, num_segments=N)
        neigh = summed / jnp.maximum(cnt, 1.0)[:, None]
        return neigh + bias

    def _L1_gnn_ref(x, edge_index, edge_type, W1, root1, b1, W2, root2, b2):
        import jax, jax.numpy as jnp
        import numpy as np
        N_NODES = 100000
        N_EDGES = 50000
        NUM_REL = 8

        def _rgcn_layer(x, src, dst, edge_type, W, root, bias):
            out = x @ root + bias
            x_src = x[src]
            for r in range(W.shape[0]):
                mask = (edge_type == r).astype(x.dtype)
                s = jax.ops.segment_sum(x_src * mask[:, None], dst, num_segments=x.shape[0])
                cnt = jax.ops.segment_sum(mask, dst, num_segments=x.shape[0])
                agg = s / jnp.clip(cnt, 1.0)[:, None]
                out = out + agg @ W[r]
            return out
        src, dst = (edge_index[0], edge_index[1])
        h = _rgcn_layer(x, src, dst, edge_type, W1, root1, b1)
        h = jax.nn.relu(h)
        h = _rgcn_layer(h, src, dst, edge_type, W2, root2, b2)
        return h
    edge_index = jnp.stack([src, dst])
    x = _layernorm(x + _L0_gnn_ref(x, edge_attr_16, L0_gnn_W_e, L0_gnn_b_e, L0_gnn_bias, src, dst), axis=-1)
    x = _layernorm(x + _L1_gnn_ref(x, edge_index, edge_type_8, L1_gnn_W1, L1_gnn_root1, L1_gnn_b1, L1_gnn_W2, L1_gnn_root2, L1_gnn_b2), axis=-1)
    return x

_drawn_inputs = setup_inputs


def setup_inputs(seed=0):
    import zlib

    import numpy as np

    out = dict(_drawn_inputs(seed))
    spreads = {'L0_gnn_b_e': (0.0, 0.1),
     'L0_gnn_bias': (0.0, 0.1),
     'L1_gnn_b1': (0.0, 0.1),
     'L1_gnn_b2': (0.0, 0.1)}
    factors = {}
    for name, (base, spread) in spreads.items():
        noise = np.random.default_rng([zlib.crc32(name.encode()), seed]).standard_normal(out[name].shape)
        drawn = base * np.exp(spread * noise) if base else spread * noise
        out[name] = jnp.asarray(drawn.astype(out[name].dtype))
    for name, factor in factors.items():
        out[name] = (out[name] * factor).astype(out[name].dtype)
    return out
```

```python
from contextlib import ExitStack

import numpy as np

import concourse.bass as bass
from concourse import mybir

ALU = mybir.AluOpType
ACT = mybir.ActivationFunctionType
AX = mybir.AxisListType
F32 = mybir.dt.float32
F16 = mybir.dt.float16
BF16 = mybir.dt.bfloat16
I32 = mybir.dt.int32

P = 128
FEAT = 16
HID = 32
REL = 8
EPS = 1e-5
K = 14
GROUPS = 4
PAD = 4 * GROUPS
STEPCOLS = 17
ROW = FEAT + HID + FEAT
HIST = 4


def group_tiles(g):
    return min(4, K - 4 * g)


def bass_gnn_resnorm(nc, x, src, dst, edge_attr, edge_type, W_e, b_e, bias0,
                     W1, root1, b1, W2, root2, b2, out):
    N, _ = x.shape
    E = src.shape[0]
    T = -(-E // (P * 2 * K)) * 2 * K
    EP = P * T
    CHUNKS = T // K
    HALF = CHUNKS // 2
    NPART = 125
    NCOL = N // NPART
    assert NPART * NCOL == N and E <= EP and T % HIST == 0
    FILL = 16
    assert NCOL % FILL == 0
    DC = 40
    DCHUNKS = NCOL // DC
    T8, T4 = DC // 8, DC // 4
    DUMP = N + 1
    NROWS = DUMP + EP + P

    d_src = nc.dram_tensor("edge_src", (EP,), I32, kind="Internal").ap()
    d_dst = nc.dram_tensor("edge_dst", (EP + 2,), I32, kind="Internal").ap()
    d_typ = nc.dram_tensor("edge_typ", (EP,), I32, kind="Internal").ap()
    d_ea = nc.dram_tensor("edge_att", (EP, FEAT), F32, kind="Internal").ap()
    d_xl = nc.dram_tensor("node_x_last", (N, STEPCOLS), F32, kind="Internal").ap()
    d_a0 = nc.dram_tensor("edge_sum0", (EP + P, FEAT), F32, kind="Internal").ap()
    d_a1 = nc.dram_tensor("edge_sum1", (EP + P, HID), F32, kind="Internal").ap()
    d_nodes = nc.dram_tensor("node_sums", (NROWS, ROW), F32, kind="Internal").ap()

    def by_edge(ap):
        return ap.rearrange("(p t) -> p t", p=P)

    def by_edge_row(ap):
        return ap.rearrange("(p t) f -> p t f", p=P)

    d_cur, d_prev, d_next = (by_edge(d_dst[s:s + EP]) for s in (1, 0, 2))
    d_src_t, d_typ_t = by_edge(d_src), by_edge(d_typ)
    d_ea_t = by_edge_row(d_ea)
    d_a0_t, d_a1_t = by_edge_row(d_a0[0:EP, :]), by_edge_row(d_a1[0:EP, :])
    x_t = x.rearrange("(p c) f -> p c f", p=NPART)
    out_t = out.rearrange("(p c) f -> p c f", p=NPART)
    d_xl_t = d_xl.rearrange("(p c) f -> p c f", p=NPART)
    d_nodes_t = d_nodes[0:N, :].rearrange("(p c) f -> p c f", p=NPART)
    NODE_PARTS = (slice(0, 112), slice(112, NPART))

    with ExitStack() as ctx:
        def sb(name, shape, dt=F32):
            return ctx.enter_context(nc.sbuf_tensor(name, shape, dt))

        def psum(name, shape):
            return ctx.enter_context(nc.psum_tensor(name, shape, F32))

        def sem(name):
            return ctx.enter_context(nc.semaphore(name))

        def pair(name, shape, dt=F32):
            return [sb(f"{name}{j}", shape, dt) for j in range(2)]

        ps_turn = psum("ps_turn", [P, 512])
        ps_root = psum("ps_root", [P, 512])
        ps_msg = [psum(f"ps_msg{j}", [P, 1024]) for j in range(2)]
        ps_hist = psum("ps_hist", [P, 1024])

        ident = sb("ident", [P, P])
        iota_lo = sb("iota_lo", [P, NCOL], F16)
        iota_hi = sb("iota_hi", [P, P], F16)
        part_i = sb("part_i", [P, 4], I32)
        part = sb("part", [P, 4])
        dump_row = sb("dump_row", [P, T])
        before = sb("before", [P, P])
        eight = sb("eight", [P, REL])
        ones_t = sb("ones_t", [P, T])
        eps = sb("eps", [P, 1])
        w0 = sb("w0", [P, 4, 256])
        w1 = sb("w1", [P, 4, REL * HID + HID])
        w2 = sb("w2", [P, 4, REL * FEAT])
        wr1 = sb("wr1", [P, 8, HID])
        wr2 = sb("wr2", [P, 4, FEAT])
        bias_row = sb("bias_row", [P, ROW])
        fill = sb("fill", [P, FILL, ROW])
        pad_dst = sb("pad_dst", [1, EP - E + 2], I32)
        pad_i = sb("pad_i", [1, EP - E], I32)
        pad_att = sb("pad_att", [FEAT, EP - E])

        dst0_i = sb("dst0_i", [P, T], I32)
        cur_i = sb("cur_i", [P, T], I32)
        prev_i = sb("prev_i", [P, T], I32)
        next_i = sb("next_i", [P, T], I32)
        typ_i = sb("typ_i", [P, T], I32)
        hi = sb("hi", [P, T])
        lo = sb("lo", [P, T])
        fix = sb("fix", [P, T])
        same = sb("same", [P, T])
        same_next = sb("same_next", [P, T])
        run_up = sb("run_up", [P, T])
        run_down = sb("run_down", [P, T])
        inv_count = sb("inv_count", [P, T])
        first_run = sb("first_run", [P, T])
        last_run = sb("last_run", [P, T])
        node_row = sb("node_row", [P, T], I32)
        last_of_src = sb("last_of_src", [P, T], I32)
        x_src = sb("x_src", [P, T, FEAT])
        rel = sb("rel", [P, T, REL])
        arena = sb("arena", [P, NCOL * STEPCOLS])
        xl = arena[0:NPART, :].rearrange("p (c f) -> p c f", f=STEPCOLS)
        u_src = arena[:, 0:T * HID].rearrange("p (t f) -> p t f", f=HID)
        spare = x_src[:, :, :].rearrange("p t f -> p (t f)")
        iota_i = spare[:, 0:NCOL].bitcast(I32)
        count_step = spare[0:NPART, NCOL:2 * NCOL]
        last_edge = spare[0:NPART, 2 * NCOL:3 * NCOL]
        ends = spare[0:NPART, 3 * NCOL:4 * NCOL + 1]
        edge_i = last_of_src
        hi_i = node_row
        steps = rel[:, :, :].rearrange("p t f -> p (t f)").bitcast(BF16)[:, 0:HIST * NCOL]
        steps = steps.rearrange("p (s c) -> p s c", s=HIST)

        small = sb("small", [P, 8])
        total = sb("total", [P, 1])
        carry_row = sb("carry_row", [P, 1], I32)
        carry_node = sb("carry_node", [P, 1], I32)
        whole = sb("whole", [P, 2])
        whole32 = sb("whole32", [P, 2, HID])
        whole_rows = sb("whole_rows", [HID, 2, P])
        tail = sb("tail", [P, HID])
        tail_row = sb("tail_row", [HID, P])
        carry_out = sb("carry_out", [HID, P + 1])
        carry = [sb(f"carry{d}", [P, HID]) for d in range(2)]
        heads = sb("heads", [P, REL])
        up8 = sb("up8", [P, REL])
        down8 = sb("down8", [P, REL])
        carry64 = sb("carry64", [P, ROW])
        hot = sb("hot", [P, HIST, P], BF16)

        idx = pair("idx", [P, K], I32)
        sidx = pair("sidx", [P, K], I32)
        got0 = pair("got0", [P, K, STEPCOLS])
        got1 = pair("got1", [P, K, FEAT])
        got2 = pair("got2", [P, K, HID])
        att = pair("att", [P, K, FEAT])
        padded = sb("padded", [P, PAD, HID])
        turned = sb("turned", [P, GROUPS * P])
        xc = sb("xc", [P, K, FEAT])
        sq = sb("sq", [P, K, FEAT])
        cen = sb("cen", [P, K, FEAT])
        stat = sb("stat", [P, 4, K])
        hsum = sb("hsum", [P, K, HID])
        prod = pair("prod", [P, 1024])
        keep = pair("keep", [P, HID, K + 1])
        part_sum = pair("part_sum", [P, HID, K + 1])
        scanned = pair("scanned", [P, HID, K + 1])
        rows = pair("rows", [P, K * HID])
        old0 = pair("old0", [P, K, FEAT])
        old1 = pair("old1", [P, K, HID])
        node_rows = pair("node_rows", [P, K, ROW])

        at = 0

        def dense(n, cols):
            nonlocal at
            got = arena[0:n, at:at + cols]
            at += cols
            return got

        nr = [dense(NPART, DC * ROW).rearrange("p (c f) -> p c f", f=ROW) for j in range(2)]
        xn = [dense(NPART, DC * FEAT).rearrange("p (c f) -> p c f", f=FEAT) for j in range(2)]
        res = [dense(NPART, DC * FEAT).rearrange("p (c f) -> p c f", f=FEAT) for j in range(2)]
        vv, v2, x1n = (dense(NPART, DC * FEAT).rearrange("p (c f) -> p c f", f=FEAT) for _ in range(3))
        x1t = dense(P, T8 * NPART)
        hn = dense(NPART, DC * HID).rearrange("p (c f) -> p c f", f=HID)
        ht = dense(P, T4 * NPART)
        assert at <= NCOL * STEPCOLS
        dstat = sb("dstat", [P, 4, DC])

        iotas_made = sem("iotas_made")
        zeroed = sem("zeroed")
        consts_made = sem("consts_made")
        dve_prep = sem("dve_prep")
        weights_in = sem("weights_in")
        bias_in = sem("bias_in")
        fill_made = sem("fill_made")
        pads_made = sem("pads_made")
        filled = sem("filled")
        edges_copied = sem("edges_copied")
        dst_copied = sem("dst_copied")
        dst0_in = sem("dst0_in")
        edges_in = sem("edges_in")
        digits = sem("digits")
        hot_ready = sem("hot_ready")
        hot_used = sem("hot_used")
        hist_done = sem("hist_done")
        total_ready = sem("total_ready")
        base_ready = sem("base_ready")
        last_step = sem("last_step")
        x_in = [sem(f"x_in{j}") for j in range(2)]
        x_placed = [sem(f"x_placed{j}") for j in range(2)]
        xl_stored = sem("xl_stored")
        prep = sem("prep")
        prep_done = sem("prep_done")
        begun = sem("begun")
        lists_free = sem("lists_free")
        turn_ready = sem("turn_ready")
        turn_done = sem("turn_done")
        row_ready = sem("row_ready")
        row_turned = sem("row_turned")
        row_copied = sem("row_copied")
        scan_ready = sem("scan_ready")
        back_done = sem("back_done")
        carry_ready = sem("carry_ready")
        carry_added = sem("carry_added")
        nodes_idx_in = [sem(f"nodes_idx_in{j}") for j in range(2)]

        def layer_sems(n, single, paired):
            s = {m: sem(f"l{n}_{m}") for m in single.split()}
            s.update({m: [sem(f"l{n}_{m}{j}") for j in range(2)] for m in paired.split()})
            return s

        L0, L1, L2 = (layer_sems(n, "turned turned_sb msg reduced state" + more,
                                 "idx_in got padded mask mult scan rows stored" + pairs)
                      for n, more, pairs in ((0, "", " att_in saved scaled"), (1, " stat std inv root_saved", " sum"),
                                             (2, "", " att_in saved sum")))
        D = layer_sems("d", "stat center std inv x1 x1t x1t_sb h_mm h ht ht_sb y", "in out h_sum y_read result")

        CARRIES = (0, 1, 0, 0, 1, 0, 0)
        CONSTS, LAST_STEPS = 18, 7

        def chunk(k):
            return bass.ds(k * K, K)

        def back(ap):
            dims = [list(d) for d in ap.ap]
            n, step = dims[-1][1], dims[-1][0]
            dims[-1] = [-step, n]
            return bass.AP(ap.tensor, ap.offset + (n - 1) * step, dims)

        def over_rows(ap, n, f):
            return ap.unsqueeze(1).to_broadcast([ap.shape[0], n, f])

        def over_last(ap, f):
            return ap.unsqueeze(len(ap.shape)).to_broadcast([*ap.shape, f])

        block = ctx.enter_context(nc.Block())

        GOT = 16 * K
        FILLED = 16 * (2 + 2 * (NCOL // FILL))

        @block.sync
        def _(sp):
            sp.dma_start(d_dst[1:1 + E].rearrange("(a b) -> a b", a=80),
                         dst.rearrange("(a b) -> a b", a=80)).then_inc(dst_copied, 16)
            sp.wait_ge(pads_made, 4)
            sp.dma_start(d_dst[1 + E:EP + 2].rearrange("(a b) -> a b", a=1),
                         pad_dst[:, 0:EP - E + 1]).then_inc(dst_copied, 16)
            sp.dma_start(d_dst[0:1].rearrange("(a b) -> a b", a=1),
                         pad_dst[:, EP - E + 1:]).then_inc(dst_copied, 16)
            sp.wait_ge(dst_copied, 48)
            sp.dma_start(dst0_i[:, :], d_cur).then_inc(dst0_in, 16)
            sp.dma_start(d_src[0:E].rearrange("(a b) -> a b", a=80),
                         src.rearrange("(a b) -> a b", a=80)).then_inc(edges_copied, 16)
            sp.dma_start(d_typ[0:E].rearrange("(a b) -> a b", a=80),
                         edge_type.rearrange("(a b) -> a b", a=80)).then_inc(edges_copied, 16)
            sp.dma_start(d_src[E:EP].rearrange("(a b) -> a b", a=1), pad_i[:, :]).then_inc(edges_copied, 16)
            sp.dma_start(d_typ[E:EP].rearrange("(a b) -> a b", a=1), pad_i[:, :]).then_inc(edges_copied, 16)
            sp.dma_start(d_ea[0:E, :].rearrange("(a b) f -> a (b f)", a=80),
                         edge_attr.rearrange("(a b) f -> a (b f)", a=80)).then_inc(edges_copied, 16)
            sp.dma_start(d_ea[E:EP, :].rearrange("(a b) f -> a (b f)", a=FEAT),
                         pad_att[:, :]).then_inc(edges_copied, 16)
            sp.wait_ge(edges_copied, 96)
            for to, of in ((cur_i, d_cur), (prev_i, d_prev), (next_i, d_next), (typ_i, d_typ_t)):
                sp.dma_start(to[:, :], of).then_inc(edges_in, 16)

            with sp.Fori(0, DCHUNKS // 2) as i:
                for j in range(2):
                    sp.wait_ge(x_placed[j], i)
                    for ps in NODE_PARTS:
                        sp.dma_start(node_rows[j][ps, :, :].rearrange("p k f -> p (k f)")[:, 0:DC * FEAT],
                                     x_t[ps, bass.ds((i * 2 + j) * DC, DC), :]
                                     .rearrange("p c f -> p (c f)")).then_inc(x_in[j], 16)

            sp.wait_ge(fill_made, 1)
            sp.dma_start(d_a0[EP:EP + P, :], bias_row[:, 0:FEAT]).then_inc(filled, 16)
            sp.dma_start(d_a1[EP:EP + P, :], bias_row[:, FEAT:FEAT + HID]).then_inc(filled, 16)
            with sp.Fori(0, NCOL // FILL) as i:
                for ps in NODE_PARTS:
                    sp.dma_start(d_nodes_t[ps, bass.ds(i * FILL, FILL), :], fill[ps, :, :]).then_inc(filled, 16)

            sp.wait_ge(last_step, LAST_STEPS)
            for ps in NODE_PARTS:
                sp.dma_start(d_xl_t[ps, :, :], xl[ps, :, :]).then_inc(xl_stored, 16)

            def loads0(j, i):
                k = i * 2 + j
                sp.wait_ge(L0["got"][j], GOT * i)
                sp.dma_start(idx[j][:, :], d_src_t[:, chunk(k)]).then_inc(L0["idx_in"][j], 16)
                sp.wait_ge(L0["padded"][j], i)
                sp.dma_start(att[j][:, :, :], d_ea_t[:, chunk(k), :]).then_inc(L0["att_in"][j], 16)

            def store0(j, i):
                k = i * 2 + j
                sp.wait_ge(L0["rows"][j], i + 1)
                sp.dma_start(d_a0_t[:, chunk(k), :],
                             rows[j][:, 0:K * FEAT].rearrange("p (k f) -> p k f", k=K)).then_inc(L0["stored"][j], 16)

            loads0(0, 0)
            with sp.Fori(0, HALF - 1) as i:
                loads0(1, i)
                store0(0, i)
                loads0(0, i + 1)
                store0(1, i)
            loads0(1, HALF - 1)
            store0(0, HALF - 1)
            store0(1, HALF - 1)

            def loads1(j, i):
                k = i * 2 + j
                sp.wait_ge(L1["got"][j], GOT * i)
                sp.dma_start(idx[j][:, :], last_of_src[:, chunk(k)]).then_inc(L1["idx_in"][j], 16)

            def store1(j, i):
                k = i * 2 + j
                sp.wait_ge(L1["rows"][j], i + 1)
                sp.dma_start(d_a1_t[:, chunk(k), :],
                             rows[j][:, :].rearrange("p (k f) -> p k f", k=K)).then_inc(L1["stored"][j], 16)

            sp.wait_ge(L0["got"][0], GOT * HALF)
            sp.wait_ge(L0["got"][1], GOT * HALF)
            sp.wait_ge(L0["saved"][0], 2 * HALF)
            sp.wait_ge(L0["saved"][1], 2 * HALF)
            loads1(0, 0)
            with sp.Fori(0, HALF - 1) as i:
                loads1(1, i)
                store1(0, i)
                loads1(0, i + 1)
                store1(1, i)
            loads1(1, HALF - 1)
            store1(0, HALF - 1)
            store1(1, HALF - 1)

            def loads2(j, i):
                k = i * 2 + j
                sp.wait_ge(L2["got"][j], GOT * i)
                sp.dma_start(idx[j][:, :], last_of_src[:, chunk(k)]).then_inc(L2["idx_in"][j], 16)
                sp.wait_ge(L2["saved"][j], 2 * i)
                sp.dma_start(old0[j][:, :, :], d_a0_t[:, chunk(k), :]).then_inc(L2["att_in"][j], 16)
                sp.dma_start(old1[j][:, :, :], d_a1_t[:, chunk(k), :]).then_inc(L2["att_in"][j], 16)
                sp.wait_ge(L2["stored"][j], GOT * i)
                sp.sem_inc(lists_free, 1)
                sp.dma_start(sidx[j][:, :], node_row[:, chunk(k)]).then_inc(nodes_idx_in[j], 16)

            sp.wait_ge(L1["got"][0], GOT * HALF)
            sp.wait_ge(L1["got"][1], GOT * HALF)
            sp.wait_ge(carry_added, 32)
            loads2(0, 0)
            with sp.Fori(0, HALF - 1) as i:
                loads2(1, i)
                loads2(0, i + 1)
            loads2(1, HALF - 1)

            sp.wait_ge(carry_added, 48)
            sp.wait_ge(L2["sum"][0], HALF)
            sp.wait_ge(L2["sum"][1], HALF)

            def loadn(j, i):
                cols = bass.ds((i * 2 + j) * DC, DC)
                sp.wait_ge(D["y_read"][j], i)
                for ps in NODE_PARTS:
                    sp.dma_start(nr[j][ps, :, :], d_nodes_t[ps, cols, :]).then_inc(D["in"][j], 16)
                    sp.dma_start(xn[j][ps, :, :], x_t[ps, cols, :]).then_inc(D["in"][j], 16)

            def storen(j, i):
                cols = bass.ds((i * 2 + j) * DC, DC)
                sp.wait_ge(D["result"][j], i + 1)
                for ps in NODE_PARTS:
                    sp.dma_start(out_t[ps, cols, :], res[j][ps, :, :]).then_inc(D["out"][j], 16)

            loadn(0, 0)
            with sp.Fori(0, DCHUNKS // 2 - 1) as i:
                loadn(1, i)
                storen(0, i)
                loadn(0, i + 1)
                storen(1, i)
            loadn(1, DCHUNKS // 2 - 1)
            storen(0, DCHUNKS // 2 - 1)
            storen(1, DCHUNKS // 2 - 1)
            sp.wait_ge(D["out"][0], 32 * (DCHUNKS // 2))
            sp.wait_ge(D["out"][1], 32 * (DCHUNKS // 2))

        @block.gpsimd
        def _(pool):
            pool.memset(pad_dst[:, 0:EP - E], N).then_inc(pads_made, 1)
            pool.memset(pad_dst[:, EP - E:], -1).then_inc(pads_made, 1)
            pool.memset(pad_i[:, :], 0).then_inc(pads_made, 1)
            pool.memset(pad_att[:, :], 0.0).then_inc(pads_made, 1)
            pool.iota(iota_i, [[1, NCOL]], base=0, channel_multiplier=0).then_inc(iotas_made, 1)
            for n, (base, times) in enumerate(((0, 1), (0, T), (EP, 1), (DUMP + EP, 1))):
                pool.iota(part_i[:, n:n + 1], [[0, 1]], base=base, channel_multiplier=times).then_inc(iotas_made, 1)
            pool.iota(edge_i[:, :], [[1, T]], base=DUMP, channel_multiplier=T).then_inc(iotas_made, 1)

            def gather(layer, table, to, j, i, freed, complete):
                pool.wait_ge(layer["idx_in"][j], 16 * (i + 1))
                for free, n in freed:
                    pool.wait_ge(layer[free][j], n * i)
                pool.wait_ge(*complete)
                pool.sem_inc(begun, 1)
                for t in range(K):
                    pool.indirect_dma_start(
                        out=to[j][:, t, :], out_offset=None, in_=table,
                        in_offset=bass.IndirectOffsetOnAxis(ap=idx[j][:, t:t + 1], axis=0),
                    ).then_inc(layer["got"][j], 16)

            def scatter(j, i):
                pool.wait_ge(nodes_idx_in[j], 16 * (i + 1))
                pool.wait_ge(L2["saved"][j], 2 * (i + 1))
                pool.wait_ge(L2["rows"][j], i + 1)
                pool.wait_ge(filled, FILLED)
                pool.sem_inc(begun, 1)
                for t in range(K):
                    pool.indirect_dma_start(
                        out=d_nodes[:, :], out_offset=bass.IndirectOffsetOnAxis(ap=sidx[j][:, t:t + 1], axis=0),
                        in_=node_rows[j][:, t, :], in_offset=None,
                    ).then_inc(L2["stored"][j], 16)

            def add_carry(n, table, rows_of, what):
                pool.wait_ge(carry_ready, n + 1)
                pool.indirect_dma_start(
                    out=table, out_offset=bass.IndirectOffsetOnAxis(ap=rows_of[:, 0:1], axis=0),
                    in_=what, in_offset=None, compute_op=ALU.add,
                ).then_inc(carry_added, 16)

            pool.wait_ge(xl_stored, 32)
            with pool.Fori(0, HALF) as i:
                for j in range(2):
                    gather(L0, d_xl[:, :], got0, j, i, (("saved", 2), ("scaled", 1)), (xl_stored, 32))
            pool.wait_ge(L0["stored"][0], 16 * HALF)
            pool.wait_ge(L0["stored"][1], 16 * HALF)
            add_carry(0, d_a0[:, :], carry_row, carry[0][:, 0:FEAT])
            pool.wait_ge(carry_added, 16)
            pool.wait_ge(filled, FILLED)

            with pool.Fori(0, HALF) as i:
                for j in range(2):
                    gather(L1, d_a0[:, :], got1, j, i, (("sum", 1),), (carry_added, 16))
            pool.wait_ge(L1["stored"][0], 16 * HALF)
            pool.wait_ge(L1["stored"][1], 16 * HALF)
            add_carry(1, d_a1[:, :], carry_row, carry[0][:, 0:HID])
            pool.wait_ge(carry_added, 32)

            gather(L2, d_a1[:, :], got2, 0, 0, (("sum", 1),), (carry_added, 32))
            with pool.Fori(0, HALF - 1) as i:
                gather(L2, d_a1[:, :], got2, 1, i, (("sum", 1),), (carry_added, 32))
                scatter(0, i)
                gather(L2, d_a1[:, :], got2, 0, i + 1, (("sum", 1),), (carry_added, 32))
                scatter(1, i)
            gather(L2, d_a1[:, :], got2, 1, HALF - 1, (("sum", 1),), (carry_added, 32))
            scatter(0, HALF - 1)
            scatter(1, HALF - 1)
            pool.wait_ge(L2["stored"][0], GOT * HALF)
            pool.wait_ge(L2["stored"][1], GOT * HALF)
            add_carry(2, d_nodes[:, :], carry_node, carry64[:, :])

        @block.tensor
        def _(pe):
            pe.wait_ge(consts_made, CONSTS)

            def count_group(g, first, last):
                for s in range(HIST):
                    pe.wait_ge(hot_ready, g * HIST + s + 1)
                    for h in range(2):
                        mm = pe.matmul(ps_hist[0:NPART, 512 * h:512 * h + NCOL // 2], hot[:, s, 0:NPART],
                                       steps[:, s, h * NCOL // 2:(h + 1) * NCOL // 2],
                                       start=first and s == 0, stop=last and s == HIST - 1)
                    mm.then_inc(hot_used, 1)

            count_group(0, True, False)
            with pe.Fori(1, T // HIST - 1) as g:
                count_group(g, False, False)
            count_group(T // HIST - 1, False, True)
            pe.wait_ge(total_ready, 1)
            pe.matmul(ps_root[0:NPART, 0:1], before[0:NPART, 0:NPART], total[0:NPART, :],
                      start=True, stop=True).then_inc(base_ready, 1)
            pe.wait_ge(turn_ready, 1)
            for d in range(2):
                mm = pe.transpose(ps_turn[0:HID, d * P:(d + 1) * P], whole32[:, d, :], ident[:, :])
            mm.then_inc(turn_done, 1)

            def carry_turns(n):
                pe.wait_ge(row_ready, n + 1)
                pe.transpose(ps_root[0:HID, 0:P], tail[:, :], ident[:, :]).then_inc(row_turned, 1)
                pe.wait_ge(scan_ready, n + 1)
                at = 1 if CARRIES[n] else 0
                pe.transpose(ps_root[:, 256:256 + HID], carry_out[:, at:at + P], ident[0:HID, 0:HID]) \
                    .then_inc(back_done, 1)

            carry_turns(0)
            carry_turns(1)

            def turn_chunk(layer, j, i):
                k = i * 2 + j
                pe.wait_ge(layer["padded"][j], i + 1)
                pe.wait_ge(layer["turned_sb"], k)
                for g in range(GROUPS):
                    mm = pe.transpose(ps_turn[:, g * P:(g + 1) * P],
                                      padded[:, 4 * g:4 * g + 4, :].rearrange("p t f -> p (t f)"), ident[:, :])
                mm.then_inc(layer["turned"], 1)

            pe.wait_ge(weights_in, 16 * 32)

            def layer0(j, i):
                k = i * 2 + j
                turn_chunk(L0, j, i)
                pe.wait_ge(L0["turned_sb"], k + 1)
                for g in range(GROUPS):
                    pe.wait_ge(L0["mult"][g % 2], 2 * k + g // 2)
                    for t in range(group_tiles(g)):
                        mm = pe.matmul(ps_msg[g % 2][:, 256 * t:256 * t + 256], turned[:, g * P:(g + 1) * P],
                                       w0[:, t, :], start=True, stop=True)
                    mm.then_inc(L0["msg"], 1)

            with pe.Fori(0, HALF) as i:
                layer0(0, i)
                layer0(1, i)
            for n in range(2, 5):
                carry_turns(n)

            def layer1(j, i):
                k = i * 2 + j
                turn_chunk(L1, j, i)
                pe.wait_ge(L1["turned_sb"], k + 1)
                for g in range(GROUPS):
                    pe.wait_ge(L1["mult"][g % 2], 2 * k + g // 2)
                    if g == 0:
                        pe.wait_ge(L1["root_saved"], k)
                    for t in range(group_tiles(g)):
                        turns = turned[:, g * P:(g + 1) * P]
                        pe.matmul(ps_msg[g % 2][:, 256 * t:256 * t + 256], turns,
                                  w1[:, t, 0:REL * HID], start=True, stop=True)
                        tile = 4 * g + t
                        mm = pe.matmul(ps_root[:, tile * HID:(tile + 1) * HID], turns,
                                       w1[:, t, REL * HID:], start=True, stop=True)
                    mm.then_inc(L1["msg"], 1)

            with pe.Fori(0, HALF) as i:
                layer1(0, i)
                layer1(1, i)
            pe.wait_ge(L1["root_saved"], CHUNKS)
            carry_turns(5)

            def layer2(j, i):
                k = i * 2 + j
                turn_chunk(L2, j, i)
                pe.wait_ge(L2["turned_sb"], k + 1)
                for g in range(GROUPS):
                    pe.wait_ge(L2["mult"][g % 2], 2 * k + g // 2)
                    for t in range(group_tiles(g)):
                        mm = pe.matmul(ps_msg[g % 2][:, P * t:P * t + P], turned[:, g * P:(g + 1) * P],
                                       w2[:, t, :], start=True, stop=True)
                    mm.then_inc(L2["msg"], 1)

            with pe.Fori(0, HALF) as i:
                layer2(0, i)
                layer2(1, i)
            carry_turns(6)

            idn = ident[0:NPART, 0:NPART]

            def dense_chunk(j, i):
                k = i * 2 + j
                pe.wait_ge(D["x1"], k + 1)
                for h in range(2):
                    pe.wait_ge(D["x1t_sb"], 2 * k + h)
                    for m in range(4 * h, min(4 * h + 4, T8)):
                        mm = pe.transpose(ps_turn[:, (m % 4) * NPART:(m % 4 + 1) * NPART],
                                          x1n[:, 8 * m:8 * m + 8, :].rearrange("p c f -> p (c f)"), idn)
                    mm.then_inc(D["x1t"], 1)
                pe.wait_ge(D["x1t_sb"], 2 * k + 2)
                for m in range(T8):
                    if m % 2 == 0:
                        pe.wait_ge(D["h_sum"][m // 2 % 2], (2 if m // 2 % 2 == 0 else 1) * k + m // 4)
                    mm = pe.matmul(ps_msg[m // 2 % 2][0:NPART, 256 * (m % 2):256 * (m % 2) + 256],
                                   x1t[:, m * NPART:(m + 1) * NPART], wr1[:, :, :].rearrange("p c f -> p (c f)"),
                                   start=True, stop=True)
                    if m % 2 == 1 or m == T8 - 1:
                        mm.then_inc(D["h_mm"], 1)
                pe.wait_ge(D["h"], k + 1)
                for h in range(3):
                    pe.wait_ge(D["ht_sb"], 3 * k + h)
                    for m in range(4 * h, min(4 * h + 4, T4)):
                        mm = pe.transpose(ps_root[:, (m % 4) * NPART:(m % 4 + 1) * NPART],
                                          hn[:, 4 * m:4 * m + 4, :].rearrange("p c f -> p (c f)"), idn)
                    mm.then_inc(D["ht"], 1)
                pe.wait_ge(D["ht_sb"], 3 * k + 3)
                pe.wait_ge(D["y_read"][1 - j], i + j)
                for m in range(T4):
                    mm = pe.matmul(ps_hist[0:NPART, 512 * (m // 8) + 64 * (m % 8):512 * (m // 8) + 64 * (m % 8) + 64],
                                   ht[:, m * NPART:(m + 1) * NPART], wr2[:, :, :].rearrange("p c f -> p (c f)"),
                                   start=True, stop=True)
                mm.then_inc(D["y"], 1)

            with pe.Fori(0, DCHUNKS // 2) as i:
                dense_chunk(0, i)
                dense_chunk(1, i)

        @block.scalar
        def _(act):
            act.wait_ge(zeroed, 5)
            for j in range(4):
                block_rows = slice(32 * j, 32 * j + FEAT)
                act.dma_start(w0[block_rows, j, :], W_e).then_inc(weights_in, 16)
                act.dma_start(w0[32 * j + FEAT:32 * j + FEAT + 1, j, :],
                              b_e.rearrange("(a f) -> a f", a=1)).then_inc(weights_in, 16)
                act.dma_start(w1[block_rows, j, 0:REL * HID].rearrange("p (r o) -> p r o", r=REL),
                              W1.rearrange("r i o -> i r o")).then_inc(weights_in, 16)
                act.dma_start(w1[block_rows, j, REL * HID:], root1).then_inc(weights_in, 16)
                act.dma_start(w2[32 * j:32 * j + HID, j, :].rearrange("p (r o) -> p r o", r=REL),
                              W2.rearrange("r i o -> i r o")).then_inc(weights_in, 16)
                act.dma_start(wr2[32 * j:32 * j + HID, j, :], root2).then_inc(weights_in, 16)
            for m in range(8):
                act.dma_start(wr1[FEAT * m:FEAT * m + FEAT, m, :], root1).then_inc(weights_in, 16)
            for c, n, b in ((0, FEAT, bias0), (FEAT, HID, b1), (FEAT + HID, FEAT, b2)):
                act.dma_start(bias_row[:, c:c + n],
                              b.rearrange("(a f) -> a f", a=1).to_broadcast([P, n])).then_inc(bias_in, 16)

            with act.Fori(0, DCHUNKS // 2) as i:
                for j in range(2):
                    act.wait_ge(x_in[j], 32 * (i + 1))
                    act.wait_ge(zeroed, 5)
                    act.activation(xl[:, bass.ds((i * 2 + j) * DC, DC), 0:FEAT],
                                   node_rows[j][0:NPART, :, :].rearrange("p k f -> p (k f)")[:, 0:DC * FEAT]
                                   .rearrange("p (c f) -> p c f", f=FEAT), ACT.Copy).then_inc(x_placed[j], 1)

            def runs_go_on(layer, j, i, f):
                act.wait_ge(layer["scan"][j], i)
                act.wait_ge(prep_done, 1)
                act.activation(keep[j][:, 0:f, 1:], over_rows(same[:, chunk(i * 2 + j)], f, K),
                               ACT.Copy).then_inc(layer["mask"][j], 1)

            def copy_turns(layer, k):
                act.wait_ge(layer["turned"], k + 1)
                act.wait_ge(layer["msg"], 4 * k)
                act.activation(turned[:, :], ps_turn[:, :], ACT.Copy).then_inc(layer["turned_sb"], 1)

            def layer0(j, i):
                k = i * 2 + j
                act.wait_ge(L0["att_in"][j], 16 * (i + 1))
                act.wait_ge(L0["turned"], k)
                act.activation(padded[:, 0:K, 0:FEAT], att[j][:, :, :], ACT.Copy).then_inc(L0["padded"][j], 1)
                copy_turns(L0, k)
                runs_go_on(L0, j, i, FEAT)
                act.wait_ge(L0["got"][j], GOT * (i + 1))
                act.wait_ge(prep_done, 1)
                act.activation(x_src[:, chunk(k), :], got0[j][:, :, 0:FEAT], ACT.Copy).then_inc(L0["saved"][j], 1)
                act.activation(last_of_src[:, chunk(k)], got0[j][:, :, FEAT], ACT.Copy).then_inc(L0["saved"][j], 1)

            with act.Fori(0, HALF) as i:
                layer0(0, i)
                layer0(1, i)

            act.wait_ge(L0["scan"][0], HALF)
            act.wait_ge(L0["scan"][1], HALF)
            def layer1(j, i):
                k = i * 2 + j
                runs_go_on(L1, j, i, HID)
                act.wait_ge(L1["stat"], 4 * k + 4)
                act.activation(stat[:, 2, :], stat[:, 1, :], ACT.Sqrt, bias=eps[:, :], scale=1.0 / FEAT) \
                    .then_inc(L1["std"], 1)
                copy_turns(L1, k)
                act.wait_ge(L1["msg"], 4 * k + 4)
                act.wait_ge(prep_done, 1)
                act.activation(u_src[:, chunk(k), :], ps_root[:, 0:K * HID].rearrange("p (k f) -> p k f", k=K),
                               ACT.Copy).then_inc(L1["root_saved"], 1)

            with act.Fori(0, HALF) as i:
                layer1(0, i)
                layer1(1, i)

            act.wait_ge(L1["scan"][0], HALF)
            act.wait_ge(L1["scan"][1], HALF)
            def layer2(j, i):
                k = i * 2 + j
                runs_go_on(L2, j, i, FEAT)
                act.wait_ge(L2["turned"], k)
                act.wait_ge(L2["sum"][j], i + 1)
                act.activation(padded[:, 0:K, :], hsum[:, :, :], ACT.Relu).then_inc(L2["padded"][j], 1)
                copy_turns(L2, k)
                act.wait_ge(L2["att_in"][j], 32 * (i + 1))
                act.wait_ge(L2["stored"][j], GOT * i)
                act.activation(node_rows[j][:, :, 0:FEAT], old0[j][:, :, :], ACT.Copy).then_inc(L2["saved"][j], 1)
                act.activation(node_rows[j][:, :, FEAT:FEAT + HID], old1[j][:, :, :], ACT.Copy) \
                    .then_inc(L2["saved"][j], 1)

            with act.Fori(0, HALF) as i:
                layer2(0, i)
                layer2(1, i)

            def deviation(n):
                act.wait_ge(D["stat"], n)
                act.activation(dstat[0:NPART, 2, :], dstat[0:NPART, 1, :], ACT.Sqrt,
                               bias=eps[0:NPART, :], scale=1.0 / FEAT).then_inc(D["std"], 1)

            def dense_chunk(j, i):
                k = i * 2 + j
                deviation(8 * k + 4)
                for h in range(2):
                    a, b = 4 * h * NPART, min(4 * h + 4, T8) * NPART
                    act.wait_ge(D["x1t"], 2 * k + h + 1)
                    act.activation(x1t[:, a:b], ps_turn[:, 0:b - a], ACT.Copy).then_inc(D["x1t_sb"], 1)
                act.wait_ge(D["h_sum"][0], 2 * k + 2)
                act.wait_ge(D["h_sum"][1], k + 1)
                act.activation(hn, hn, ACT.Relu).then_inc(D["h"], 1)
                for h in range(3):
                    a, b = 4 * h * NPART, min(4 * h + 4, T4) * NPART
                    act.wait_ge(D["ht"], 3 * k + h + 1)
                    act.activation(ht[:, a:b], ps_root[:, 0:b - a], ACT.Copy).then_inc(D["ht_sb"], 1)
                deviation(8 * k + 8)

            with act.Fori(0, DCHUNKS // 2) as i:
                dense_chunk(0, i)
                dense_chunk(1, i)

        @block.vector
        def _(dve):
            for w in (w0, w1, w2, wr1, wr2):
                dve.memset(w[:, :, :], 0.0).then_inc(zeroed, 1)
            dve.memset(ones_t[:, :], 1.0).then_inc(consts_made, 1)
            dve.memset(eps[:, :], EPS).then_inc(consts_made, 1)
            dve.memset(tail[:, :], 0.0).then_inc(consts_made, 1)
            dve.memset(carry_out[:, :], 0.0).then_inc(consts_made, 1)
            dve.memset(carry64[:, :], 0.0).then_inc(consts_made, 1)
            dve.memset(padded[:, :, :], 0.0).then_inc(consts_made, 1)
            for j in range(2):
                dve.memset(keep[j][:, :, 0:1], 0.0).then_inc(consts_made, 1)
                dve.memset(scanned[j][:, :, :], 0.0).then_inc(consts_made, 1)
            dve.wait_ge(consts_made, 10)
            dve.memset(padded[:, :, FEAT:FEAT + 1], 1.0).then_inc(consts_made, 1)
            dve.wait_ge(iotas_made, 6)
            dve.tensor_copy(iota_lo[:, :], iota_i).then_inc(consts_made, 1)
            dve.tensor_copy(iota_hi[:, :], iota_i[:, 0:P]).then_inc(consts_made, 1)
            dve.tensor_copy(eight[:, :], iota_i[:, 0:REL]).then_inc(consts_made, 1)
            dve.tensor_copy(part[:, :], part_i[:, :]).then_inc(consts_made, 1)
            dve.tensor_copy(dump_row[:, :], edge_i[:, :]).then_inc(consts_made, 1)
            dve.wait_ge(consts_made, 16)
            dve.tensor_scalar(ident[:, :], iota_hi[:, :], part[:, 0:1], None, ALU.is_equal).then_inc(consts_made, 1)
            dve.tensor_scalar(before[:, :], iota_hi[:, :], part[:, 0:1], None, ALU.is_gt).then_inc(consts_made, 1)

            dve.wait_ge(dst0_in, 16)
            dve.tensor_scalar(hi_i[:, :], dst0_i[:, :], 1.0 / NCOL, None, ALU.mult).then_inc(digits, 1)
            dve.wait_ge(digits, 1)
            dve.tensor_copy(hi[:, :], hi_i[:, :]).then_inc(digits, 1)
            dve.wait_ge(digits, 2)
            dve.scalar_tensor_tensor(lo[:, :], hi[:, :], -float(NCOL), dst0_i[:, :], ALU.mult, ALU.add) \
               .then_inc(digits, 1)
            dve.wait_ge(digits, 3)
            dve.tensor_scalar(fix[:, :], lo[:, :], 0.0, None, ALU.is_lt).then_inc(digits, 1)
            dve.wait_ge(digits, 4)
            dve.tensor_tensor(hi[:, :], hi[:, :], fix[:, :], ALU.subtract).then_inc(digits, 1)
            dve.scalar_tensor_tensor(lo[:, :], fix[:, :], float(NCOL), lo[:, :], ALU.mult, ALU.add) \
               .then_inc(digits, 1)
            dve.wait_ge(digits, 6)
            dve.tensor_scalar(fix[:, :], lo[:, :], float(NCOL), None, ALU.is_ge).then_inc(digits, 1)
            dve.wait_ge(digits, 7)
            dve.tensor_tensor(hi[:, :], hi[:, :], fix[:, :], ALU.add).then_inc(digits, 1)
            dve.scalar_tensor_tensor(lo[:, :], fix[:, :], -float(NCOL), lo[:, :], ALU.mult, ALU.add) \
               .then_inc(digits, 1)
            dve.wait_ge(digits, 9)

            dve.wait_ge(bias_in, 48)
            dve.tensor_copy(fill[:, :, :], over_rows(bias_row[:, :], FILL, ROW)).then_inc(fill_made, 1)

            def count_tile(s, t, used):
                if used is not None:
                    dve.wait_ge(hot_used, used)
                dve.tensor_scalar(hot[:, s, :], iota_hi[:, :], hi[:, bass.ds(t, 1)], None, ALU.is_equal)
                dve.tensor_scalar(steps[:, s, :], iota_lo[:, :], lo[:, bass.ds(t, 1)], None, ALU.is_ge) \
                   .then_inc(hot_ready, 1)

            for s in range(HIST):
                count_tile(s, s, None)
            with dve.Fori(1, T // HIST) as g:
                for s in range(HIST):
                    count_tile(s, g * HIST + s, g * HIST + s - (HIST - 1))

            dve.wait_ge(hot_used, T)
            dve.tensor_copy(total[0:NPART, :], ps_hist[0:NPART, 512 + NCOL // 2 - 1:512 + NCOL // 2]) \
               .then_inc(total_ready, 1)
            dve.wait_ge(base_ready, 1)
            dve.tensor_copy(ends[:, 0:1], ps_root[0:NPART, 0:1]).then_inc(last_step, 1)
            dve.wait_ge(last_step, 1)
            for h in range(2):
                dve.tensor_scalar(ends[:, 1 + h * NCOL // 2:1 + (h + 1) * NCOL // 2],
                                  ps_hist[0:NPART, 512 * h:512 * h + NCOL // 2], ends[:, 0:1], None, ALU.add) \
                   .then_inc(last_step, 1)
            dve.wait_ge(last_step, 3)
            dve.tensor_tensor(count_step, ends[:, 1:], ends[:, 0:NCOL], ALU.subtract).then_inc(last_step, 1)
            dve.tensor_scalar(last_edge, ends[:, 1:], part[0:NPART, 2:3], 1.0, ALU.subtract, ALU.subtract) \
               .then_inc(last_step, 1)
            dve.wait_ge(last_step, 5)
            dve.scalar_tensor_tensor(last_edge, count_step, 0.0, last_edge, ALU.is_gt, ALU.mult).then_inc(last_step, 1)
            dve.wait_ge(last_step, 6)
            dve.wait_ge(x_placed[0], DCHUNKS // 2)
            dve.wait_ge(x_placed[1], DCHUNKS // 2)
            dve.tensor_scalar(xl[:, :, FEAT], last_edge, part[0:NPART, 2:3], None, ALU.add).then_inc(last_step, 1)

            steps_done = 0

            def step(ins):
                nonlocal steps_done
                steps_done += 1
                ins.then_inc(prep, 1)
                return steps_done

            dve.wait_ge(edges_in, 64)
            step(dve.tensor_tensor(same[:, :], cur_i[:, :], prev_i[:, :], ALU.is_equal))
            n = step(dve.tensor_tensor(same_next[:, :], cur_i[:, :], next_i[:, :], ALU.is_equal))
            dve.wait_ge(prep, n)
            step(dve.tensor_tensor_scan(run_up[:, :], same[:, :], ones_t[:, :], 0.0, ALU.mult, ALU.add))
            step(dve.tensor_tensor_scan(back(run_down[:, :]), back(same_next[:, :]), ones_t[:, :], 0.0,
                                        ALU.mult, ALU.add))
            step(dve.tensor_tensor_scan(first_run[:, :], same[:, :], ones_t[:, :], 1.0, ALU.mult, ALU.mult))
            n = step(dve.tensor_tensor_scan(back(last_run[:, :]), back(same_next[:, :]), ones_t[:, :], 1.0,
                                            ALU.mult, ALU.mult))
            dve.wait_ge(prep, n)
            step(dve.tensor_copy(whole[:, 0:1], first_run[:, T - 1:T]))
            n = step(dve.tensor_copy(whole[:, 1:2], last_run[:, 0:1]))
            dve.wait_ge(prep, n)
            dve.tensor_copy(whole32[:, :, :], over_last(whole[:, :], HID)).then_inc(turn_ready, 1)
            dve.wait_ge(turn_done, 1)
            n = step(dve.tensor_copy(whole_rows[:, :, :], ps_turn[0:HID, 0:2 * P].rearrange("p (d q) -> p d q", d=2)))
            dve.wait_ge(prep, n)

            def bring_along(n):
                dve.wait_ge(row_turned, n + 1)
                dve.tensor_copy(tail_row[:, :], ps_root[0:HID, 0:P]).then_inc(row_copied, 1)
                dve.wait_ge(row_copied, n + 1)
                if CARRIES[n] == 0:
                    dve.tensor_tensor_scan(carry_out[:, 1:P + 1], whole_rows[:, 0, :], tail_row[:, :], 0.0,
                                           ALU.mult, ALU.add).then_inc(scan_ready, 1)
                else:
                    dve.tensor_tensor_scan(back(carry_out[:, 0:P]), back(whole_rows[:, 1, :]), back(tail_row[:, :]),
                                           0.0, ALU.mult, ALU.add).then_inc(scan_ready, 1)
                dve.wait_ge(back_done, n + 1)

            def clear_end(n):
                at = 0 if CARRIES[n] == 0 else P
                return dve.memset(carry_out[:, at:at + 1], 0.0)

            for n, (of, at) in enumerate(((run_up, T - 1), (run_down, 0))):
                m = step(clear_end(n))
                dve.wait_ge(prep, m)
                dve.tensor_copy(tail[:, 0:1], of[:, at:at + 1]).then_inc(row_ready, 1)
                bring_along(n)
                m = step(dve.tensor_copy(carry[n][:, :], ps_root[:, 256:256 + HID]))
                dve.wait_ge(prep, m)
            step(dve.tensor_tensor_scan(run_up[:, :], same[:, :], ones_t[:, :], carry[0][:, 0:1], ALU.mult, ALU.add))
            n = step(dve.tensor_tensor_scan(back(run_down[:, :]), back(same_next[:, :]), ones_t[:, :],
                                            carry[1][:, 0:1], ALU.mult, ALU.add))
            dve.wait_ge(prep, n)
            n = step(dve.tensor_tensor(inv_count[:, :], run_up[:, :], run_down[:, :], ALU.add))
            dve.wait_ge(prep, n)
            n = step(dve.tensor_scalar(inv_count[:, :], inv_count[:, :], -1.0, 1.0, ALU.add, ALU.max))
            dve.wait_ge(prep, n)
            n = step(dve.reciprocal(inv_count[:, :], inv_count[:, :]))
            dve.wait_ge(prep, n)

            n = step(dve.tensor_tensor(fix[:, :], dump_row[:, :], cur_i[:, :], ALU.subtract))
            dve.wait_ge(prep, n)
            n = step(dve.tensor_tensor(fix[:, :], fix[:, :], same_next[:, :], ALU.mult))
            dve.wait_ge(prep, n)
            n = step(dve.tensor_tensor(node_row[:, :], fix[:, :], cur_i[:, :], ALU.add))
            step(dve.tensor_reduce(small[:, 0:1], first_run[:, :], AX.X, ALU.add))
            n = step(dve.tensor_copy(small[:, 4:5], cur_i[:, 0:1]))
            dve.wait_ge(prep, n)
            step(dve.tensor_scalar(small[:, 1:2], small[:, 0:1], -1.0, 0.0, ALU.add, ALU.max))
            step(dve.tensor_tensor(small[:, 3:4], whole[:, 0:1], same_next[:, T - 1:T], ALU.mult))
            n = step(dve.tensor_tensor(small[:, 5:6], part[:, 3:4], small[:, 4:5], ALU.subtract))
            dve.wait_ge(prep, n)
            step(dve.tensor_tensor(carry_row[:, :], small[:, 1:2], part[:, 1:2], ALU.add))
            n = step(dve.tensor_tensor(small[:, 6:7], small[:, 5:6], small[:, 3:4], ALU.mult))
            dve.wait_ge(prep, n)
            dve.tensor_tensor(carry_node[:, :], small[:, 6:7], small[:, 4:5], ALU.add).then_inc(prep_done, 1)

            def add_up(layer, j, i, f, b0):
                k = i * 2 + j
                dve.wait_ge(layer["scan"][1 - j], i + j)
                dve.tensor_copy(part_sum[j][:, 0:f, 0:1], scanned[1 - j][:, 0:f, K:K + 1]).then_inc(layer["state"], 1)
                dve.wait_ge(layer["mask"][j], i + 1)
                dve.wait_ge(layer["reduced"], 4 * k + 4)
                dve.wait_ge(layer["state"], k + 1)
                dve.tensor_tensor_scan(scanned[j][:, 0:f, :].rearrange("p f k -> p (f k)"),
                                       keep[j][:, 0:f, :].rearrange("p f k -> p (f k)"),
                                       part_sum[j][:, 0:f, :].rearrange("p f k -> p (f k)"),
                                       0.0, ALU.mult, ALU.add).then_inc(layer["scan"][j], 1)
                dve.wait_ge(layer["scan"][j], i + 1)
                dve.wait_ge(layer["stored"][j], (16 if layer is not L2 else GOT) * i)
                if layer is L2:
                    to = node_rows[j][:, :, FEAT + HID:]
                else:
                    to = rows[j][:, 0:K * f].rearrange("p (k f) -> p k f", k=K)
                dve.tensor_tensor(to, scanned[j][:, 0:f, 1:].rearrange("p f k -> p k f"),
                                  over_rows(bias_row[:, b0:b0 + f], K, f), ALU.add).then_inc(layer["rows"][j], 1)

            def messages(layer, j, i, a, b, scale_of):
                k = i * 2 + j
                for g in range(GROUPS):
                    n = group_tiles(g)
                    dve.wait_ge(layer["msg"], 4 * k + g + 1)
                    dve.tensor_tensor(prod[g % 2][:, 0:n * a * b].rearrange("p (t a b) -> p t a b", t=n, a=a),
                                      ps_msg[g % 2][:, 0:n * a * b].rearrange("p (t a b) -> p t a b", t=n, a=a),
                                      over_last(scale_of(g, n), b), ALU.mult).then_inc(layer["mult"][g % 2], 1)
                    dve.wait_ge(layer["mult"][g % 2], 2 * k + g // 2 + 1)
                    dve.tensor_reduce(part_sum[j][:, 0:b, 1 + 4 * g:1 + 4 * g + n].rearrange("p b t -> p t b"),
                                      prod[g % 2][:, 0:n * a * b].rearrange("p (t a b) -> p t b a", t=n, a=a),
                                      AX.X, ALU.add).then_inc(layer["reduced"], 1)

            def layer0(j, i):
                k = i * 2 + j
                dve.wait_ge(L0["got"][j], GOT * (i + 1))
                dve.tensor_tensor(xc[:, :, :], got0[j][:, :, 0:FEAT], over_last(inv_count[:, chunk(k)], FEAT),
                                  ALU.mult).then_inc(L0["scaled"][j], 1)
                dve.wait_ge(L0["scaled"][j], i + 1)
                messages(L0, j, i, FEAT, FEAT, lambda g, n: xc[:, 4 * g:4 * g + n, :])
                add_up(L0, j, i, FEAT, 0)

            with dve.Fori(0, HALF) as i:
                layer0(0, i)
                layer0(1, i)

            def sum_carry(n, layer, f, to):
                dve.wait_ge(layer["scan"][1], HALF)
                m = step(clear_end(n))
                dve.wait_ge(prep, m)
                dve.tensor_copy(tail[:, 0:f], scanned[1][:, 0:f, K]).then_inc(row_ready, 1)
                bring_along(n)
                dve.tensor_scalar(to, ps_root[:, 256:256 + f], same[:, 0:1], None, ALU.mult).then_inc(carry_ready, 1)

            sum_carry(2, L0, FEAT, carry[0][:, 0:FEAT])

            n = step(dve.tensor_tensor(rel[:, :, :], over_last(typ_i[:, :], REL), over_rows(eight[:, :], T, REL),
                                       ALU.is_equal))
            dve.wait_ge(prep, n)
            dve.wait_ge(row_turned, 3)
            m = step(clear_end(3))
            dve.wait_ge(prep, m)
            for r in range(REL):
                m = step(dve.tensor_tensor_scan(run_up[:, :], same[:, :], rel[:, :, r], 0.0, ALU.mult, ALU.add))
                dve.wait_ge(prep, m)
                ins = dve.tensor_copy(tail[:, r:r + 1], run_up[:, T - 1:T])
                if r == REL - 1:
                    ins.then_inc(row_ready, 1)
                else:
                    m = step(ins)
                    dve.wait_ge(prep, m)
            for r in range(REL):
                m = step(dve.tensor_tensor_scan(back(run_down[:, :]), back(same_next[:, :]), back(rel[:, :, r]), 0.0,
                                                ALU.mult, ALU.add))
                dve.wait_ge(prep, m)
                m = step(dve.tensor_copy(heads[:, r:r + 1], run_down[:, 0:1]))
                dve.wait_ge(prep, m)
            bring_along(3)
            m = step(dve.tensor_copy(up8[:, :], ps_root[:, 256:256 + REL]))
            m = step(clear_end(4))
            dve.wait_ge(prep, m)
            dve.tensor_copy(tail[:, 0:REL], heads[:, :]).then_inc(row_ready, 1)
            bring_along(4)
            m = step(dve.tensor_copy(down8[:, :], ps_root[:, 256:256 + REL]))
            dve.wait_ge(prep, m)
            for r in range(REL):
                step(dve.tensor_tensor_scan(run_up[:, :], same[:, :], rel[:, :, r], up8[:, r:r + 1],
                                            ALU.mult, ALU.add))
                m = step(dve.tensor_tensor_scan(back(run_down[:, :]), back(same_next[:, :]), back(rel[:, :, r]),
                                                down8[:, r:r + 1], ALU.mult, ALU.add))
                dve.wait_ge(prep, m)
                m = step(dve.tensor_tensor(fix[:, :], run_up[:, :], run_down[:, :], ALU.add))
                dve.wait_ge(prep, m)
                to = first_run if r == 0 else last_run
                m = step(dve.tensor_tensor(to[:, :], fix[:, :], rel[:, :, r], ALU.mult))
                dve.wait_ge(prep, m)
                if r:
                    m = step(dve.tensor_tensor(first_run[:, :], first_run[:, :], last_run[:, :], ALU.add))
                    dve.wait_ge(prep, m)
            m = step(dve.tensor_scalar(first_run[:, :], first_run[:, :], -1.0, 1.0, ALU.add, ALU.max))
            dve.wait_ge(prep, m)
            m = step(dve.reciprocal(first_run[:, :], first_run[:, :]))
            dve.wait_ge(prep, m)
            m = step(dve.tensor_tensor(rel[:, :, :], rel[:, :, :], over_last(first_run[:, :], REL), ALU.mult))
            dve.wait_ge(prep, m)
            dve.wait_ge(L0["scan"][1], HALF)
            m = step(dve.memset(scanned[1][:, :, :], 0.0))
            dve.wait_ge(prep, m)

            dve.wait_ge(L0["stored"][0], 16 * HALF)
            dve.wait_ge(L0["stored"][1], 16 * HALF)

            def layer1(j, i):
                k = i * 2 + j
                dve.wait_ge(L1["got"][j], GOT * (i + 1))
                dve.tensor_tensor(cen[:, :, :], x_src[:, chunk(k), :], got1[j][:, :, :], ALU.add) \
                   .then_inc(L1["sum"][j], 1)
                dve.wait_ge(L1["sum"][j], i + 1)
                dve.tensor_reduce(stat[:, 0, :], cen[:, :, :], AX.X, ALU.add).then_inc(L1["stat"], 1)
                dve.wait_ge(L1["stat"], 4 * k + 1)
                dve.scalar_tensor_tensor(cen[:, :, :], over_last(stat[:, 0, :], FEAT), -1.0 / FEAT, cen[:, :, :],
                                         ALU.mult, ALU.add).then_inc(L1["stat"], 1)
                dve.wait_ge(L1["stat"], 4 * k + 2)
                dve.tensor_tensor(sq[:, :, :], cen[:, :, :], cen[:, :, :], ALU.mult).then_inc(L1["stat"], 1)
                dve.wait_ge(L1["stat"], 4 * k + 3)
                dve.tensor_reduce(stat[:, 1, :], sq[:, :, :], AX.X, ALU.add).then_inc(L1["stat"], 1)
                dve.wait_ge(L1["std"], k + 1)
                dve.reciprocal(stat[:, 3, :], stat[:, 2, :]).then_inc(L1["inv"], 1)
                dve.wait_ge(L1["inv"], k + 1)
                dve.wait_ge(L1["turned"], k)
                dve.tensor_tensor(padded[:, 0:K, 0:FEAT], cen[:, :, :], over_last(stat[:, 3, :], FEAT), ALU.mult) \
                   .then_inc(L1["padded"][j], 1)
                messages(L1, j, i, REL, HID, lambda g, n: rel[:, bass.ds(k * K + 4 * g, n), :])
                add_up(L1, j, i, HID, FEAT)

            with dve.Fori(0, HALF) as i:
                layer1(0, i)
                layer1(1, i)
            dve.wait_ge(carry_added, 16)
            sum_carry(5, L1, HID, carry[0][:, :])
            m = step(dve.memset(scanned[1][:, :, :], 0.0))
            dve.wait_ge(prep, m)

            def layer2(j, i):
                k = i * 2 + j
                dve.wait_ge(L2["padded"][1 - j], i + j)
                dve.wait_ge(L2["got"][j], GOT * (i + 1))
                dve.tensor_tensor(hsum[:, :, :], u_src[:, chunk(k), :], got2[j][:, :, :], ALU.add) \
                   .then_inc(L2["sum"][j], 1)
                messages(L2, j, i, REL, FEAT, lambda g, n: rel[:, bass.ds(k * K + 4 * g, n), :])
                add_up(L2, j, i, FEAT, FEAT + HID)

            with dve.Fori(0, HALF) as i:
                layer2(0, i)
                layer2(1, i)
            sum_carry(6, L2, FEAT, carry64[:, FEAT + HID:])

            st = dstat[0:NPART, :, :]

            def normed(at, to, k, c):
                dve.wait_ge(D["stat"], at)
                dve.tensor_reduce(st[:, 0, :], vv, AX.X, ALU.add).then_inc(D["stat"], 1)
                dve.wait_ge(D["stat"], at + 1)
                dve.scalar_tensor_tensor(vv, over_last(st[:, 0, :], FEAT), -1.0 / FEAT, vv, ALU.mult, ALU.add) \
                   .then_inc(D["center"], 1)
                dve.wait_ge(D["center"], 2 * k + c + 1)
                dve.tensor_tensor(v2, vv, vv, ALU.mult).then_inc(D["stat"], 1)
                dve.wait_ge(D["stat"], at + 2)
                dve.tensor_reduce(st[:, 1, :], v2, AX.X, ALU.add).then_inc(D["stat"], 1)
                dve.wait_ge(D["std"], 2 * k + c + 1)
                dve.reciprocal(st[:, 3, :], st[:, 2, :]).then_inc(D["inv"], 1)
                dve.wait_ge(D["inv"], 2 * k + c + 1)
                return dve.tensor_tensor(to, vv, over_last(st[:, 3, :], FEAT), ALU.mult)

            def dense_chunk(j, i):
                k = i * 2 + j
                dve.wait_ge(D["in"][j], 64 * (i + 1))
                dve.wait_ge(D["result"][1 - j], i + j)
                dve.tensor_tensor(vv, xn[j], nr[j][:, :, 0:FEAT], ALU.add).then_inc(D["stat"], 1)
                dve.wait_ge(D["x1t"], 2 * k)
                normed(8 * k + 1, x1n, k, 0).then_inc(D["x1"], 1)
                dve.wait_ge(D["ht"], 3 * k)
                for q in range(3):
                    n = min(16, DC - 16 * q)
                    dve.wait_ge(D["h_mm"], 3 * k + q + 1)
                    dve.tensor_tensor(hn[:, 16 * q:16 * q + n, :],
                                      ps_msg[q % 2][0:NPART, 0:n * HID].rearrange("p (c f) -> p c f", f=HID),
                                      nr[j][:, 16 * q:16 * q + n, FEAT:FEAT + HID], ALU.add) \
                       .then_inc(D["h_sum"][q % 2], 1)
                dve.wait_ge(D["y"], k + 1)
                dve.tensor_tensor(v2, ps_hist[0:NPART, 0:DC * FEAT].rearrange("p (c f) -> p c f", f=FEAT),
                                  nr[j][:, :, FEAT + HID:], ALU.add).then_inc(D["y_read"][j], 1)
                dve.wait_ge(D["y_read"][j], i + 1)
                dve.wait_ge(D["x1"], k + 1)
                dve.tensor_tensor(vv, v2, x1n, ALU.add).then_inc(D["stat"], 1)
                dve.wait_ge(D["out"][j], 32 * i)
                normed(8 * k + 5, res[j], k, 1).then_inc(D["result"][j], 1)

            with dve.Fori(0, DCHUNKS // 2) as i:
                dense_chunk(0, i)
                dense_chunk(1, i)


_INS = ["x", "src", "dst", "edge_attr_16", "edge_type_8", "L0_gnn_W_e", "L0_gnn_b_e", "L0_gnn_bias",
        "L1_gnn_W1", "L1_gnn_root1", "L1_gnn_b1", "L1_gnn_W2", "L1_gnn_root2", "L1_gnn_b2"]


def kernel(**inputs):
    import concourse.bacc as bacc
    from concourse.bass_utils import run_bass_kernel_spmd

    nc = bacc.Bacc("TRN2", target_bir_lowering=False, num_devices=1)
    arrays, args = {}, []
    for name in _INS:
        a = np.ascontiguousarray(inputs[name])
        arrays[f"in_{name}"] = a
        args.append(nc.dram_tensor(f"in_{name}", a.shape, mybir.dt.from_np(a.dtype), kind="ExternalInput").ap())
    out = nc.dram_tensor("out", inputs["x"].shape, F32, kind="ExternalOutput").ap()
    bass_gnn_resnorm(nc, *args, out)
    r = run_bass_kernel_spmd(nc, [arrays], core_ids=[0])
    return r.results[0]["out"]
```

```python
from contextlib import ExitStack

import numpy as np

import concourse.bass as bass
from concourse import mybir

ALU = mybir.AluOpType
ACT = mybir.ActivationFunctionType
AX = mybir.AxisListType
F32 = mybir.dt.float32
F16 = mybir.dt.float16
BF16 = mybir.dt.bfloat16
I32 = mybir.dt.int32

P = 128
FEAT = 16
HID = 32
REL = 8
EPS = 1e-5
K = 14
GROUPS = 4
PAD = 4 * GROUPS
STEPCOLS = 17
ROW = FEAT + HID + FEAT
HIST = 4


def group_tiles(g):
    return min(4, K - 4 * g)


def bass_gnn_resnorm(nc, x, src, dst, edge_attr, edge_type, W_e, b_e, bias0,
                     W1, root1, b1, W2, root2, b2, out):
    N, _ = x.shape
    E = src.shape[0]
    T = -(-E // (P * 2 * K)) * 2 * K
    EP = P * T
    CHUNKS = T // K
    HALF = CHUNKS // 2
    NPART = 125
    NCOL = N // NPART
    assert NPART * NCOL == N and E <= EP and T % HIST == 0
    FILL = 16
    assert NCOL % FILL == 0
    DC = 40
    DCHUNKS = NCOL // DC
    T8, T4 = DC // 8, DC // 4
    DUMP = N + 1
    NROWS = DUMP + EP + P

    d_src = nc.dram_tensor("edge_src", (EP,), I32, kind="Internal").ap()
    d_dst = nc.dram_tensor("edge_dst", (EP + 2,), I32, kind="Internal").ap()
    d_typ = nc.dram_tensor("edge_typ", (EP,), I32, kind="Internal").ap()
    d_ea = nc.dram_tensor("edge_att", (EP, FEAT), F32, kind="Internal").ap()
    d_xl = nc.dram_tensor("node_x_last", (N, STEPCOLS), F32, kind="Internal").ap()
    d_a0 = nc.dram_tensor("edge_sum0", (EP + P, FEAT), F32, kind="Internal").ap()
    d_a1 = nc.dram_tensor("edge_sum1", (EP + P, HID), F32, kind="Internal").ap()
    d_nodes = nc.dram_tensor("node_sums", (NROWS, ROW), F32, kind="Internal").ap()

    def by_edge(ap):
        return ap.rearrange("(p t) -> p t", p=P)

    def by_edge_row(ap):
        return ap.rearrange("(p t) f -> p t f", p=P)

    d_cur, d_prev, d_next = (by_edge(d_dst[s:s + EP]) for s in (1, 0, 2))
    d_src_t, d_typ_t = by_edge(d_src), by_edge(d_typ)
    d_ea_t = by_edge_row(d_ea)
    d_a0_t, d_a1_t = by_edge_row(d_a0[0:EP, :]), by_edge_row(d_a1[0:EP, :])
    x_t = x.rearrange("(p c) f -> p c f", p=NPART)
    out_t = out.rearrange("(p c) f -> p c f", p=NPART)
    d_xl_t = d_xl.rearrange("(p c) f -> p c f", p=NPART)
    d_nodes_t = d_nodes[0:N, :].rearrange("(p c) f -> p c f", p=NPART)
    NODE_PARTS = (slice(0, 112), slice(112, NPART))

    with ExitStack() as ctx:
        def sb(name, shape, dt=F32):
            return ctx.enter_context(nc.sbuf_tensor(name, shape, dt))

        def psum(name, shape):
            return ctx.enter_context(nc.psum_tensor(name, shape, F32))

        def sem(name):
            return ctx.enter_context(nc.semaphore(name))

        def pair(name, shape, dt=F32):
            return [sb(f"{name}{j}", shape, dt) for j in range(2)]

        ps_turn = psum("ps_turn", [P, 512])
        ps_root = psum("ps_root", [P, 512])
        ps_m = psum("ps_m", [P, 2048])
        ps_msg = [ps_m[:, 0:1024], ps_m[:, 1024:2048]]
        ps_hist = psum("ps_hist", [P, 1024])
        ps_turns = [ps_turn, ps_hist]

        ident = sb("ident", [P, P])
        iota_lo = sb("iota_lo", [P, NCOL], F16)
        iota_hi = sb("iota_hi", [P, P], F16)
        part_i = sb("part_i", [P, 4], I32)
        part = sb("part", [P, 4])
        dump_row = sb("dump_row", [P, T])
        before = sb("before", [P, P])
        eight = sb("eight", [P, REL])
        ones_t = sb("ones_t", [P, T])
        eps = sb("eps", [P, 1])
        w0 = sb("w0", [P, 4, 256])
        w1 = sb("w1", [P, 2 * HID])
        w2 = sb("w2", [P, 4, REL * FEAT])
        wr1 = sb("wr1", [P, 8, HID])
        wr2 = sb("wr2", [P, 4, FEAT])
        bias_row = sb("bias_row", [P, ROW])
        fill = sb("fill", [P, FILL, ROW])
        pad_dst = sb("pad_dst", [1, EP - E + 2], I32)
        pad_i = sb("pad_i", [1, EP - E], I32)
        pad_att = sb("pad_att", [FEAT, EP - E])

        dst0_i = sb("dst0_i", [P, T], I32)
        cur_i = sb("cur_i", [P, T], I32)
        prev_i = sb("prev_i", [P, T], I32)
        next_i = sb("next_i", [P, T], I32)
        typ_i = sb("typ_i", [P, T], I32)
        hi = sb("hi", [P, T])
        lo = sb("lo", [P, T])
        fix = sb("fix", [P, T])
        same = sb("same", [P, T])
        same_next = sb("same_next", [P, T])
        run_up = sb("run_up", [P, T])
        run_down = sb("run_down", [P, T])
        inv_count = sb("inv_count", [P, T])
        first_run = sb("first_run", [P, T])
        last_run = sb("last_run", [P, T])
        node_row = sb("node_row", [P, T], I32)
        last_of_src = sb("last_of_src", [P, T], I32)
        x_src = sb("x_src", [P, T, FEAT])
        rel = sb("rel", [P, T, REL])
        inv_rel = sb("inv_rel", [P, T])
        arena = sb("arena", [P, NCOL * STEPCOLS])
        xl = arena[0:NPART, :].rearrange("p (c f) -> p c f", f=STEPCOLS)
        u_src = arena[:, 0:T * HID].rearrange("p (t f) -> p t f", f=HID)
        spare = x_src[:, :, :].rearrange("p t f -> p (t f)")
        iota_i = spare[:, 0:NCOL].bitcast(I32)
        count_step = spare[0:NPART, NCOL:2 * NCOL]
        last_edge = spare[0:NPART, 2 * NCOL:3 * NCOL]
        ends = spare[0:NPART, 3 * NCOL:4 * NCOL + 1]
        edge_i = last_of_src
        hi_i = node_row
        steps = rel[:, :, :].rearrange("p t f -> p (t f)").bitcast(BF16)[:, 0:HIST * NCOL]
        steps = steps.rearrange("p (s c) -> p s c", s=HIST)

        SORT_PARTS = 8
        SORT_CHUNKS = P // SORT_PARTS
        sort_row = spare[:, 0:SORT_PARTS * T].bitcast(I32)
        sort_low = spare[:, SORT_PARTS * T:2 * SORT_PARTS * T]
        sort_less = rel[:, :, :].rearrange("p t f -> p (t f)")
        cur_col = sb("cur_col", [P, 1], I32)
        unsorted = sb("unsorted", [1, 1], I32)

        small = sb("small", [P, 8])
        total = sb("total", [P, 1])
        carry_row = sb("carry_row", [P, 1], I32)
        carry_node = sb("carry_node", [P, 1], I32)
        whole = sb("whole", [P, 2])
        whole32 = sb("whole32", [P, 2, HID])
        whole_rows = sb("whole_rows", [HID, 2, P])
        tail = sb("tail", [P, HID])
        tail_row = sb("tail_row", [HID, P])
        carry_out = sb("carry_out", [HID, P + 1])
        carry = [sb(f"carry{d}", [P, HID]) for d in range(2)]
        heads = sb("heads", [P, REL])
        up8 = sb("up8", [P, REL])
        down8 = sb("down8", [P, REL])
        carry64 = sb("carry64", [P, ROW])
        hot = sb("hot", [P, HIST, P], BF16)

        idx = pair("idx", [P, K], I32)
        sidx = pair("sidx", [P, K], I32)
        got0 = pair("got0", [P, K, STEPCOLS])
        got1 = pair("got1", [P, K, FEAT])
        got2 = pair("got2", [P, K, HID])
        att = pair("att", [P, K, FEAT])
        padded = sb("padded", [P, PAD, HID])
        turned = pair("turned", [P, GROUPS * P])
        xc = sb("xc", [P, K, FEAT])
        sq = sb("sq", [P, K, FEAT])
        cen = sb("cen", [P, K, FEAT])
        stat = sb("stat", [P, 4, K])
        hsum = sb("hsum", [P, K, HID])
        prod_both = sb("prod_both", [P, 2048])
        prod = [prod_both[:, 1024 * j:1024 * (j + 1)] for j in range(2)]
        outer = prod_both[:, 0:K * P].rearrange("p (k r f) -> p k r f", k=K, r=REL)
        keep = pair("keep", [P, HID, K + 1])
        part_sum = pair("part_sum", [P, HID, K + 1])
        scanned = pair("scanned", [P, HID, K + 1])
        rows = pair("rows", [P, K * HID])
        old0 = pair("old0", [P, K, FEAT])
        old1 = pair("old1", [P, K, HID])
        node_rows = pair("node_rows", [P, K, ROW])

        flat_x = x_src[:, :, :].rearrange("p t f -> p (t f)")
        flat_rel = rel[:, :, :].rearrange("p t f -> p (t f)")
        room = [[arena[:, :], 0, NCOL * STEPCOLS], [flat_x, 0, T * FEAT], [flat_rel, 0, T * REL]]
        room += [[prod[j][:, :], 0, 1024] for j in range(2)]
        room += [[node_rows[j][:, :, :].rearrange("p k f -> p (k f)"), 0, K * ROW] for j in range(2)]

        def dense(n, cols, f=None):
            for region in room:
                if region[1] + cols <= region[2]:
                    got = region[0][0:n, region[1]:region[1] + cols]
                    region[1] += cols
                    return got if f is None else got.rearrange("p (c f) -> p c f", f=f)
            raise AssertionError("no room")

        nr = [dense(NPART, DC * ROW, ROW) for _ in range(4)]
        hn = dense(NPART, DC * HID, HID)
        ht = dense(P, T4 * NPART)
        x1t = dense(P, T8 * NPART)
        xn = [dense(NPART, DC * FEAT, FEAT) for _ in range(2)]
        vv, cc1, x1n, zz, cc2, res, qq = ([dense(NPART, DC * FEAT, FEAT) for _ in range(2)] for _ in range(7))
        ww = dense(NPART, DC * FEAT, FEAT)
        dst_ = {n: sb("d_" + n, [P, DC])[0:NPART, :] for n in ("1sum", "1ss", "1dev", "1inv", "2sum", "2ss", "2dev")}
        inv2 = [sb(f"d_inv2{j}", [P, DC])[0:NPART, :] for j in range(2)]
        ps_h = [ps_m[:, 512 * g:512 * (g + 1)] for g in range(3)]
        ps_ht = [ps_root[:, :], ps_m[:, 1536:2048]]
        ps_y = ps_hist[0:NPART, 0:DC * FEAT]
        idn = ident[0:NPART, 0:NPART]

        pool_made = sem("pool_made")
        zeroed = sem("zeroed")
        consts_made = sem("consts_made")
        weights_in = sem("weights_in")
        bias_in = sem("bias_in")
        fill_made = sem("fill_made")
        filled = sem("filled")
        edges_copied = sem("edges_copied")
        dst_copied = sem("dst_copied")
        dst0_in = sem("dst0_in")
        edges_in = sem("edges_in")
        digits = sem("digits")
        disorder_sum = sem("disorder_sum")
        flag_ready = sem("flag_ready")
        sort_in = sem("sort_in")
        sort_row_in = sem("sort_row_in")
        sort_read = sem("sort_read")
        sort_step = sem("sort_step")
        sort_cmp = sem("sort_cmp")
        sort_ranked = sem("sort_ranked")
        sort_col = sem("sort_col")
        sort_out = sem("sort_out")
        hot_ready = sem("hot_ready")
        hot_used = sem("hot_used")
        total_ready = sem("total_ready")
        base_ready = sem("base_ready")
        last_step = sem("last_step")
        x_in = [sem(f"x_in{j}") for j in range(2)]
        x_placed = [sem(f"x_placed{j}") for j in range(2)]
        xl_stored = sem("xl_stored")
        prep = sem("prep")
        prep_done = sem("prep_done")
        begun = sem("begun")
        lists_free = sem("lists_free")
        turn_ready = sem("turn_ready")
        turn_done = sem("turn_done")
        row_ready = sem("row_ready")
        row_turned = sem("row_turned")
        row_copied = sem("row_copied")
        scan_ready = sem("scan_ready")
        back_done = sem("back_done")
        carry_ready = sem("carry_ready")
        carry_added = sem("carry_added")
        nodes_idx_in = [sem(f"nodes_idx_in{j}") for j in range(2)]

        def layer_sems(n, single, paired):
            s = {m: sem(f"l{n}_{m}") for m in single.split()}
            s.update({m: [sem(f"l{n}_{m}{j}") for j in range(2)] for m in paired.split()})
            return s

        L0, L1, L2 = (layer_sems(n, "turned turned_sb msg reduced" + more, "idx_in got mask scan rows stored" + pairs)
                      for n, more, pairs in ((0, "", " padded mult att_in saved scaled"),
                                             (1, " stat squared std inv x1 outer root_saved", " sum"),
                                             (2, "", " padded mult att_in saved sum")))
        D = layer_sems("d", "v stat1 center1 q1 ss1 std1 x1 x1t x1t_sb h_mm h ht ht_sb y z w sum2 center2 q2 ss2 std2"
                       " inv2 result", "out")
        D["in"] = [sem(f"ld_in{s}") for s in range(4)]

        CARRIES = (0, 1, 0, 0, 1, 0, 0)
        CONSTS, LAST_STEPS = 18, 7

        def chunk(k):
            return bass.ds(k * K, K)

        def back(ap):
            dims = [list(d) for d in ap.ap]
            n, step = dims[-1][1], dims[-1][0]
            dims[-1] = [-step, n]
            return bass.AP(ap.tensor, ap.offset + (n - 1) * step, dims)

        def above(eng, s, value):
            if not isinstance(value, int) or value > 0:
                eng.wait_ge(s, value)

        def over_chunks(eng, stage, lag):
            for k in range(4):
                stage(k, k, 0)
            with eng.Fori(1, DCHUNKS // 4) as i:
                for s in range(4):
                    stage(i * 4 + s, s, i)
            for k in range(DCHUNKS, DCHUNKS + lag):
                stage(k, k % 4, k // 4)

        def over_rows(ap, n, f):
            return ap.unsqueeze(1).to_broadcast([ap.shape[0], n, f])

        def over_last(ap, f):
            return ap.unsqueeze(len(ap.shape)).to_broadcast([*ap.shape, f])

        block = ctx.enter_context(nc.Block())

        GOT = 16 * K
        FILLED = 16 * (2 + 2 * (NCOL // FILL))

        @block.sync
        def _(sp):
            sp.dma_start(d_dst[1:1 + E].rearrange("(a b) -> a b", a=80),
                         dst.rearrange("(a b) -> a b", a=80)).then_inc(dst_copied, 16)
            sp.wait_ge(pool_made, 4)
            sp.dma_start(d_dst[1 + E:EP + 2].rearrange("(a b) -> a b", a=1),
                         pad_dst[:, 0:EP - E + 1]).then_inc(dst_copied, 16)
            sp.dma_start(d_dst[0:1].rearrange("(a b) -> a b", a=1),
                         pad_dst[:, EP - E + 1:]).then_inc(dst_copied, 16)
            sp.wait_ge(dst_copied, 48)
            sp.dma_start(dst0_i[:, :], d_cur).then_inc(dst0_in, 16)
            sp.dma_start(prev_i[:, :], d_prev).then_inc(dst0_in, 16)
            sp.dma_start(d_src[0:E].rearrange("(a b) -> a b", a=80),
                         src.rearrange("(a b) -> a b", a=80)).then_inc(edges_copied, 16)
            sp.dma_start(d_typ[0:E].rearrange("(a b) -> a b", a=80),
                         edge_type.rearrange("(a b) -> a b", a=80)).then_inc(edges_copied, 16)
            sp.dma_start(d_src[E:EP].rearrange("(a b) -> a b", a=1), pad_i[:, :]).then_inc(edges_copied, 16)
            sp.dma_start(d_typ[E:EP].rearrange("(a b) -> a b", a=1), pad_i[:, :]).then_inc(edges_copied, 16)
            sp.dma_start(d_ea[0:E, :].rearrange("(a b) f -> a (b f)", a=80),
                         edge_attr.rearrange("(a b) f -> a (b f)", a=80)).then_inc(edges_copied, 16)
            sp.dma_start(d_ea[E:EP, :].rearrange("(a b) f -> a (b f)", a=FEAT),
                         pad_att[:, :]).then_inc(edges_copied, 16)
            sp.wait_ge(edges_copied, 96)

            with sp.Fori(0, DCHUNKS // 2) as i:
                for j in range(2):
                    sp.wait_ge(x_placed[j], i)
                    for ps in NODE_PARTS:
                        sp.dma_start(node_rows[j][ps, :, :].rearrange("p k f -> p (k f)")[:, 0:DC * FEAT],
                                     x_t[ps, bass.ds((i * 2 + j) * DC, DC), :]
                                     .rearrange("p c f -> p (c f)")).then_inc(x_in[j], 16)

            sp.wait_ge(fill_made, 1)
            sp.dma_start(d_a0[EP:EP + P, :], bias_row[:, 0:FEAT]).then_inc(filled, 16)
            sp.dma_start(d_a1[EP:EP + P, :], bias_row[:, FEAT:FEAT + HID]).then_inc(filled, 16)
            with sp.Fori(0, NCOL // FILL) as i:
                for ps in NODE_PARTS:
                    sp.dma_start(d_nodes_t[ps, bass.ds(i * FILL, FILL), :], fill[ps, :, :]).then_inc(filled, 16)

            sp.wait_ge(flag_ready, 1)
            with sp.If(sp.value_load(unsorted[0:1, 0:1], min_val=0, max_val=EP)):
                sp.dma_start(next_i[:, :], d_src_t).then_inc(sort_in, 16)
                sp.dma_start(prev_i[:, :], d_typ_t).then_inc(sort_in, 16)
                sp.wait_ge(last_step, LAST_STEPS)
                with sp.Fori(0, SORT_CHUNKS) as c:
                    sp.wait_ge(sort_read, c)
                    sp.dma_start(sort_row[:, :], d_dst[bass.ds(1 + c * (T * SORT_PARTS), T * SORT_PARTS)]
                                 .rearrange("(a f) -> a f", a=1).to_broadcast([P, T * SORT_PARTS])) \
                      .then_inc(sort_row_in, 16)
                sp.wait_ge(sort_ranked, 1)
                sp.dma_start(x_src[:, :, :], d_ea_t).then_inc(sort_in, 16)
                sp.wait_ge(sort_in, 48)
                with sp.Fori(0, T) as t:
                    col = bass.ds(t, 1)
                    sp.wait_ge(sort_out, 64 * t)
                    for to, of in ((idx[0], cur_i), (idx[1], node_row), (sidx[0], next_i), (sidx[1], prev_i)):
                        sp.dma_start(to[:, 0:1], of[:, col]).then_inc(sort_col, 16)
                    sp.dma_start(cur_col[:, :], dst0_i[:, col]).then_inc(sort_col, 16)
                    sp.dma_start(got1[0][:, 0:1, :], x_src[:, col, :]).then_inc(sort_col, 16)
                sp.wait_ge(sort_out, 64 * T)
            for to, of in ((cur_i, d_cur), (prev_i, d_prev), (next_i, d_next), (typ_i, d_typ_t)):
                sp.dma_start(to[:, :], of).then_inc(edges_in, 16)

            sp.wait_ge(last_step, LAST_STEPS)
            for ps in NODE_PARTS:
                sp.dma_start(d_xl_t[ps, :, :], xl[ps, :, :]).then_inc(xl_stored, 16)

            def loads0(j, i):
                k = i * 2 + j
                sp.wait_ge(L0["got"][j], GOT * i)
                sp.dma_start(idx[j][:, :], d_src_t[:, chunk(k)]).then_inc(L0["idx_in"][j], 16)
                sp.wait_ge(L0["padded"][j], i)
                sp.dma_start(att[j][:, :, :], d_ea_t[:, chunk(k), :]).then_inc(L0["att_in"][j], 16)

            def store0(j, i):
                k = i * 2 + j
                sp.wait_ge(L0["rows"][j], i + 1)
                sp.dma_start(d_a0_t[:, chunk(k), :],
                             rows[j][:, 0:K * FEAT].rearrange("p (k f) -> p k f", k=K)).then_inc(L0["stored"][j], 16)

            loads0(0, 0)
            with sp.Fori(0, HALF - 1) as i:
                loads0(1, i)
                store0(0, i)
                loads0(0, i + 1)
                store0(1, i)
            loads0(1, HALF - 1)
            store0(0, HALF - 1)
            store0(1, HALF - 1)

            def loads1(j, i):
                k = i * 2 + j
                sp.wait_ge(L1["got"][j], GOT * i)
                sp.dma_start(idx[j][:, :], last_of_src[:, chunk(k)]).then_inc(L1["idx_in"][j], 16)

            def store1(j, i):
                k = i * 2 + j
                sp.wait_ge(L1["rows"][j], i + 1)
                sp.dma_start(d_a1_t[:, chunk(k), :],
                             rows[j][:, :].rearrange("p (k f) -> p k f", k=K)).then_inc(L1["stored"][j], 16)

            sp.wait_ge(L0["got"][0], GOT * HALF)
            sp.wait_ge(L0["got"][1], GOT * HALF)
            sp.wait_ge(L0["saved"][0], 2 * HALF)
            sp.wait_ge(L0["saved"][1], 2 * HALF)
            loads1(0, 0)
            loads1(1, 0)
            with sp.Fori(0, HALF - 1) as i:
                for j in range(2):
                    loads1(j, i + 1)
                    store1(j, i)
            store1(0, HALF - 1)
            store1(1, HALF - 1)

            def loads2(j, i):
                k = i * 2 + j
                sp.wait_ge(L2["got"][j], GOT * i)
                sp.dma_start(idx[j][:, :], last_of_src[:, chunk(k)]).then_inc(L2["idx_in"][j], 16)
                sp.wait_ge(L2["saved"][j], 2 * i)
                sp.dma_start(old0[j][:, :, :], d_a0_t[:, chunk(k), :]).then_inc(L2["att_in"][j], 16)
                sp.dma_start(old1[j][:, :, :], d_a1_t[:, chunk(k), :]).then_inc(L2["att_in"][j], 16)
                sp.wait_ge(L2["stored"][j], GOT * i)
                sp.sem_inc(lists_free, 1)
                sp.dma_start(sidx[j][:, :], node_row[:, chunk(k)]).then_inc(nodes_idx_in[j], 16)

            sp.wait_ge(L1["got"][0], GOT * HALF)
            sp.wait_ge(L1["got"][1], GOT * HALF)
            sp.wait_ge(carry_added, 32)
            loads2(0, 0)
            with sp.Fori(0, HALF - 1) as i:
                loads2(1, i)
                loads2(0, i + 1)
            loads2(1, HALF - 1)

            sp.wait_ge(carry_added, 48)
            sp.wait_ge(L2["sum"][0], HALF)
            sp.wait_ge(L2["sum"][1], HALF)

            def load_nodes(k, s, u):
                above(sp, D["h"], 3 * (k - 3))
                sp.sem_inc(lists_free, 1)
                above(sp, D["z"], k - 3)
                sp.sem_inc(lists_free, 1)
                above(sp, D["v"], k - 1)
                sp.sem_inc(lists_free, 1)
                for ps in NODE_PARTS:
                    sp.dma_start(nr[s][ps, :, :], d_nodes_t[ps, bass.ds(k * DC, DC), :]).then_inc(D["in"][s], 16)
                    sp.dma_start(xn[s % 2][ps, :, :], x_t[ps, bass.ds(k * DC, DC), :]).then_inc(D["in"][s], 16)

            def store_nodes(k, s):
                above(sp, D["result"], k + 1)
                sp.sem_inc(lists_free, 1)
                for ps in NODE_PARTS:
                    sp.dma_start(out_t[ps, bass.ds(k * DC, DC), :], res[s % 2][ps, :, :]) \
                      .then_inc(D["out"][s % 2], 16)

            def nodes(k, s, u):
                if not isinstance(k, int) or k < DCHUNKS:
                    load_nodes(k, s, u)
                if not isinstance(k, int) or k >= 4:
                    store_nodes(k - 4, s)

            over_chunks(sp, nodes, 4)
            sp.wait_ge(D["out"][0], 32 * (DCHUNKS // 2))
            sp.wait_ge(D["out"][1], 32 * (DCHUNKS // 2))

        @block.gpsimd
        def _(pool):
            pool.memset(pad_dst[:, 0:EP - E], N).then_inc(pool_made, 1)
            pool.memset(pad_dst[:, EP - E:], -1).then_inc(pool_made, 1)
            pool.memset(pad_i[:, :], 0).then_inc(pool_made, 1)
            pool.memset(pad_att[:, :], 0.0).then_inc(pool_made, 1)
            pool.iota(iota_i, [[1, NCOL]], base=0, channel_multiplier=0).then_inc(pool_made, 1)
            for n, (base, times) in enumerate(((0, 1), (0, T), (EP, 1), (DUMP + EP, 1))):
                pool.iota(part_i[:, n:n + 1], [[0, 1]], base=base, channel_multiplier=times).then_inc(pool_made, 1)
            pool.iota(edge_i[:, :], [[1, T]], base=DUMP, channel_multiplier=T).then_inc(pool_made, 1)

            def gather(layer, table, to, j, i, freed, complete):
                pool.wait_ge(layer["idx_in"][j], 16 * (i + 1))
                for free, n in freed:
                    pool.wait_ge(layer[free][j], n * i)
                pool.wait_ge(*complete)
                pool.sem_inc(begun, 1)
                for t in range(K):
                    pool.indirect_dma_start(
                        out=to[j][:, t, :], out_offset=None, in_=table,
                        in_offset=bass.IndirectOffsetOnAxis(ap=idx[j][:, t:t + 1], axis=0),
                    ).then_inc(layer["got"][j], 16)

            def scatter(j, i):
                pool.wait_ge(nodes_idx_in[j], 16 * (i + 1))
                pool.wait_ge(L2["saved"][j], 2 * (i + 1))
                pool.wait_ge(L2["rows"][j], i + 1)
                pool.wait_ge(filled, FILLED)
                pool.sem_inc(begun, 1)
                for t in range(K):
                    pool.indirect_dma_start(
                        out=d_nodes[:, :], out_offset=bass.IndirectOffsetOnAxis(ap=sidx[j][:, t:t + 1], axis=0),
                        in_=node_rows[j][:, t, :], in_offset=None,
                    ).then_inc(L2["stored"][j], 16)

            def add_carry(n, table, rows_of, what):
                pool.wait_ge(carry_ready, n + 1)
                pool.indirect_dma_start(
                    out=table, out_offset=bass.IndirectOffsetOnAxis(ap=rows_of[:, 0:1], axis=0),
                    in_=what, in_offset=None, compute_op=ALU.add,
                ).then_inc(carry_added, 16)

            pool.wait_ge(flag_ready, 1)
            with pool.If(pool.value_load(unsorted[0:1, 0:1], min_val=0, max_val=EP)):
                with pool.Fori(0, T) as t:
                    pool.wait_ge(sort_col, 96 * (t + 1))
                    pool.sem_inc(begun, 1)
                    for table, rows_of, what in ((d_src, idx[0], sidx[0]), (d_dst, idx[1], cur_col),
                                                 (d_typ, idx[0], sidx[1])):
                        pool.indirect_dma_start(
                            out=table.rearrange("(e a) -> e a", a=1),
                            out_offset=bass.IndirectOffsetOnAxis(ap=rows_of[:, 0:1], axis=0),
                            in_=what[:, 0:1], in_offset=None).then_inc(sort_out, 16)
                    pool.indirect_dma_start(
                        out=d_ea[:, :], out_offset=bass.IndirectOffsetOnAxis(ap=idx[0][:, 0:1], axis=0),
                        in_=got1[0][:, 0, :], in_offset=None).then_inc(sort_out, 16)

            pool.wait_ge(xl_stored, 32)
            with pool.Fori(0, HALF) as i:
                for j in range(2):
                    gather(L0, d_xl[:, :], got0, j, i, (("saved", 2), ("scaled", 1)), (xl_stored, 32))
            pool.wait_ge(L0["stored"][0], 16 * HALF)
            pool.wait_ge(L0["stored"][1], 16 * HALF)
            add_carry(0, d_a0[:, :], carry_row, carry[0][:, 0:FEAT])
            pool.wait_ge(carry_added, 16)
            pool.wait_ge(filled, FILLED)

            with pool.Fori(0, HALF) as i:
                for j in range(2):
                    gather(L1, d_a0[:, :], got1, j, i, (("sum", 1),), (carry_added, 16))
            pool.wait_ge(L1["stored"][0], 16 * HALF)
            pool.wait_ge(L1["stored"][1], 16 * HALF)
            add_carry(1, d_a1[:, :], carry_row, carry[0][:, 0:HID])
            pool.wait_ge(carry_added, 32)

            gather(L2, d_a1[:, :], got2, 0, 0, (("sum", 1),), (carry_added, 32))
            with pool.Fori(0, HALF - 1) as i:
                gather(L2, d_a1[:, :], got2, 1, i, (("sum", 1),), (carry_added, 32))
                scatter(0, i)
                gather(L2, d_a1[:, :], got2, 0, i + 1, (("sum", 1),), (carry_added, 32))
                scatter(1, i)
            gather(L2, d_a1[:, :], got2, 1, HALF - 1, (("sum", 1),), (carry_added, 32))
            scatter(0, HALF - 1)
            scatter(1, HALF - 1)
            pool.wait_ge(L2["stored"][0], GOT * HALF)
            pool.wait_ge(L2["stored"][1], GOT * HALF)
            add_carry(2, d_nodes[:, :], carry_node, carry64[:, :])

            def nodes(k, s, u):
                static = isinstance(k, int)
                if not static or k < DCHUNKS:
                    above(pool, D["center1"], k - 1)
                    above(pool, D["in"][s], 64 * (u + 1))
                    pool.tensor_tensor(vv[s % 2], xn[s % 2], nr[s][:, :, 0:FEAT], ALU.add).then_inc(D["v"], 1)
                if not static or 1 <= k <= DCHUNKS:
                    above(pool, D["w"], k - 2)
                    above(pool, D["x1"], k)
                    pool.tensor_tensor(zz[(s + 1) % 2], x1n[(s + 1) % 2], nr[(s + 3) % 4][:, :, FEAT + HID:],
                                       ALU.add).then_inc(D["z"], 1)
                if not static or 3 <= k < DCHUNKS + 3:
                    m = (s + 1) % 4
                    uses = 2 * u + ((s - 3) // 2 if s >= 3 else -((3 - s + 1) // 2))
                    above(pool, D["out"][m % 2], 32 * uses)
                    above(pool, D["inv2"], k - 2)
                    pool.tensor_tensor(res[m % 2], cc2[m % 2], over_last(inv2[m % 2], FEAT), ALU.mult) \
                        .then_inc(D["result"], 1)

            over_chunks(pool, nodes, 3)

        @block.tensor
        def _(pe):
            pe.wait_ge(consts_made, CONSTS)

            pe.wait_ge(digits, 2)
            pe.matmul(ps_root[:, 0:1], ones_t[:, 0:P], small[:, 0:1], start=True, stop=True).then_inc(disorder_sum, 1)

            def count_group(g, first, last):
                for s in range(HIST):
                    pe.wait_ge(hot_ready, g * HIST + s + 1)
                    for h in range(2):
                        mm = pe.matmul(ps_hist[0:NPART, 512 * h:512 * h + NCOL // 2], hot[:, s, 0:NPART],
                                       steps[:, s, h * NCOL // 2:(h + 1) * NCOL // 2],
                                       start=first and s == 0, stop=last and s == HIST - 1)
                    mm.then_inc(hot_used, 1)

            count_group(0, True, False)
            with pe.Fori(1, T // HIST - 1) as g:
                count_group(g, False, False)
            count_group(T // HIST - 1, False, True)
            pe.wait_ge(total_ready, 1)
            pe.matmul(ps_root[0:NPART, 0:1], before[0:NPART, 0:NPART], total[0:NPART, :],
                      start=True, stop=True).then_inc(base_ready, 1)
            pe.wait_ge(turn_ready, 1)
            for d in range(2):
                mm = pe.transpose(ps_turn[0:HID, d * P:(d + 1) * P], whole32[:, d, :], ident[:, :])
            mm.then_inc(turn_done, 1)

            def carry_turns(n):
                pe.wait_ge(row_ready, n + 1)
                pe.transpose(ps_root[0:HID, 0:P], tail[:, :], ident[:, :]).then_inc(row_turned, 1)
                pe.wait_ge(scan_ready, n + 1)
                at = 1 if CARRIES[n] else 0
                pe.transpose(ps_root[:, 256:256 + HID], carry_out[:, at:at + P], ident[0:HID, 0:HID]) \
                    .then_inc(back_done, 1)

            carry_turns(0)
            carry_turns(1)

            def turn_chunk(layer, j, i):
                k = i * 2 + j
                pe.wait_ge(layer["padded"][j], i + 1)
                pe.wait_ge(layer["turned_sb"], k)
                for g in range(GROUPS):
                    mm = pe.transpose(ps_turn[:, g * P:(g + 1) * P],
                                      padded[:, 4 * g:4 * g + 4, :].rearrange("p t f -> p (t f)"), ident[:, :])
                mm.then_inc(layer["turned"], 1)

            def products(layer, k, g, turns, w):
                pe.wait_ge(layer["mult"][g % 2], 2 * k + g // 2)
                n, cols = group_tiles(g), w.shape[2]
                at_once = min(n, 512 // cols)
                for t in range(0, n, at_once):
                    mm = pe.matmul(ps_msg[g % 2][:, cols * t:cols * (t + at_once)], turns[:, g * P:(g + 1) * P],
                                   w[:, t:t + at_once, :], start=True, stop=True)
                return mm

            pe.wait_ge(weights_in, 16 * 33)

            def layer0(j, i):
                k = i * 2 + j
                turn_chunk(L0, j, i)
                pe.wait_ge(L0["turned_sb"], k + 1)
                for g in range(GROUPS):
                    products(L0, k, g, turned[0], w0).then_inc(L0["msg"], 1)

            with pe.Fori(0, HALF) as i:
                layer0(0, i)
                layer0(1, i)
            for n in range(2, 5):
                carry_turns(n)

            def layer1(j, i):
                k = i * 2 + j

                def turn(g):
                    if g == 0:
                        pe.wait_ge(L1["outer"], k + 1)
                    above(pe, L1["turned_sb"], 4 * k + g - 1)
                    for t in range(group_tiles(g)):
                        mm = pe.transpose(ps_turns[g % 2][:, P * t:P * t + P],
                                          outer[:, 4 * g + t, :, :].rearrange("p r f -> p (r f)"), ident[:, :])
                    mm.then_inc(L1["turned"], 1)

                def multiply(g):
                    if g == 0:
                        above(pe, L1["root_saved"], k - 1)
                    pe.wait_ge(L1["turned_sb"], 4 * k + g + 1)
                    for t in range(group_tiles(g)):
                        tile = 4 * g + t
                        mm = pe.matmul(ps_msg[j][:, 2 * HID * tile:2 * HID * (tile + 1)],
                                       turned[g % 2][:, P * t:P * t + P], w1[:, :], start=True, stop=True)
                    mm.then_inc(L1["msg"], 1)

                turn(0)
                for g in range(1, GROUPS):
                    turn(g)
                    multiply(g - 1)
                multiply(GROUPS - 1)

            layer1(0, 0)
            layer1(1, 0)
            with pe.Fori(1, HALF) as i:
                layer1(0, i)
                layer1(1, i)
            pe.wait_ge(L1["root_saved"], CHUNKS)
            carry_turns(5)

            def layer2(j, i):
                k = i * 2 + j
                turn_chunk(L2, j, i)
                pe.wait_ge(L2["turned_sb"], k + 1)
                for g in range(GROUPS):
                    products(L2, k, g, turned[0], w2).then_inc(L2["msg"], 1)

            with pe.Fori(0, HALF) as i:
                layer2(0, i)
                layer2(1, i)
            carry_turns(6)

            def nodes(k, s, u):
                static = isinstance(k, int)
                second = not static or 1 <= k <= DCHUNKS

                def turn_x1(g):
                    above(pe, D["x1"], k + 1)
                    above(pe, D["x1t_sb"], 2 * k + g)
                    for m in range(4 * g, min(4 * g + 4, T8)):
                        mm = pe.transpose(ps_turn[:, (m % 4) * NPART:(m % 4 + 1) * NPART],
                                          x1n[s % 2][:, 8 * m:8 * m + 8, :].rearrange("p c f -> p (c f)"), idn)
                    mm.then_inc(D["x1t"], 1)

                def turn_h(g):
                    above(pe, D["ht_sb"], 3 * (k - 1) + g - 1)
                    above(pe, D["h"], 3 * (k - 1) + g + 1)
                    for m in range(4 * g, min(4 * g + 4, T4)):
                        mm = pe.transpose(ps_ht[(s + 1 + g) % 2][:, (m % 4) * NPART:(m % 4 + 1) * NPART],
                                          hn[:, 4 * m:4 * m + 4, :].rearrange("p c f -> p (c f)"), idn)
                    mm.then_inc(D["ht"], 1)

                if second:
                    above(pe, D["x1t_sb"], 2 * k)
                    above(pe, D["h"], 3 * (k - 1))
                    for g in range(3):
                        for m in range(2 * g, min(2 * g + 2, T8)):
                            mm = pe.matmul(ps_h[g][0:NPART, 256 * (m % 2):256 * (m % 2) + 256],
                                           x1t[:, m * NPART:(m + 1) * NPART],
                                           wr1[:, :, :].rearrange("p c f -> p (c f)"), start=True, stop=True)
                        mm.then_inc(D["h_mm"], 1)
                if not static or k < DCHUNKS:
                    turn_x1(0)
                if second:
                    turn_h(0)
                if not static or k < DCHUNKS:
                    turn_x1(1)
                if second:
                    turn_h(1)
                    turn_h(2)
                if second:
                    above(pe, D["w"], k - 1)
                    above(pe, D["ht_sb"], 3 * k)
                    for m in range(T4):
                        mm = pe.matmul(ps_y[:, 64 * m:64 * m + 64], ht[:, m * NPART:(m + 1) * NPART],
                                       wr2[:, :, :].rearrange("p c f -> p (c f)"), start=True, stop=True)
                    mm.then_inc(D["y"], 1)

            over_chunks(pe, nodes, 1)

        @block.scalar
        def _(act):
            act.wait_ge(zeroed, 4)
            for j in range(4):
                block_rows = slice(32 * j, 32 * j + FEAT)
                act.dma_start(w0[block_rows, j, :], W_e).then_inc(weights_in, 16)
                act.dma_start(w0[32 * j + FEAT:32 * j + FEAT + 1, j, :],
                              b_e.rearrange("(a f) -> a f", a=1)).then_inc(weights_in, 16)
                act.dma_start(w2[32 * j:32 * j + HID, j, :].rearrange("p (r o) -> p r o", r=REL),
                              W2.rearrange("r i o -> i r o")).then_inc(weights_in, 16)
                act.dma_start(wr2[32 * j:32 * j + HID, j, :], root2).then_inc(weights_in, 16)
            for m in range(8):
                act.dma_start(wr1[FEAT * m:FEAT * m + FEAT, m, :], root1).then_inc(weights_in, 16)
                act.dma_start(w1[FEAT * m:FEAT * m + FEAT, HID:], root1).then_inc(weights_in, 16)
            act.dma_start(w1[:, 0:HID], W1.rearrange("r i o -> (r i) o")).then_inc(weights_in, 16)
            for c, n, b in ((0, FEAT, bias0), (FEAT, HID, b1), (FEAT + HID, FEAT, b2)):
                act.dma_start(bias_row[:, c:c + n],
                              b.rearrange("(a f) -> a f", a=1).to_broadcast([P, n])).then_inc(bias_in, 16)

            with act.Fori(0, DCHUNKS // 2) as i:
                for j in range(2):
                    act.wait_ge(x_in[j], 32 * (i + 1))
                    act.wait_ge(zeroed, 4)
                    act.activation(xl[:, bass.ds((i * 2 + j) * DC, DC), 0:FEAT],
                                   node_rows[j][0:NPART, :, :].rearrange("p k f -> p (k f)")[:, 0:DC * FEAT]
                                   .rearrange("p (c f) -> p c f", f=FEAT), ACT.Copy).then_inc(x_placed[j], 1)

            def runs_go_on(layer, j, i, f):
                act.wait_ge(layer["scan"][j], i)
                act.wait_ge(prep_done, 1)
                act.activation(keep[j][:, 0:f, 1:], over_rows(same[:, chunk(i * 2 + j)], f, K),
                               ACT.Copy).then_inc(layer["mask"][j], 1)

            def copy_turns(layer, k, to, used):
                act.wait_ge(layer["turned"], k + 1)
                act.wait_ge(layer["msg"], used)
                act.activation(to[:, :], ps_turn[:, :], ACT.Copy).then_inc(layer["turned_sb"], 1)

            def layer0(j, i):
                k = i * 2 + j
                act.wait_ge(L0["att_in"][j], 16 * (i + 1))
                act.wait_ge(L0["turned"], k)
                act.activation(padded[:, 0:K, 0:FEAT], att[j][:, :, :], ACT.Copy).then_inc(L0["padded"][j], 1)
                copy_turns(L0, k, turned[0], 4 * k)
                runs_go_on(L0, j, i, FEAT)
                act.wait_ge(L0["got"][j], GOT * (i + 1))
                act.wait_ge(prep_done, 1)
                act.activation(x_src[:, chunk(k), :], got0[j][:, :, 0:FEAT], ACT.Copy).then_inc(L0["saved"][j], 1)
                act.activation(last_of_src[:, chunk(k)], got0[j][:, :, FEAT], ACT.Copy).then_inc(L0["saved"][j], 1)

            with act.Fori(0, HALF) as i:
                layer0(0, i)
                layer0(1, i)

            act.wait_ge(L0["scan"][0], HALF)
            act.wait_ge(L0["scan"][1], HALF)
            def x1_ahead(j, i):
                k = i * 2 + j
                act.wait_ge(L1["stat"], 3 * k + 2)
                act.activation(sq[:, :, :], cen[:, :, :], ACT.Square).then_inc(L1["squared"], 1)

            def x1_deviation(j, i):
                k = i * 2 + j
                act.wait_ge(L1["stat"], 3 * k + 3)
                act.activation(stat[:, 2, :], stat[:, 1, :], ACT.Sqrt, bias=eps[:, :], scale=1.0 / FEAT) \
                    .then_inc(L1["std"], 1)
                for g in range(GROUPS):
                    above(act, L1["msg"], 4 * k + g - 1)
                    act.wait_ge(L1["turned"], 4 * k + g + 1)
                    n = group_tiles(g) * P
                    act.activation(turned[g % 2][:, 0:n], ps_turns[g % 2][:, 0:n], ACT.Copy) \
                        .then_inc(L1["turned_sb"], 1)

            def layer1(j, i, ahead):
                k = i * 2 + j
                runs_go_on(L1, j, i, HID)
                if ahead:
                    x1_ahead(1 - j, i + j)
                act.wait_ge(L1["msg"], 4 * k + 4)
                act.wait_ge(L1["reduced"], 2 * k + 1)
                act.wait_ge(prep_done, 1)
                act.activation(u_src[:, chunk(k), :], ps_msg[j][:, 0:K * 2 * HID]
                               .rearrange("p (k f) -> p k f", k=K)[:, :, HID:], ACT.Copy).then_inc(L1["root_saved"], 1)
                if ahead:
                    x1_deviation(1 - j, i + j)

            x1_ahead(0, 0)
            x1_deviation(0, 0)
            with act.Fori(0, HALF - 1) as i:
                layer1(0, i, True)
                layer1(1, i, True)
            layer1(0, HALF - 1, True)
            layer1(1, HALF - 1, False)

            act.wait_ge(L1["scan"][0], HALF)
            act.wait_ge(L1["scan"][1], HALF)
            def layer2(j, i):
                k = i * 2 + j
                runs_go_on(L2, j, i, FEAT)
                act.wait_ge(L2["turned"], k)
                act.wait_ge(L2["sum"][j], i + 1)
                act.activation(padded[:, 0:K, :], hsum[:, :, :], ACT.Relu).then_inc(L2["padded"][j], 1)
                copy_turns(L2, k, turned[0], 4 * k)
                act.wait_ge(L2["att_in"][j], 32 * (i + 1))
                act.wait_ge(L2["stored"][j], GOT * i)
                act.activation(node_rows[j][:, :, 0:FEAT], old0[j][:, :, :], ACT.Copy).then_inc(L2["saved"][j], 1)
                act.activation(node_rows[j][:, :, FEAT:FEAT + HID], old1[j][:, :, :], ACT.Copy) \
                    .then_inc(L2["saved"][j], 1)

            with act.Fori(0, HALF) as i:
                layer2(0, i)
                layer2(1, i)

            def deviation(n, k):
                act.activation(dst_[n + "dev"], dst_[n + "ss"], ACT.Sqrt, bias=eps[0:NPART, :], scale=1.0 / FEAT) \
                    .then_inc(D["std" + n], 1)

            def nodes(k, s, u):
                static = isinstance(k, int)
                first = not static or k < DCHUNKS
                hidden = not static or 1 <= k <= DCHUNKS
                second = not static or 2 <= k < DCHUNKS + 2

                def turned_h(g):
                    a, b = 4 * g * NPART, min(4 * g + 4, T4) * NPART
                    above(act, D["y"], k - 1)
                    above(act, D["ht"], 3 * (k - 1) + g + 1)
                    act.activation(ht[:, a:b], ps_ht[(s + 1 + g) % 2][:, 0:b - a], ACT.Relu).then_inc(D["ht_sb"], 1)

                def turned_x1(g):
                    a, b = 4 * g * NPART, min(4 * g + 4, T8) * NPART
                    above(act, D["h_mm"], 3 * k)
                    above(act, D["x1t"], 2 * k + g + 1)
                    act.activation(x1t[:, a:b], ps_turn[:, 0:b - a], ACT.Copy).then_inc(D["x1t_sb"], 1)

                if first:
                    above(act, D["ss1"], k)
                    above(act, D["center1"], k + 1)
                    act.activation(qq[0], cc1[s % 2], ACT.Square).then_inc(D["q1"], 1)
                    above(act, D["ss1"], k + 1)
                    deviation("1", k)
                    turned_x1(0)
                if hidden:
                    turned_h(0)
                if first:
                    turned_x1(1)
                if hidden:
                    turned_h(1)
                if second:
                    above(act, D["ss2"], k - 2)
                    above(act, D["center2"], k - 1)
                    act.activation(qq[1], cc2[s % 2], ACT.Square).then_inc(D["q2"], 1)
                if hidden:
                    turned_h(2)
                if second:
                    above(act, D["inv2"], k - 2)
                    above(act, D["ss2"], k - 1)
                    deviation("2", k)

            over_chunks(act, nodes, 2)

        @block.vector
        def _(dve):
            for w in (w0, w2, wr1, wr2):
                dve.memset(w[:, :, :], 0.0).then_inc(zeroed, 1)
            dve.memset(ones_t[:, :], 1.0).then_inc(consts_made, 1)
            dve.memset(eps[:, :], EPS).then_inc(consts_made, 1)
            dve.memset(tail[:, :], 0.0).then_inc(consts_made, 1)
            dve.memset(carry_out[:, :], 0.0).then_inc(consts_made, 1)
            dve.memset(carry64[:, :], 0.0).then_inc(consts_made, 1)
            dve.memset(padded[:, :, :], 0.0).then_inc(consts_made, 1)
            for j in range(2):
                dve.memset(keep[j][:, :, 0:1], 0.0).then_inc(consts_made, 1)
                dve.memset(scanned[j][:, :, :], 0.0).then_inc(consts_made, 1)
            dve.wait_ge(consts_made, 10)
            dve.memset(padded[:, :, FEAT:FEAT + 1], 1.0).then_inc(consts_made, 1)
            dve.wait_ge(pool_made, 10)
            dve.tensor_copy(iota_lo[:, :], iota_i).then_inc(consts_made, 1)
            dve.tensor_copy(iota_hi[:, :], iota_i[:, 0:P]).then_inc(consts_made, 1)
            dve.tensor_copy(eight[:, :], iota_i[:, 0:REL]).then_inc(consts_made, 1)
            dve.tensor_copy(part[:, :], part_i[:, :]).then_inc(consts_made, 1)
            dve.tensor_copy(dump_row[:, :], edge_i[:, :]).then_inc(consts_made, 1)
            dve.wait_ge(consts_made, 16)
            dve.tensor_scalar(ident[:, :], iota_hi[:, :], part[:, 0:1], None, ALU.is_equal).then_inc(consts_made, 1)
            dve.tensor_scalar(before[:, :], iota_hi[:, :], part[:, 0:1], None, ALU.is_gt).then_inc(consts_made, 1)

            dve.wait_ge(dst0_in, 32)
            dve.tensor_tensor(fix[:, :], dst0_i[:, :], prev_i[:, :], ALU.is_lt).then_inc(digits, 1)
            dve.wait_ge(digits, 1)
            dve.tensor_reduce(small[:, 0:1], fix[:, :], AX.X, ALU.add).then_inc(digits, 1)
            dve.wait_ge(digits, 2)

            dve.tensor_scalar(hi_i[:, :], dst0_i[:, :], 1.0 / NCOL, None, ALU.mult).then_inc(digits, 1)
            dve.wait_ge(digits, 3)
            dve.tensor_copy(hi[:, :], hi_i[:, :]).then_inc(digits, 1)
            dve.wait_ge(digits, 4)
            dve.scalar_tensor_tensor(lo[:, :], hi[:, :], -float(NCOL), dst0_i[:, :], ALU.mult, ALU.add) \
               .then_inc(digits, 1)
            dve.wait_ge(digits, 5)
            dve.tensor_scalar(fix[:, :], lo[:, :], 0.0, None, ALU.is_lt).then_inc(digits, 1)
            dve.wait_ge(digits, 6)
            dve.tensor_tensor(hi[:, :], hi[:, :], fix[:, :], ALU.subtract).then_inc(digits, 1)
            dve.scalar_tensor_tensor(lo[:, :], fix[:, :], float(NCOL), lo[:, :], ALU.mult, ALU.add) \
               .then_inc(digits, 1)
            dve.wait_ge(digits, 8)
            dve.tensor_scalar(fix[:, :], lo[:, :], float(NCOL), None, ALU.is_ge).then_inc(digits, 1)
            dve.wait_ge(digits, 9)
            dve.tensor_tensor(hi[:, :], hi[:, :], fix[:, :], ALU.add).then_inc(digits, 1)
            dve.scalar_tensor_tensor(lo[:, :], fix[:, :], -float(NCOL), lo[:, :], ALU.mult, ALU.add) \
               .then_inc(digits, 1)
            dve.wait_ge(digits, 11)

            dve.wait_ge(disorder_sum, 1)
            dve.tensor_copy(unsorted[:, :], ps_root[0:1, 0:1]).then_inc(flag_ready, 1)

            dve.wait_ge(bias_in, 48)
            dve.tensor_copy(fill[:, :, :], over_rows(bias_row[:, :], FILL, ROW)).then_inc(fill_made, 1)

            def count_tile(s, t, used):
                if used is not None:
                    dve.wait_ge(hot_used, used)
                dve.tensor_scalar(hot[:, s, :], iota_hi[:, :], hi[:, bass.ds(t, 1)], None, ALU.is_equal)
                dve.tensor_scalar(steps[:, s, :], iota_lo[:, :], lo[:, bass.ds(t, 1)], None, ALU.is_ge) \
                   .then_inc(hot_ready, 1)

            for s in range(HIST):
                count_tile(s, s, None)
            with dve.Fori(1, T // HIST) as g:
                for s in range(HIST):
                    count_tile(s, g * HIST + s, g * HIST + s - (HIST - 1))

            dve.wait_ge(hot_used, T)
            dve.tensor_copy(total[0:NPART, :], ps_hist[0:NPART, 512 + NCOL // 2 - 1:512 + NCOL // 2]) \
               .then_inc(total_ready, 1)
            dve.wait_ge(base_ready, 1)
            dve.tensor_copy(ends[:, 0:1], ps_root[0:NPART, 0:1]).then_inc(last_step, 1)
            dve.wait_ge(last_step, 1)
            for h in range(2):
                dve.tensor_scalar(ends[:, 1 + h * NCOL // 2:1 + (h + 1) * NCOL // 2],
                                  ps_hist[0:NPART, 512 * h:512 * h + NCOL // 2], ends[:, 0:1], None, ALU.add) \
                   .then_inc(last_step, 1)
            dve.wait_ge(last_step, 3)
            dve.tensor_tensor(count_step, ends[:, 1:], ends[:, 0:NCOL], ALU.subtract).then_inc(last_step, 1)
            dve.tensor_scalar(last_edge, ends[:, 1:], part[0:NPART, 2:3], 1.0, ALU.subtract, ALU.subtract) \
               .then_inc(last_step, 1)
            dve.wait_ge(last_step, 5)
            dve.scalar_tensor_tensor(last_edge, count_step, 0.0, last_edge, ALU.is_gt, ALU.mult).then_inc(last_step, 1)
            dve.wait_ge(last_step, 6)
            dve.wait_ge(x_placed[0], DCHUNKS // 2)
            dve.wait_ge(x_placed[1], DCHUNKS // 2)
            dve.tensor_scalar(xl[:, :, FEAT], last_edge, part[0:NPART, 2:3], None, ALU.add).then_inc(last_step, 1)

            with dve.If(dve.value_load(unsorted[0:1, 0:1], min_val=0, max_val=EP)):
                dve.tensor_copy(lo[:, :], dst0_i[:, :]).then_inc(sort_step, 1)
                dve.tensor_scalar(before[:, :], iota_hi[:, :], part[:, 0:1], None, ALU.is_lt).then_inc(sort_step, 1)
                dve.memset(hi[:, :], 0.0).then_inc(sort_step, 1)
                dve.tensor_copy(run_up[:, :], iota_lo[:, 0:T]).then_inc(sort_step, 1)
                dve.wait_ge(sort_step, 4)
                with dve.Fori(0, SORT_CHUNKS) as c:
                    dve.wait_ge(sort_row_in, 16 * (c + 1))
                    dve.scalar_tensor_tensor(sort_low.rearrange("p (q t) -> p q t", t=T),
                                             over_last(before[:, bass.ds(c * SORT_PARTS, SORT_PARTS)], T), -0.5,
                                             sort_row.rearrange("p (q t) -> p q t", t=T), ALU.mult, ALU.add) \
                       .then_inc(sort_read, 1)
                    with dve.Fori(0, T) as t:
                        dve.wait_ge(sort_read, c + 1)
                        dve.tensor_scalar(sort_less, sort_low, lo[:, bass.ds(t, 1)], None, ALU.is_lt) \
                           .then_inc(sort_cmp, 1)
                        dve.wait_ge(sort_cmp, c * (2 * T + 1) + 2 * t + 1)
                        dve.tensor_reduce(fix[:, bass.ds(t, 1)], sort_less, AX.X, ALU.add).then_inc(sort_cmp, 1)
                        dve.wait_ge(sort_cmp, c * (2 * T + 1) + 2 * t + 2)
                    dve.tensor_tensor(hi[:, :], hi[:, :], fix[:, :], ALU.add).then_inc(sort_cmp, 1)
                    dve.wait_ge(sort_cmp, (c + 1) * (2 * T + 1))
                ranked_from = SORT_CHUNKS * (2 * T + 1)
                with dve.Fori(0, T) as t:
                    dve.tensor_scalar(run_down[:, :], lo[:, :], lo[:, bass.ds(t, 1)], None, ALU.is_equal) \
                       .then_inc(sort_cmp, 1)
                    dve.wait_ge(sort_cmp, 3 * t + (ranked_from + 1))
                    dve.scalar_tensor_tensor(first_run[:, :], run_up[:, :], run_up[:, bass.ds(t, 1)], run_down[:, :],
                                             ALU.is_lt, ALU.mult).then_inc(sort_cmp, 1)
                    dve.wait_ge(sort_cmp, 3 * t + (ranked_from + 2))
                    dve.tensor_reduce(fix[:, bass.ds(t, 1)], first_run[:, :], AX.X, ALU.add).then_inc(sort_cmp, 1)
                    dve.wait_ge(sort_cmp, 3 * t + (ranked_from + 3))
                dve.tensor_tensor(cur_i[:, :], hi[:, :], fix[:, :], ALU.add).then_inc(sort_step, 1)
                dve.wait_ge(sort_step, 5)
                dve.tensor_scalar(node_row[:, :], cur_i[:, :], 1.0, None, ALU.add).then_inc(sort_ranked, 1)

            steps_done = 0

            def step(ins):
                nonlocal steps_done
                steps_done += 1
                ins.then_inc(prep, 1)
                return steps_done

            dve.wait_ge(edges_in, 64)
            step(dve.tensor_tensor(same[:, :], cur_i[:, :], prev_i[:, :], ALU.is_equal))
            n = step(dve.tensor_tensor(same_next[:, :], cur_i[:, :], next_i[:, :], ALU.is_equal))
            dve.wait_ge(prep, n)
            step(dve.tensor_tensor_scan(run_up[:, :], same[:, :], ones_t[:, :], 0.0, ALU.mult, ALU.add))
            step(dve.tensor_tensor_scan(back(run_down[:, :]), back(same_next[:, :]), ones_t[:, :], 0.0,
                                        ALU.mult, ALU.add))
            step(dve.tensor_tensor_scan(first_run[:, :], same[:, :], ones_t[:, :], 1.0, ALU.mult, ALU.mult))
            n = step(dve.tensor_tensor_scan(back(last_run[:, :]), back(same_next[:, :]), ones_t[:, :], 1.0,
                                            ALU.mult, ALU.mult))
            dve.wait_ge(prep, n)
            step(dve.tensor_copy(whole[:, 0:1], first_run[:, T - 1:T]))
            n = step(dve.tensor_copy(whole[:, 1:2], last_run[:, 0:1]))
            dve.wait_ge(prep, n)
            dve.tensor_copy(whole32[:, :, :], over_last(whole[:, :], HID)).then_inc(turn_ready, 1)
            dve.wait_ge(turn_done, 1)
            n = step(dve.tensor_copy(whole_rows[:, :, :], ps_turn[0:HID, 0:2 * P].rearrange("p (d q) -> p d q", d=2)))
            dve.wait_ge(prep, n)

            def bring_along(n):
                dve.wait_ge(row_turned, n + 1)
                dve.tensor_copy(tail_row[:, :], ps_root[0:HID, 0:P]).then_inc(row_copied, 1)
                dve.wait_ge(row_copied, n + 1)
                if CARRIES[n] == 0:
                    dve.tensor_tensor_scan(carry_out[:, 1:P + 1], whole_rows[:, 0, :], tail_row[:, :], 0.0,
                                           ALU.mult, ALU.add).then_inc(scan_ready, 1)
                else:
                    dve.tensor_tensor_scan(back(carry_out[:, 0:P]), back(whole_rows[:, 1, :]), back(tail_row[:, :]),
                                           0.0, ALU.mult, ALU.add).then_inc(scan_ready, 1)
                dve.wait_ge(back_done, n + 1)

            def clear_end(n):
                at = 0 if CARRIES[n] == 0 else P
                return dve.memset(carry_out[:, at:at + 1], 0.0)

            for n, (of, at) in enumerate(((run_up, T - 1), (run_down, 0))):
                m = step(clear_end(n))
                dve.wait_ge(prep, m)
                dve.tensor_copy(tail[:, 0:1], of[:, at:at + 1]).then_inc(row_ready, 1)
                bring_along(n)
                m = step(dve.tensor_copy(carry[n][:, :], ps_root[:, 256:256 + HID]))
                dve.wait_ge(prep, m)
            step(dve.tensor_tensor_scan(run_up[:, :], same[:, :], ones_t[:, :], carry[0][:, 0:1], ALU.mult, ALU.add))
            n = step(dve.tensor_tensor_scan(back(run_down[:, :]), back(same_next[:, :]), ones_t[:, :],
                                            carry[1][:, 0:1], ALU.mult, ALU.add))
            dve.wait_ge(prep, n)
            n = step(dve.tensor_tensor(inv_count[:, :], run_up[:, :], run_down[:, :], ALU.add))
            dve.wait_ge(prep, n)
            n = step(dve.tensor_scalar(inv_count[:, :], inv_count[:, :], -1.0, 1.0, ALU.add, ALU.max))
            dve.wait_ge(prep, n)
            n = step(dve.reciprocal(inv_count[:, :], inv_count[:, :]))
            dve.wait_ge(prep, n)

            n = step(dve.tensor_tensor(fix[:, :], dump_row[:, :], cur_i[:, :], ALU.subtract))
            dve.wait_ge(prep, n)
            n = step(dve.tensor_tensor(fix[:, :], fix[:, :], same_next[:, :], ALU.mult))
            dve.wait_ge(prep, n)
            n = step(dve.tensor_tensor(node_row[:, :], fix[:, :], cur_i[:, :], ALU.add))
            step(dve.tensor_reduce(small[:, 0:1], first_run[:, :], AX.X, ALU.add))
            n = step(dve.tensor_copy(small[:, 4:5], cur_i[:, 0:1]))
            dve.wait_ge(prep, n)
            step(dve.tensor_scalar(small[:, 1:2], small[:, 0:1], -1.0, 0.0, ALU.add, ALU.max))
            step(dve.tensor_tensor(small[:, 3:4], whole[:, 0:1], same_next[:, T - 1:T], ALU.mult))
            n = step(dve.tensor_tensor(small[:, 5:6], part[:, 3:4], small[:, 4:5], ALU.subtract))
            dve.wait_ge(prep, n)
            step(dve.tensor_tensor(carry_row[:, :], small[:, 1:2], part[:, 1:2], ALU.add))
            n = step(dve.tensor_tensor(small[:, 6:7], small[:, 5:6], small[:, 3:4], ALU.mult))
            dve.wait_ge(prep, n)
            dve.tensor_tensor(carry_node[:, :], small[:, 6:7], small[:, 4:5], ALU.add).then_inc(prep_done, 1)

            PARTS = {id(L0): 5, id(L1): 2, id(L2): 6}

            def run_sums(layer, j, i, f):
                k, parts = i * 2 + j, PARTS[id(layer)]
                dve.wait_ge(layer["scan"][1 - j], i + j)
                dve.tensor_copy(part_sum[j][:, 0:f, 0:1], scanned[1 - j][:, 0:f, K:K + 1]).then_inc(layer["reduced"], 1)
                dve.wait_ge(layer["mask"][j], i + 1)
                dve.wait_ge(layer["reduced"], parts * k + parts)
                dve.tensor_tensor_scan(scanned[j][:, 0:f, :].rearrange("p f k -> p (f k)"),
                                       keep[j][:, 0:f, :].rearrange("p f k -> p (f k)"),
                                       part_sum[j][:, 0:f, :].rearrange("p f k -> p (f k)"),
                                       0.0, ALU.mult, ALU.add).then_inc(layer["scan"][j], 1)

            def sums_out(layer, j, i, f, b0):
                dve.wait_ge(layer["scan"][j], i + 1)
                dve.wait_ge(layer["stored"][j], (16 if layer is not L2 else GOT) * i)
                if layer is L2:
                    to = node_rows[j][:, :, FEAT + HID:]
                else:
                    to = rows[j][:, 0:K * f].rearrange("p (k f) -> p k f", k=K)
                dve.tensor_tensor(to, scanned[j][:, 0:f, 1:].rearrange("p f k -> p k f"),
                                  over_rows(bias_row[:, b0:b0 + f], K, f), ALU.add).then_inc(layer["rows"][j], 1)

            def messages(layer, j, i, a, b, scale_of):
                k, parts = i * 2 + j, PARTS[id(layer)]

                def scale(g):
                    n = group_tiles(g)
                    if g >= 2:
                        dve.wait_ge(layer["reduced"], parts * k + g - 1)
                    dve.wait_ge(layer["msg"], 4 * k + g + 1)
                    dve.tensor_tensor(prod[g % 2][:, 0:n * a * b].rearrange("p (t a b) -> p t a b", t=n, a=a),
                                      ps_msg[g % 2][:, 0:n * a * b].rearrange("p (t a b) -> p t a b", t=n, a=a),
                                      over_last(scale_of(g, n), b), ALU.mult).then_inc(layer["mult"][g % 2], 1)

                def add(g):
                    n = group_tiles(g)
                    dve.wait_ge(layer["mult"][g % 2], 2 * k + g // 2 + 1)
                    dve.tensor_reduce(part_sum[j][:, 0:b, 1 + 4 * g:1 + 4 * g + n].rearrange("p b t -> p t b"),
                                      prod[g % 2][:, 0:n * a * b].rearrange("p (t a b) -> p t b a", t=n, a=a),
                                      AX.X, ALU.add).then_inc(layer["reduced"], 1)

                scale(0)
                for g in range(1, GROUPS):
                    scale(g)
                    add(g - 1)
                add(GROUPS - 1)

            def layer0(j, i):
                k = i * 2 + j
                dve.wait_ge(L0["got"][j], GOT * (i + 1))
                dve.tensor_tensor(xc[:, :, :], got0[j][:, :, 0:FEAT], over_last(inv_count[:, chunk(k)], FEAT),
                                  ALU.mult).then_inc(L0["scaled"][j], 1)
                dve.wait_ge(L0["scaled"][j], i + 1)
                messages(L0, j, i, FEAT, FEAT, lambda g, n: xc[:, 4 * g:4 * g + n, :])
                run_sums(L0, j, i, FEAT)
                sums_out(L0, j, i, FEAT, 0)

            with dve.Fori(0, HALF) as i:
                layer0(0, i)
                layer0(1, i)

            def sum_carry(n, layer, f, to):
                dve.wait_ge(layer["scan"][1], HALF)
                m = step(clear_end(n))
                dve.wait_ge(prep, m)
                dve.tensor_copy(tail[:, 0:f], scanned[1][:, 0:f, K]).then_inc(row_ready, 1)
                bring_along(n)
                dve.tensor_scalar(to, ps_root[:, 256:256 + f], same[:, 0:1], None, ALU.mult).then_inc(carry_ready, 1)

            sum_carry(2, L0, FEAT, carry[0][:, 0:FEAT])

            n = step(dve.tensor_tensor(rel[:, :, :], over_last(typ_i[:, :], REL), over_rows(eight[:, :], T, REL),
                                       ALU.is_equal))
            dve.wait_ge(prep, n)
            dve.wait_ge(row_turned, 3)
            m = step(clear_end(3))
            dve.wait_ge(prep, m)
            for r in range(REL):
                m = step(dve.tensor_tensor_scan(run_up[:, :], same[:, :], rel[:, :, r], 0.0, ALU.mult, ALU.add))
                dve.wait_ge(prep, m)
                ins = dve.tensor_copy(tail[:, r:r + 1], run_up[:, T - 1:T])
                if r == REL - 1:
                    ins.then_inc(row_ready, 1)
                else:
                    m = step(ins)
                    dve.wait_ge(prep, m)
            for r in range(REL):
                m = step(dve.tensor_tensor_scan(back(run_down[:, :]), back(same_next[:, :]), back(rel[:, :, r]), 0.0,
                                                ALU.mult, ALU.add))
                dve.wait_ge(prep, m)
                m = step(dve.tensor_copy(heads[:, r:r + 1], run_down[:, 0:1]))
                dve.wait_ge(prep, m)
            bring_along(3)
            m = step(dve.tensor_copy(up8[:, :], ps_root[:, 256:256 + REL]))
            m = step(clear_end(4))
            dve.wait_ge(prep, m)
            dve.tensor_copy(tail[:, 0:REL], heads[:, :]).then_inc(row_ready, 1)
            bring_along(4)
            m = step(dve.tensor_copy(down8[:, :], ps_root[:, 256:256 + REL]))
            dve.wait_ge(prep, m)
            for r in range(REL):
                step(dve.tensor_tensor_scan(run_up[:, :], same[:, :], rel[:, :, r], up8[:, r:r + 1],
                                            ALU.mult, ALU.add))
                m = step(dve.tensor_tensor_scan(back(run_down[:, :]), back(same_next[:, :]), back(rel[:, :, r]),
                                                down8[:, r:r + 1], ALU.mult, ALU.add))
                dve.wait_ge(prep, m)
                m = step(dve.tensor_tensor(fix[:, :], run_up[:, :], run_down[:, :], ALU.add))
                dve.wait_ge(prep, m)
                to = first_run if r == 0 else last_run
                m = step(dve.tensor_tensor(to[:, :], fix[:, :], rel[:, :, r], ALU.mult))
                dve.wait_ge(prep, m)
                if r:
                    m = step(dve.tensor_tensor(first_run[:, :], first_run[:, :], last_run[:, :], ALU.add))
                    dve.wait_ge(prep, m)
            m = step(dve.tensor_scalar(first_run[:, :], first_run[:, :], -1.0, 1.0, ALU.add, ALU.max))
            dve.wait_ge(prep, m)
            m = step(dve.reciprocal(inv_rel[:, :], first_run[:, :]))
            dve.wait_ge(prep, m)
            dve.wait_ge(L0["scan"][1], HALF)
            m = step(dve.memset(scanned[1][:, :, :], 0.0))
            dve.wait_ge(prep, m)

            dve.wait_ge(L0["stored"][0], 16 * HALF)
            dve.wait_ge(L0["stored"][1], 16 * HALF)

            def x1_sums(j, i):
                k = i * 2 + j
                above(dve, L1["x1"], k)
                dve.wait_ge(L1["got"][j], GOT * (i + 1))
                dve.tensor_tensor(cen[:, :, :], x_src[:, chunk(k), :], got1[j][:, :, :], ALU.add) \
                   .then_inc(L1["sum"][j], 1)
                dve.wait_ge(L1["sum"][j], i + 1)
                dve.tensor_reduce(stat[:, 0, :], cen[:, :, :], AX.X, ALU.add).then_inc(L1["stat"], 1)
                dve.wait_ge(L1["stat"], 3 * k + 1)
                dve.scalar_tensor_tensor(cen[:, :, :], over_last(stat[:, 0, :], FEAT), -1.0 / FEAT, cen[:, :, :],
                                         ALU.mult, ALU.add).then_inc(L1["stat"], 1)

            def x1_squares(j, i):
                k = i * 2 + j
                dve.wait_ge(L1["squared"], k + 1)
                dve.tensor_reduce(stat[:, 1, :], sq[:, :, :], AX.X, ALU.add).then_inc(L1["stat"], 1)

            def x1_rows(j, i):
                k = i * 2 + j
                dve.wait_ge(L1["std"], k + 1)
                dve.reciprocal(stat[:, 3, :], stat[:, 2, :]).then_inc(L1["inv"], 1)
                dve.wait_ge(L1["inv"], k + 1)
                dve.tensor_tensor(xc[:, :, :], cen[:, :, :], over_last(stat[:, 3, :], FEAT), ALU.mult) \
                   .then_inc(L1["x1"], 1)
                dve.wait_ge(L1["x1"], k + 1)
                above(dve, L1["turned"], 4 * k)
                dve.tensor_tensor(outer, over_last(rel[:, chunk(k), :], FEAT),
                                  xc[:, :, :].unsqueeze(2).to_broadcast([P, K, REL, FEAT]), ALU.mult) \
                   .then_inc(L1["outer"], 1)

            def layer1(j, i, ahead):
                k, nxt = i * 2 + j, (1 - j, i + j)
                if ahead:
                    x1_sums(*nxt)
                dve.wait_ge(L1["msg"], 4 * k + 4)
                dve.tensor_tensor(part_sum[j][:, :, 1:].rearrange("p f k -> p k f"),
                                  ps_msg[j][:, 0:K * 2 * HID].rearrange("p (k f) -> p k f", k=K)[:, :, 0:HID],
                                  over_last(inv_rel[:, chunk(k)], HID), ALU.mult).then_inc(L1["reduced"], 1)
                if ahead:
                    x1_squares(*nxt)
                run_sums(L1, j, i, HID)
                if ahead:
                    x1_rows(*nxt)
                sums_out(L1, j, i, HID, FEAT)

            x1_sums(0, 0)
            x1_squares(0, 0)
            x1_rows(0, 0)
            with dve.Fori(0, HALF - 1) as i:
                layer1(0, i, True)
                layer1(1, i, True)
            layer1(0, HALF - 1, True)
            layer1(1, HALF - 1, False)
            dve.wait_ge(carry_added, 16)
            sum_carry(5, L1, HID, carry[0][:, :])
            m = step(dve.memset(scanned[1][:, :, :], 0.0))
            dve.wait_ge(prep, m)

            def layer2(j, i):
                k = i * 2 + j
                dve.wait_ge(L2["padded"][1 - j], i + j)
                dve.wait_ge(L2["got"][j], GOT * (i + 1))
                dve.tensor_tensor(hsum[:, :, :], u_src[:, chunk(k), :], got2[j][:, :, :], ALU.add) \
                   .then_inc(L2["sum"][j], 1)
                messages(L2, j, i, REL, FEAT, lambda g, n: rel[:, bass.ds(k * K + 4 * g, n), :])
                sums = part_sum[j][:, 0:FEAT, 1:].rearrange("p f k -> p k f")
                dve.wait_ge(L2["reduced"], 6 * k + 4)
                dve.tensor_tensor(sums, sums, over_last(inv_rel[:, chunk(k)], FEAT), ALU.mult).then_inc(L2["reduced"], 1)
                run_sums(L2, j, i, FEAT)
                sums_out(L2, j, i, FEAT, FEAT + HID)

            with dve.Fori(0, HALF) as i:
                layer2(0, i)
                layer2(1, i)
            sum_carry(6, L2, FEAT, carry64[:, FEAT + HID:])

            def hidden(k, s, g):
                if not isinstance(k, int) or 1 <= k <= DCHUNKS:
                    n = min(16, DC - 16 * g)
                    above(dve, D["h_mm"], 3 * (k - 1) + g + 1)
                    above(dve, D["ht"], 3 * (k - 2) + g + 1)
                    dve.tensor_tensor(hn[:, 16 * g:16 * g + n, :],
                                      ps_h[g][0:NPART, 0:n * HID].rearrange("p (c f) -> p c f", f=HID),
                                      nr[(s + 3) % 4][:, 16 * g:16 * g + n, FEAT:FEAT + HID],
                                      ALU.add).then_inc(D["h"], 1)

            def nodes(k, s, u):
                static = isinstance(k, int)
                first = not static or k < DCHUNKS
                second = not static or 2 <= k < DCHUNKS + 2
                if not static or 3 <= k < DCHUNKS + 3:
                    above(dve, D["std2"], k - 2)
                    above(dve, D["result"], k - 4)
                    dve.reciprocal(inv2[(s + 1) % 2], dst_["2dev"]).then_inc(D["inv2"], 1)
                if first:
                    above(dve, D["v"], k + 1)
                    dve.tensor_reduce(dst_["1sum"], vv[s % 2], AX.X, ALU.add).then_inc(D["stat1"], 1)
                    above(dve, D["q1"], k - 1)
                    above(dve, D["stat1"], 2 * k + 1)
                    dve.scalar_tensor_tensor(cc1[s % 2], over_last(dst_["1sum"], FEAT), -1.0 / FEAT, vv[s % 2],
                                             ALU.mult, ALU.add).then_inc(D["center1"], 1)
                if second:
                    above(dve, D["z"], k - 1)
                    above(dve, D["y"], k - 1)
                    above(dve, D["center2"], k - 2)
                    dve.tensor_tensor(ww, ps_y.rearrange("p (c f) -> p c f", f=FEAT),
                                      zz[s % 2], ALU.add).then_inc(D["w"], 1)
                if first:
                    above(dve, D["q1"], k + 1)
                    dve.tensor_reduce(dst_["1ss"], qq[0], AX.X, ALU.add).then_inc(D["ss1"], 1)
                if second:
                    above(dve, D["w"], k - 1)
                    dve.tensor_reduce(dst_["2sum"], ww, AX.X, ALU.add).then_inc(D["sum2"], 1)
                if first:
                    above(dve, D["std1"], k + 1)
                    dve.reciprocal(dst_["1inv"], dst_["1dev"]).then_inc(D["stat1"], 1)
                    above(dve, D["stat1"], 2 * k + 2)
                    above(dve, D["x1t"], 2 * (k - 1))
                    above(dve, D["z"], k - 1)
                    dve.tensor_tensor(x1n[s % 2], cc1[s % 2], over_last(dst_["1inv"], FEAT), ALU.mult) \
                       .then_inc(D["x1"], 1)
                hidden(k, s, 0)
                hidden(k, s, 1)
                if second:
                    above(dve, D["sum2"], k - 1)
                    above(dve, D["result"], k - 3)
                    dve.scalar_tensor_tensor(cc2[s % 2], over_last(dst_["2sum"], FEAT), -1.0 / FEAT, ww,
                                             ALU.mult, ALU.add).then_inc(D["center2"], 1)
                hidden(k, s, 2)
                if second:
                    above(dve, D["q2"], k - 1)
                    dve.tensor_reduce(dst_["2ss"], qq[1], AX.X, ALU.add).then_inc(D["ss2"], 1)

            over_chunks(dve, nodes, 3)


_INS = ["x", "src", "dst", "edge_attr_16", "edge_type_8", "L0_gnn_W_e", "L0_gnn_b_e", "L0_gnn_bias",
        "L1_gnn_W1", "L1_gnn_root1", "L1_gnn_b1", "L1_gnn_W2", "L1_gnn_root2", "L1_gnn_b2"]


def kernel(**inputs):
    import concourse.bacc as bacc
    from concourse.bass_utils import run_bass_kernel_spmd

    nc = bacc.Bacc("TRN2", target_bir_lowering=False, num_devices=1)
    arrays, args = {}, []
    for name in _INS:
        a = np.ascontiguousarray(inputs[name])
        arrays[f"in_{name}"] = a
        args.append(nc.dram_tensor(f"in_{name}", a.shape, mybir.dt.from_np(a.dtype), kind="ExternalInput").ap())
    out = nc.dram_tensor("out", inputs["x"].shape, F32, kind="ExternalOutput").ap()
    bass_gnn_resnorm(nc, *args, out)
    r = run_bass_kernel_spmd(nc, [arrays], core_ids=[0])
    return r.results[0]["out"]
```

```python
from contextlib import ExitStack

import numpy as np

import concourse.bass as bass
from concourse import mybir

ALU = mybir.AluOpType
ACT = mybir.ActivationFunctionType
AX = mybir.AxisListType
F32 = mybir.dt.float32
F16 = mybir.dt.float16
BF16 = mybir.dt.bfloat16
I32 = mybir.dt.int32

P = 128
FEAT = 16
HID = 32
REL = 8
EPS = 1e-5
K = 14
GROUPS = 4
PAD = 4 * GROUPS
STEPCOLS = 17
ROW = FEAT + HID + FEAT
HIST = K
HIST_HOT = HIST // 2
HIST_ACT = (1, 3, 5, 8, 10, 12)


def group_tiles(g):
    return min(4, K - 4 * g)


def bass_gnn_resnorm(nc, x, src, dst, edge_attr, edge_type, W_e, b_e, bias0,
                     W1, root1, b1, W2, root2, b2, out):
    N, _ = x.shape
    E = src.shape[0]
    T = -(-E // (P * 2 * K)) * 2 * K
    EP = P * T
    CHUNKS = T // K
    HALF = CHUNKS // 2
    NPART = 125
    NCOL = N // NPART
    assert NPART * NCOL == N and E <= EP and T % HIST == 0
    FILL = 16
    assert NCOL % FILL == 0
    DC = 40
    DCHUNKS = NCOL // DC
    T8, T4 = DC // 8, DC // 4
    DUMP = N + 1
    NROWS = DUMP + EP + P

    d_src = nc.dram_tensor("edge_src", (EP,), I32, kind="Internal").ap()
    d_dst = nc.dram_tensor("edge_dst", (EP + 2,), I32, kind="Internal").ap()
    d_typ = nc.dram_tensor("edge_typ", (EP,), I32, kind="Internal").ap()
    d_ea = nc.dram_tensor("edge_att", (EP, FEAT), F32, kind="Internal").ap()
    d_xl = nc.dram_tensor("node_x_last", (N, STEPCOLS), F32, kind="Internal").ap()
    d_a0 = nc.dram_tensor("edge_sum0", (EP + P, FEAT), F32, kind="Internal").ap()
    d_a1 = nc.dram_tensor("edge_sum1", (EP + P, HID), F32, kind="Internal").ap()
    d_nodes = nc.dram_tensor("node_sums", (NROWS, ROW), F32, kind="Internal").ap()

    def by_edge(ap):
        return ap.rearrange("(p t) -> p t", p=P)

    def by_edge_row(ap):
        return ap.rearrange("(p t) f -> p t f", p=P)

    d_cur, d_prev, d_next = (by_edge(d_dst[s:s + EP]) for s in (1, 0, 2))
    d_src_t, d_typ_t = by_edge(d_src), by_edge(d_typ)
    d_ea_t = by_edge_row(d_ea)
    d_a0_t, d_a1_t = by_edge_row(d_a0[0:EP, :]), by_edge_row(d_a1[0:EP, :])
    x_t = x.rearrange("(p c) f -> p c f", p=NPART)
    out_t = out.rearrange("(p c) f -> p c f", p=NPART)
    d_xl_t = d_xl.rearrange("(p c) f -> p c f", p=NPART)
    d_nodes_t = d_nodes[0:N, :].rearrange("(p c) f -> p c f", p=NPART)
    NODE_PARTS = (slice(0, 112), slice(112, NPART))

    with ExitStack() as ctx:
        def sb(name, shape, dt=F32):
            return ctx.enter_context(nc.sbuf_tensor(name, shape, dt))

        def psum(name, shape):
            return ctx.enter_context(nc.psum_tensor(name, shape, F32))

        def sem(name):
            return ctx.enter_context(nc.semaphore(name))

        def pair(name, shape, dt=F32):
            return [sb(f"{name}{j}", shape, dt) for j in range(2)]

        ps_turn = psum("ps_turn", [P, 512])
        ps_root = psum("ps_root", [P, 512])
        ps_m = psum("ps_m", [P, 2048])
        ps_msg = [ps_m[:, 0:1024], ps_m[:, 1024:2048]]
        ps_hist = psum("ps_hist", [P, 1024])
        ps_turns = [ps_turn, ps_hist]

        ident = sb("ident", [P, P])
        iota_lo = sb("iota_lo", [P, NCOL], F16)
        iota_hi = sb("iota_hi", [P, P], F16)
        part_i = sb("part_i", [P, 4], I32)
        part = sb("part", [P, 4])
        dump_row = sb("dump_row", [P, T])
        before = sb("before", [P, P])
        eight = sb("eight", [P, REL])
        ones_t = sb("ones_t", [P, T])
        eps = sb("eps", [P, 1])
        w0 = sb("w0", [P, 4, 256])
        w1 = sb("w1", [P, 2 * HID])
        w2 = sb("w2", [P, 4, REL * FEAT])
        wr1 = sb("wr1", [P, 8, HID])
        wr2 = sb("wr2", [P, 4, FEAT])
        bias_row = sb("bias_row", [P, ROW])
        fill = sb("fill", [P, FILL, ROW])
        pad_dst = sb("pad_dst", [1, EP - E + 2], I32)
        pad_i = sb("pad_i", [1, EP - E], I32)
        pad_att = sb("pad_att", [FEAT, EP - E])

        dst0_i = sb("dst0_i", [P, T], I32)
        cur_i = sb("cur_i", [P, T], I32)
        prev_i = sb("prev_i", [P, T], I32)
        next_i = sb("next_i", [P, T], I32)
        typ_i = sb("typ_i", [P, T], I32)
        hi = sb("hi", [P, T])
        lo = sb("lo", [P, T])
        half_lo = sb("half_lo", [P, T])
        fix = sb("fix", [P, T])
        same = sb("same", [P, T])
        same_next = sb("same_next", [P, T])
        run_up = sb("run_up", [P, T])
        run_down = sb("run_down", [P, T])
        inv_count = sb("inv_count", [P, T])
        first_run = sb("first_run", [P, T])
        last_run = sb("last_run", [P, T])
        node_row = sb("node_row", [P, T], I32)
        last_of_src = sb("last_of_src", [P, T], I32)
        x_src = sb("x_src", [P, T, FEAT])
        rel = sb("rel", [P, T, REL])
        inv_rel = sb("inv_rel", [P, T])
        arena = sb("arena", [P, NCOL * STEPCOLS])
        xl = arena[0:NPART, :].rearrange("p (c f) -> p c f", f=STEPCOLS)
        u_src = arena[:, 0:T * HID].rearrange("p (t f) -> p t f", f=HID)
        spare = x_src[:, :, :].rearrange("p t f -> p (t f)")
        iota_i = spare[:, 0:NCOL].bitcast(I32)
        count_step = spare[0:NPART, NCOL:2 * NCOL]
        last_edge = spare[0:NPART, 2 * NCOL:3 * NCOL]
        ends = spare[0:NPART, 3 * NCOL:4 * NCOL + 1]
        edge_i = last_of_src
        hi_i = node_row
        half = HIST // 2 * NCOL // 2
        step_halves = [rel[:, :, :].rearrange("p t f -> p (t f)")[:, 0:half], spare[:, T * FEAT - half:]]
        step_halves = [h.bitcast(BF16).rearrange("p (s c) -> p s c", c=NCOL) for h in step_halves]
        steps = [step_halves[s // (HIST // 2)][:, s % (HIST // 2), :] for s in range(HIST)]

        SORT_PARTS = 8
        SORT_CHUNKS = P // SORT_PARTS
        sort_row = spare[:, 0:SORT_PARTS * T].bitcast(I32)
        sort_low = spare[:, SORT_PARTS * T:2 * SORT_PARTS * T]
        sort_less = rel[:, :, :].rearrange("p t f -> p (t f)")
        cur_col = sb("cur_col", [P, 1], I32)
        unsorted = sb("unsorted", [1, 1], I32)

        small = sb("small", [P, 8])
        ones16 = sb("ones16", [P, 1], BF16)
        total = sb("total", [P, 1])
        halves = sb("halves", [P, 1])
        carry_row = sb("carry_row", [P, 1], I32)
        carry_node = sb("carry_node", [P, 1], I32)
        whole = sb("whole", [P, 2])
        whole32 = sb("whole32", [P, 2, HID])
        whole_rows = sb("whole_rows", [HID, 2, P])
        tail = sb("tail", [P, HID])
        tail_row = sb("tail_row", [HID, P])
        carry_out = sb("carry_out", [HID, P + 1])
        carry = [sb(f"carry{d}", [P, HID]) for d in range(2)]
        heads = sb("heads", [P, REL])
        up8 = sb("up8", [P, REL])
        down8 = sb("down8", [P, REL])
        carry64 = sb("carry64", [P, ROW])
        hot = sb("hot", [P, HIST, P], BF16)

        idx = pair("idx", [P, K], I32)
        sidx = pair("sidx", [P, K], I32)
        got0 = pair("got0", [P, K, STEPCOLS])
        got1 = pair("got1", [P, K, FEAT])
        got2 = pair("got2", [P, K, HID])
        att = pair("att", [P, K, FEAT])
        padded = sb("padded", [P, PAD, HID])
        turned = pair("turned", [P, GROUPS * P])
        xc = sb("xc", [P, K, FEAT])
        sq = sb("sq", [P, K, FEAT])
        cen = sb("cen", [P, K, FEAT])
        stat = sb("stat", [P, 4, K])
        hsum = sb("hsum", [P, K, HID])
        prod_both = sb("prod_both", [P, 2048])
        prod = [prod_both[:, 1024 * j:1024 * (j + 1)] for j in range(2)]
        outer = prod_both[:, 0:K * P].rearrange("p (k r f) -> p k r f", k=K, r=REL)
        keep = pair("keep", [P, HID, K + 1])
        part_sum = pair("part_sum", [P, HID, K + 1])
        scanned = pair("scanned", [P, HID, K + 1])
        rows = pair("rows", [P, K * HID])
        old0 = pair("old0", [P, K, FEAT])
        old1 = pair("old1", [P, K, HID])
        node_rows = pair("node_rows", [P, K, ROW])

        flat_x = x_src[:, :, :].rearrange("p t f -> p (t f)")
        flat_rel = rel[:, :, :].rearrange("p t f -> p (t f)")
        room = [[arena[:, :], 0, NCOL * STEPCOLS], [flat_x, 0, T * FEAT], [flat_rel, 0, T * REL]]
        room += [[prod[j][:, :], 0, 1024] for j in range(2)]
        room += [[node_rows[j][:, :, :].rearrange("p k f -> p (k f)"), 0, K * ROW] for j in range(2)]

        def dense(n, cols, f=None):
            for region in room:
                if region[1] + cols <= region[2]:
                    got = region[0][0:n, region[1]:region[1] + cols]
                    region[1] += cols
                    return got if f is None else got.rearrange("p (c f) -> p c f", f=f)
            raise AssertionError("no room")

        nr = [dense(NPART, DC * ROW, ROW) for _ in range(4)]
        hn = dense(NPART, DC * HID, HID)
        ht = dense(P, T4 * NPART)
        x1t = dense(P, T8 * NPART)
        xn = [dense(NPART, DC * FEAT, FEAT) for _ in range(2)]
        vv, cc1, x1n, zz, cc2, res, qq = ([dense(NPART, DC * FEAT, FEAT) for _ in range(2)] for _ in range(7))
        ww = dense(NPART, DC * FEAT, FEAT)
        dst_ = {n: sb("d_" + n, [P, DC])[0:NPART, :] for n in ("1sum", "1ss", "1dev", "1inv", "2sum", "2ss", "2dev")}
        inv2 = [sb(f"d_inv2{j}", [P, DC])[0:NPART, :] for j in range(2)]
        ps_h = [ps_m[:, 512 * g:512 * (g + 1)] for g in range(3)]
        ps_ht = [ps_root[:, :], ps_m[:, 1536:2048]]
        ps_y = ps_hist[0:NPART, 0:DC * FEAT]
        idn = ident[0:NPART, 0:NPART]

        pool_made = sem("pool_made")
        zeroed = sem("zeroed")
        consts_made = sem("consts_made")
        weights_in = sem("weights_in")
        bias_in = sem("bias_in")
        fill_made = sem("fill_made")
        filled = sem("filled")
        edges_copied = sem("edges_copied")
        dst_copied = sem("dst_copied")
        dst0_in = sem("dst0_in")
        edges_in = sem("edges_in")
        digits = sem("digits")
        disorder_sum = sem("disorder_sum")
        flag_ready = sem("flag_ready")
        sort_in = sem("sort_in")
        sort_row_in = sem("sort_row_in")
        sort_read = sem("sort_read")
        sort_step = sem("sort_step")
        sort_cmp = sem("sort_cmp")
        sort_ranked = sem("sort_ranked")
        sort_col = sem("sort_col")
        sort_out = sem("sort_out")
        steps_ready = sem("steps_ready")
        signs_ready = sem("signs_ready")
        hot_used = sem("hot_used")
        total_ready = sem("total_ready")
        base_ready = sem("base_ready")
        last_step = sem("last_step")
        x_in = [sem(f"x_in{j}") for j in range(2)]
        x_placed = [sem(f"x_placed{j}") for j in range(2)]
        xl_stored = sem("xl_stored")
        prep = sem("prep")
        prep_done = sem("prep_done")
        begun = sem("begun")
        lists_free = sem("lists_free")
        turn_ready = sem("turn_ready")
        turn_done = sem("turn_done")
        row_ready = sem("row_ready")
        row_turned = sem("row_turned")
        row_copied = sem("row_copied")
        scan_ready = sem("scan_ready")
        back_done = sem("back_done")
        carry_ready = sem("carry_ready")
        carry_added = sem("carry_added")
        nodes_idx_in = [sem(f"nodes_idx_in{j}") for j in range(2)]

        def layer_sems(n, single, paired):
            s = {m: sem(f"l{n}_{m}") for m in single.split()}
            s.update({m: [sem(f"l{n}_{m}{j}") for j in range(2)] for m in paired.split()})
            return s

        L0, L1, L2 = (layer_sems(n, "turned turned_sb msg reduced" + more, "idx_in got mask scan rows stored" + pairs)
                      for n, more, pairs in ((0, "", " padded mult att_in saved scaled"),
                                             (1, " stat squared std inv x1 outer root_saved", " sum"),
                                             (2, "", " padded mult att_in saved sum")))
        D = layer_sems("d", "v stat1 center1 q1 ss1 std1 x1 x1t x1t_sb h_mm h ht ht_sb y z w sum2 center2 q2 ss2 std2"
                       " inv2 result", "out")
        D["in"] = [sem(f"ld_in{s}") for s in range(4)]

        CARRIES = (0, 1, 0, 1, 0, 0, 0)
        CONSTS, HALF_STEPS = 19, 5
        LAST_STEPS = 3 + 2 * HALF_STEPS

        def chunk(k):
            return bass.ds(k * K, K)

        def back(ap):
            dims = [list(d) for d in ap.ap]
            n, step = dims[-1][1], dims[-1][0]
            dims[-1] = [-step, n]
            return bass.AP(ap.tensor, ap.offset + (n - 1) * step, dims)

        def above(eng, s, value):
            if not isinstance(value, int) or value > 0:
                eng.wait_ge(s, value)

        def over_chunks(eng, stage, lag, first=4):
            for k in range(first):
                stage(k, k % 4, k // 4)
            with eng.Fori(first // 4, DCHUNKS // 4) as i:
                for s in range(4):
                    stage(i * 4 + s, s, i)
            for k in range(DCHUNKS, DCHUNKS + lag):
                stage(k, k % 4, k // 4)

        def over_rows(ap, n, f):
            return ap.unsqueeze(1).to_broadcast([ap.shape[0], n, f])

        def over_last(ap, f):
            return ap.unsqueeze(len(ap.shape)).to_broadcast([*ap.shape, f])

        block = ctx.enter_context(nc.Block())

        GOT = 16 * K
        FILLED = 16 * (2 + 2 * (NCOL // FILL))

        @block.sync
        def _(sp):
            sp.dma_start(d_dst[1:1 + E].rearrange("(a b) -> a b", a=80),
                         dst.rearrange("(a b) -> a b", a=80)).then_inc(dst_copied, 16)
            sp.wait_ge(pool_made, 4)
            sp.dma_start(d_dst[1 + E:EP + 2].rearrange("(a b) -> a b", a=1),
                         pad_dst[:, 0:EP - E + 1]).then_inc(dst_copied, 16)
            sp.dma_start(d_dst[0:1].rearrange("(a b) -> a b", a=1),
                         pad_dst[:, EP - E + 1:]).then_inc(dst_copied, 16)
            sp.wait_ge(dst_copied, 48)
            sp.dma_start(dst0_i[:, :], d_cur).then_inc(dst0_in, 16)
            sp.dma_start(prev_i[:, :], d_prev).then_inc(dst0_in, 16)
            sp.dma_start(d_src[0:E].rearrange("(a b) -> a b", a=80),
                         src.rearrange("(a b) -> a b", a=80)).then_inc(edges_copied, 16)
            sp.dma_start(d_typ[0:E].rearrange("(a b) -> a b", a=80),
                         edge_type.rearrange("(a b) -> a b", a=80)).then_inc(edges_copied, 16)
            sp.dma_start(d_src[E:EP].rearrange("(a b) -> a b", a=1), pad_i[:, :]).then_inc(edges_copied, 16)
            sp.dma_start(d_typ[E:EP].rearrange("(a b) -> a b", a=1), pad_i[:, :]).then_inc(edges_copied, 16)
            sp.dma_start(d_ea[0:E, :].rearrange("(a b) f -> a (b f)", a=80),
                         edge_attr.rearrange("(a b) f -> a (b f)", a=80)).then_inc(edges_copied, 16)
            sp.dma_start(d_ea[E:EP, :].rearrange("(a b) f -> a (b f)", a=FEAT),
                         pad_att[:, :]).then_inc(edges_copied, 16)
            sp.wait_ge(edges_copied, 96)

            with sp.Fori(0, DCHUNKS // 2) as i:
                for j in range(2):
                    sp.wait_ge(x_placed[j], i)
                    for ps in NODE_PARTS:
                        sp.dma_start(node_rows[j][ps, :, :].rearrange("p k f -> p (k f)")[:, 0:DC * FEAT],
                                     x_t[ps, bass.ds((i * 2 + j) * DC, DC), :]
                                     .rearrange("p c f -> p (c f)")).then_inc(x_in[j], 16)

            sp.wait_ge(fill_made, 1)
            sp.dma_start(d_a0[EP:EP + P, :], bias_row[:, 0:FEAT]).then_inc(filled, 16)
            sp.dma_start(d_a1[EP:EP + P, :], bias_row[:, FEAT:FEAT + HID]).then_inc(filled, 16)
            with sp.Fori(0, NCOL // FILL) as i:
                for ps in NODE_PARTS:
                    sp.dma_start(d_nodes_t[ps, bass.ds(i * FILL, FILL), :], fill[ps, :, :]).then_inc(filled, 16)

            sp.wait_ge(flag_ready, 1)
            with sp.If(sp.value_load(unsorted[0:1, 0:1], min_val=0, max_val=EP)):
                sp.dma_start(next_i[:, :], d_src_t).then_inc(sort_in, 16)
                sp.dma_start(prev_i[:, :], d_typ_t).then_inc(sort_in, 16)
                sp.wait_ge(last_step, LAST_STEPS)
                with sp.Fori(0, SORT_CHUNKS) as c:
                    sp.wait_ge(sort_read, c)
                    sp.dma_start(sort_row[:, :], d_dst[bass.ds(1 + c * (T * SORT_PARTS), T * SORT_PARTS)]
                                 .rearrange("(a f) -> a f", a=1).to_broadcast([P, T * SORT_PARTS])) \
                      .then_inc(sort_row_in, 16)
                sp.wait_ge(sort_ranked, 1)
                sp.dma_start(x_src[:, :, :], d_ea_t).then_inc(sort_in, 16)
                sp.wait_ge(sort_in, 48)
                with sp.Fori(0, T) as t:
                    col = bass.ds(t, 1)
                    sp.wait_ge(sort_out, 64 * t)
                    for to, of in ((idx[0], cur_i), (idx[1], node_row), (sidx[0], next_i), (sidx[1], prev_i)):
                        sp.dma_start(to[:, 0:1], of[:, col]).then_inc(sort_col, 16)
                    sp.dma_start(cur_col[:, :], dst0_i[:, col]).then_inc(sort_col, 16)
                    sp.dma_start(got1[0][:, 0:1, :], x_src[:, col, :]).then_inc(sort_col, 16)
                sp.wait_ge(sort_out, 64 * T)
            for to, of in ((cur_i, d_cur), (prev_i, d_prev), (next_i, d_next), (typ_i, d_typ_t)):
                sp.dma_start(to[:, :], of).then_inc(edges_in, 16)

            for h in range(2):
                sp.wait_ge(last_step, 3 + HALF_STEPS * (h + 1))
                for ps in NODE_PARTS:
                    half = slice(h * NCOL // 2, (h + 1) * NCOL // 2)
                    sp.dma_start(d_xl_t[ps, half, :], xl[ps, half, :]).then_inc(xl_stored, 16)

            def loads0(j, i):
                k = i * 2 + j
                sp.wait_ge(L0["got"][j], GOT * i)
                sp.dma_start(idx[j][:, :], d_src_t[:, chunk(k)]).then_inc(L0["idx_in"][j], 16)
                sp.wait_ge(L0["padded"][j], i)
                sp.dma_start(att[j][:, :, :], d_ea_t[:, chunk(k), :]).then_inc(L0["att_in"][j], 16)

            def store0(j, i):
                k = i * 2 + j
                sp.wait_ge(L0["rows"][j], i + 1)
                sp.dma_start(d_a0_t[:, chunk(k), :],
                             rows[j][:, 0:K * FEAT].rearrange("p (k f) -> p k f", k=K)).then_inc(L0["stored"][j], 16)

            loads0(0, 0)
            loads0(1, 0)
            with sp.Fori(0, HALF - 1) as i:
                for j in range(2):
                    loads0(j, i + 1)
                    store0(j, i)
            store0(0, HALF - 1)
            store0(1, HALF - 1)

            def loads1(j, i):
                k = i * 2 + j
                sp.wait_ge(L1["got"][j], GOT * i)
                sp.dma_start(idx[j][:, :], last_of_src[:, chunk(k)]).then_inc(L1["idx_in"][j], 16)

            def store1(j, i):
                k = i * 2 + j
                sp.wait_ge(L1["rows"][j], i + 1)
                sp.dma_start(d_a1_t[:, chunk(k), :],
                             rows[j][:, :].rearrange("p (k f) -> p k f", k=K)).then_inc(L1["stored"][j], 16)

            sp.wait_ge(L0["got"][0], GOT * HALF)
            sp.wait_ge(L0["got"][1], GOT * HALF)
            sp.wait_ge(L0["saved"][0], 2 * HALF)
            sp.wait_ge(L0["saved"][1], 2 * HALF)
            loads1(0, 0)
            loads1(1, 0)
            with sp.Fori(0, HALF - 1) as i:
                for j in range(2):
                    loads1(j, i + 1)
                    store1(j, i)
            store1(0, HALF - 1)
            store1(1, HALF - 1)

            def loads2(j, i, first=False):
                k = i * 2 + j
                sp.wait_ge(L2["got"][j], GOT * i)
                sp.dma_start(idx[j][:, :], last_of_src[:, chunk(k)]).then_inc(L2["idx_in"][j], 16)
                if first:
                    sp.wait_ge(carry_added, 32)
                sp.wait_ge(L2["saved"][j], 2 * i)
                sp.dma_start(old0[j][:, :, :], d_a0_t[:, chunk(k), :]).then_inc(L2["att_in"][j], 16)
                sp.dma_start(old1[j][:, :, :], d_a1_t[:, chunk(k), :]).then_inc(L2["att_in"][j], 16)
                sp.wait_ge(L2["stored"][j], GOT * i)
                sp.sem_inc(lists_free, 1)
                sp.dma_start(sidx[j][:, :], node_row[:, chunk(k)]).then_inc(nodes_idx_in[j], 16)

            sp.wait_ge(L1["got"][0], GOT * HALF)
            sp.wait_ge(L1["got"][1], GOT * HALF)
            loads2(0, 0, first=True)
            with sp.Fori(0, HALF - 1) as i:
                loads2(1, i)
                loads2(0, i + 1)
            loads2(1, HALF - 1)

            sp.wait_ge(carry_added, 48)
            sp.wait_ge(L2["sum"][0], HALF)
            sp.wait_ge(L2["sum"][1], HALF)

            def load_nodes(k, s, u):
                above(sp, D["h"], 3 * (k - 3))
                sp.sem_inc(lists_free, 1)
                above(sp, D["z"], k - 3)
                sp.sem_inc(lists_free, 1)
                above(sp, D["v"], k - 1)
                sp.sem_inc(lists_free, 1)
                for ps in NODE_PARTS:
                    sp.dma_start(nr[s][ps, :, :], d_nodes_t[ps, bass.ds(k * DC, DC), :]).then_inc(D["in"][s], 16)
                    sp.dma_start(xn[s % 2][ps, :, :], x_t[ps, bass.ds(k * DC, DC), :]).then_inc(D["in"][s], 16)

            def store_nodes(k, s):
                above(sp, D["result"], k + 1)
                sp.sem_inc(lists_free, 1)
                for ps in NODE_PARTS:
                    sp.dma_start(out_t[ps, bass.ds(k * DC, DC), :], res[s % 2][ps, :, :]) \
                      .then_inc(D["out"][s % 2], 16)

            def nodes(k, s, u):
                if not isinstance(k, int) or k < DCHUNKS:
                    load_nodes(k, s, u)
                if not isinstance(k, int) or k >= 6:
                    store_nodes(k - 6, (s + 2) % 4)

            over_chunks(sp, nodes, 6, first=8)
            sp.wait_ge(D["out"][0], 32 * (DCHUNKS // 2))
            sp.wait_ge(D["out"][1], 32 * (DCHUNKS // 2))

        @block.gpsimd
        def _(pool):
            pool.memset(pad_dst[:, 0:EP - E], N).then_inc(pool_made, 1)
            pool.memset(pad_dst[:, EP - E:], -1).then_inc(pool_made, 1)
            pool.memset(pad_i[:, :], 0).then_inc(pool_made, 1)
            pool.memset(pad_att[:, :], 0.0).then_inc(pool_made, 1)
            pool.iota(iota_i, [[1, NCOL]], base=0, channel_multiplier=0).then_inc(pool_made, 1)
            for n, (base, times) in enumerate(((0, 1), (0, T), (EP, 1), (DUMP + EP, 1))):
                pool.iota(part_i[:, n:n + 1], [[0, 1]], base=base, channel_multiplier=times).then_inc(pool_made, 1)
            pool.iota(edge_i[:, :], [[1, T]], base=DUMP, channel_multiplier=T).then_inc(pool_made, 1)

            pool.wait_ge(bias_in, 48)
            pool.tensor_copy(fill[:, :, :], over_rows(bias_row[:, :], FILL, ROW)).then_inc(fill_made, 1)

            with pool.Fori(0, DCHUNKS // 2) as i:
                for j in range(2):
                    pool.wait_ge(x_in[j], 32 * (i + 1))
                    pool.tensor_copy(xl[:, bass.ds((i * 2 + j) * DC, DC), 0:FEAT],
                                     node_rows[j][0:NPART, :, :].rearrange("p k f -> p (k f)")[:, 0:DC * FEAT]
                                     .rearrange("p (c f) -> p c f", f=FEAT)).then_inc(x_placed[j], 1)

            def gather(layer, table, to, j, i, freed, complete):
                pool.wait_ge(layer["idx_in"][j], 16 * (i + 1))
                for free, n in freed:
                    pool.wait_ge(layer[free][j], n * i)
                pool.wait_ge(*complete)
                pool.sem_inc(begun, 1)
                for t in range(K):
                    pool.indirect_dma_start(
                        out=to[j][:, t, :], out_offset=None, in_=table,
                        in_offset=bass.IndirectOffsetOnAxis(ap=idx[j][:, t:t + 1], axis=0),
                    ).then_inc(layer["got"][j], 16)

            def scatter(j, i):
                pool.wait_ge(nodes_idx_in[j], 16 * (i + 1))
                pool.wait_ge(L2["saved"][j], 2 * (i + 1))
                pool.wait_ge(L2["rows"][j], i + 1)
                pool.wait_ge(filled, FILLED)
                pool.sem_inc(begun, 1)
                for t in range(K):
                    pool.indirect_dma_start(
                        out=d_nodes[:, :], out_offset=bass.IndirectOffsetOnAxis(ap=sidx[j][:, t:t + 1], axis=0),
                        in_=node_rows[j][:, t, :], in_offset=None,
                    ).then_inc(L2["stored"][j], 16)

            def add_carry(n, table, rows_of, what):
                pool.wait_ge(carry_ready, n + 1)
                pool.indirect_dma_start(
                    out=table, out_offset=bass.IndirectOffsetOnAxis(ap=rows_of[:, 0:1], axis=0),
                    in_=what, in_offset=None, compute_op=ALU.add,
                ).then_inc(carry_added, 16)

            pool.wait_ge(flag_ready, 1)
            with pool.If(pool.value_load(unsorted[0:1, 0:1], min_val=0, max_val=EP)):
                with pool.Fori(0, T) as t:
                    pool.wait_ge(sort_col, 96 * (t + 1))
                    pool.sem_inc(begun, 1)
                    for table, rows_of, what in ((d_src, idx[0], sidx[0]), (d_dst, idx[1], cur_col),
                                                 (d_typ, idx[0], sidx[1])):
                        pool.indirect_dma_start(
                            out=table.rearrange("(e a) -> e a", a=1),
                            out_offset=bass.IndirectOffsetOnAxis(ap=rows_of[:, 0:1], axis=0),
                            in_=what[:, 0:1], in_offset=None).then_inc(sort_out, 16)
                    pool.indirect_dma_start(
                        out=d_ea[:, :], out_offset=bass.IndirectOffsetOnAxis(ap=idx[0][:, 0:1], axis=0),
                        in_=got1[0][:, 0, :], in_offset=None).then_inc(sort_out, 16)

            pool.wait_ge(xl_stored, 64)
            with pool.Fori(0, HALF) as i:
                for j in range(2):
                    gather(L0, d_xl[:, :], got0, j, i, (("saved", 2), ("scaled", 1)), (xl_stored, 64))
            pool.wait_ge(L0["stored"][0], 16 * HALF)
            pool.wait_ge(L0["stored"][1], 16 * HALF)
            add_carry(0, d_a0[:, :], carry_row, carry[0][:, 0:FEAT])
            pool.wait_ge(carry_added, 16)
            pool.wait_ge(filled, FILLED)

            with pool.Fori(0, HALF) as i:
                for j in range(2):
                    gather(L1, d_a0[:, :], got1, j, i, (("sum", 1),), (carry_added, 16))
            pool.wait_ge(L1["stored"][0], 16 * HALF)
            pool.wait_ge(L1["stored"][1], 16 * HALF)
            add_carry(1, d_a1[:, :], carry_row, carry[0][:, 0:HID])
            pool.wait_ge(carry_added, 32)

            gather(L2, d_a1[:, :], got2, 0, 0, (("sum", 1),), (carry_added, 32))
            with pool.Fori(0, HALF - 1) as i:
                gather(L2, d_a1[:, :], got2, 1, i, (("sum", 1),), (carry_added, 32))
                scatter(0, i)
                gather(L2, d_a1[:, :], got2, 0, i + 1, (("sum", 1),), (carry_added, 32))
                scatter(1, i)
            gather(L2, d_a1[:, :], got2, 1, HALF - 1, (("sum", 1),), (carry_added, 32))
            scatter(0, HALF - 1)
            scatter(1, HALF - 1)
            pool.wait_ge(L2["stored"][0], GOT * HALF)
            pool.wait_ge(L2["stored"][1], GOT * HALF)
            add_carry(2, d_nodes[:, :], carry_node, carry64[:, :])

            def nodes(k, s, u):
                static = isinstance(k, int)
                if not static or k < DCHUNKS:
                    above(pool, D["center1"], k - 1)
                    above(pool, D["in"][s], 64 * (u + 1))
                    pool.tensor_tensor(vv[s % 2], xn[s % 2], nr[s][:, :, 0:FEAT], ALU.add).then_inc(D["v"], 1)
                if not static or 2 <= k <= DCHUNKS + 1:
                    above(pool, D["w"], k - 3)
                    above(pool, D["x1"], k - 1)
                    pool.tensor_tensor(zz[s % 2], x1n[s % 2], nr[(s + 2) % 4][:, :, FEAT + HID:],
                                       ALU.add).then_inc(D["z"], 1)
                if not static or 4 <= k < DCHUNKS + 4:
                    above(pool, D["out"][s % 2], 32 * (2 * u - 2 + s // 2))
                    above(pool, D["inv2"], k - 3)
                    pool.tensor_tensor(res[s % 2], cc2[s % 2], over_last(inv2[s % 2], FEAT), ALU.mult) \
                        .then_inc(D["result"], 1)

            over_chunks(pool, nodes, 4)

        @block.tensor
        def _(pe):
            pe.wait_ge(consts_made, CONSTS)

            pe.wait_ge(digits, 2)
            pe.matmul(ps_root[:, 0:1], ones_t[:, 0:P], small[:, 0:1], start=True, stop=True).then_inc(disorder_sum, 1)
            pe.wait_ge(flag_ready, 1)

            def count_group(g, first, last):
                by_dve, by_act = HIST + HIST // HIST_HOT - len(HIST_ACT), len(HIST_ACT)
                done = [0, 0]
                for s in range(HIST):
                    done[0] += (s % HIST_HOT == 0) + (s not in HIST_ACT)
                    pe.wait_ge(steps_ready, g * by_dve + done[0])
                    if s in HIST_ACT:
                        done[1] += 1
                        pe.wait_ge(signs_ready, g * by_act + done[1])
                        pe.matmul(ps_root[0:NPART, 8:9], hot[:, s, 0:NPART], ones16[:, :],
                                  start=first and s == HIST_ACT[0], stop=last and s == HIST_ACT[-1])
                    for h in range(2):
                        mm = pe.matmul(ps_hist[0:NPART, 512 * h:512 * h + NCOL // 2], hot[:, s, 0:NPART],
                                       steps[s][:, h * NCOL // 2:(h + 1) * NCOL // 2],
                                       start=first and s == 0, stop=last and s == HIST - 1)
                    mm.then_inc(hot_used, 1)

            count_group(0, True, False)
            with pe.Fori(1, T // HIST - 1) as g:
                count_group(g, False, False)
            count_group(T // HIST - 1, False, True)
            pe.wait_ge(total_ready, 1)
            pe.matmul(ps_root[0:NPART, 0:1], before[0:NPART, 0:NPART], total[0:NPART, :],
                      start=True, stop=True).then_inc(base_ready, 1)
            pe.wait_ge(turn_ready, 1)
            for d in range(2):
                mm = pe.transpose(ps_turn[0:HID, d * P:(d + 1) * P], whole32[:, d, :], ident[:, :])
            mm.then_inc(turn_done, 1)

            def carry_turns(n):
                pe.wait_ge(row_ready, n + 1)
                pe.transpose(ps_root[0:HID, 0:P], tail[:, :], ident[:, :]).then_inc(row_turned, 1)
                pe.wait_ge(scan_ready, n + 1)
                at = 1 if CARRIES[n] else 0
                pe.transpose(ps_root[:, 256:256 + HID], carry_out[:, at:at + P], ident[0:HID, 0:HID]) \
                    .then_inc(back_done, 1)

            for n in range(4):
                carry_turns(n)

            def turn_chunk(layer, j, i):
                k = i * 2 + j
                pe.wait_ge(layer["padded"][j], i + 1)
                pe.wait_ge(layer["turned_sb"], k)
                for g in range(GROUPS):
                    mm = pe.transpose(ps_turn[:, g * P:(g + 1) * P],
                                      padded[:, 4 * g:4 * g + 4, :].rearrange("p t f -> p (t f)"), ident[:, :])
                mm.then_inc(layer["turned"], 1)

            def products(layer, k, g, turns, w):
                pe.wait_ge(layer["mult"][g % 2], 2 * k + g // 2)
                n, cols = group_tiles(g), w.shape[2]
                at_once = min(n, 512 // cols)
                for t in range(0, n, at_once):
                    mm = pe.matmul(ps_msg[g % 2][:, cols * t:cols * (t + at_once)], turns[:, g * P:(g + 1) * P],
                                   w[:, t:t + at_once, :], start=True, stop=True)
                return mm

            pe.wait_ge(weights_in, 16 * 33)

            def layer0(j, i):
                k = i * 2 + j
                turn_chunk(L0, j, i)
                pe.wait_ge(L0["turned_sb"], k + 1)
                for g in range(GROUPS):
                    products(L0, k, g, turned[0], w0).then_inc(L0["msg"], 1)

            with pe.Fori(0, HALF) as i:
                layer0(0, i)
                layer0(1, i)
            carry_turns(4)

            def layer1(j, i):
                k = i * 2 + j

                def turn(g):
                    pe.wait_ge(L1["outer"], 4 * k + g + 1)
                    above(pe, L1["turned_sb"], 4 * k + g - 1)
                    for t in range(group_tiles(g)):
                        mm = pe.transpose(ps_turns[g % 2][:, P * t:P * t + P],
                                          outer[:, 4 * g + t, :, :].rearrange("p r f -> p (r f)"), ident[:, :])
                    mm.then_inc(L1["turned"], 1)

                def multiply(g):
                    if g == 0:
                        above(pe, L1["root_saved"], k - 1)
                    pe.wait_ge(L1["turned_sb"], 4 * k + g + 1)
                    for t in range(group_tiles(g)):
                        tile = 4 * g + t
                        mm = pe.matmul(ps_msg[j][:, 2 * HID * tile:2 * HID * (tile + 1)],
                                       turned[g % 2][:, P * t:P * t + P], w1[:, :], start=True, stop=True)
                    mm.then_inc(L1["msg"], 1)

                turn(0)
                for g in range(1, GROUPS):
                    turn(g)
                    multiply(g - 1)
                multiply(GROUPS - 1)

            layer1(0, 0)
            layer1(1, 0)
            with pe.Fori(1, HALF) as i:
                layer1(0, i)
                layer1(1, i)
            pe.wait_ge(L1["root_saved"], CHUNKS)
            carry_turns(5)

            def layer2(j, i):
                k = i * 2 + j
                turn_chunk(L2, j, i)
                pe.wait_ge(L2["turned_sb"], k + 1)
                for g in range(GROUPS):
                    products(L2, k, g, turned[0], w2).then_inc(L2["msg"], 1)

            with pe.Fori(0, HALF) as i:
                layer2(0, i)
                layer2(1, i)
            carry_turns(6)

            def nodes(k, s, u):
                static = isinstance(k, int)
                second = not static or 1 <= k <= DCHUNKS

                def turn_x1(g):
                    above(pe, D["x1"], k + 1)
                    above(pe, D["x1t_sb"], 2 * k + g)
                    for m in range(4 * g, min(4 * g + 4, T8)):
                        mm = pe.transpose(ps_turn[:, (m % 4) * NPART:(m % 4 + 1) * NPART],
                                          x1n[s % 2][:, 8 * m:8 * m + 8, :].rearrange("p c f -> p (c f)"), idn)
                    mm.then_inc(D["x1t"], 1)

                def turn_h(g):
                    above(pe, D["ht_sb"], 3 * (k - 1) + g - 1)
                    above(pe, D["h"], 3 * (k - 1) + g + 1)
                    for m in range(4 * g, min(4 * g + 4, T4)):
                        mm = pe.transpose(ps_ht[(s + 1 + g) % 2][:, (m % 4) * NPART:(m % 4 + 1) * NPART],
                                          hn[:, 4 * m:4 * m + 4, :].rearrange("p c f -> p (c f)"), idn)
                    mm.then_inc(D["ht"], 1)

                if second:
                    above(pe, D["x1t_sb"], 2 * k)
                    above(pe, D["h"], 3 * (k - 1))
                    for g in range(3):
                        for m in range(2 * g, min(2 * g + 2, T8)):
                            mm = pe.matmul(ps_h[g][0:NPART, 256 * (m % 2):256 * (m % 2) + 256],
                                           x1t[:, m * NPART:(m + 1) * NPART],
                                           wr1[:, :, :].rearrange("p c f -> p (c f)"), start=True, stop=True)
                        mm.then_inc(D["h_mm"], 1)
                if not static or k < DCHUNKS:
                    turn_x1(0)
                    turn_x1(1)
                if not static or 2 <= k <= DCHUNKS + 1:
                    above(pe, D["w"], k - 2)
                    above(pe, D["ht_sb"], 3 * (k - 1))
                    for m in range(T4):
                        mm = pe.matmul(ps_y[:, 64 * m:64 * m + 64], ht[:, m * NPART:(m + 1) * NPART],
                                       wr2[:, :, :].rearrange("p c f -> p (c f)"), start=True, stop=True)
                    mm.then_inc(D["y"], 1)
                if second:
                    for g in range(3):
                        turn_h(g)

            over_chunks(pe, nodes, 2)

        @block.scalar
        def _(act):
            act.wait_ge(zeroed, 4)
            for j in range(4):
                block_rows = slice(32 * j, 32 * j + FEAT)
                act.dma_start(w0[block_rows, j, :], W_e).then_inc(weights_in, 16)
                act.dma_start(w0[32 * j + FEAT:32 * j + FEAT + 1, j, :],
                              b_e.rearrange("(a f) -> a f", a=1)).then_inc(weights_in, 16)
                act.dma_start(w2[32 * j:32 * j + HID, j, :].rearrange("p (r o) -> p r o", r=REL),
                              W2.rearrange("r i o -> i r o")).then_inc(weights_in, 16)
                act.dma_start(wr2[32 * j:32 * j + HID, j, :], root2).then_inc(weights_in, 16)
            for m in range(8):
                act.dma_start(wr1[FEAT * m:FEAT * m + FEAT, m, :], root1).then_inc(weights_in, 16)
                act.dma_start(w1[FEAT * m:FEAT * m + FEAT, HID:], root1).then_inc(weights_in, 16)
            act.dma_start(w1[:, 0:HID], W1.rearrange("r i o -> (r i) o")).then_inc(weights_in, 16)
            for c, n, b in ((0, FEAT, bias0), (FEAT, HID, b1), (FEAT + HID, FEAT, b2)):
                act.dma_start(bias_row[:, c:c + n],
                              b.rearrange("(a f) -> a f", a=1).to_broadcast([P, n])).then_inc(bias_in, 16)

            def sign_tile(s, t, used):
                if used is not None:
                    act.wait_ge(hot_used, used)
                act.wait_ge(digits, 12)
                act.activation(steps[s], iota_lo[:, :], ACT.Sign, bias=half_lo[:, bass.ds(t, 1)]) \
                    .then_inc(signs_ready, 1)

            act.wait_ge(consts_made, CONSTS)
            for s in HIST_ACT:
                sign_tile(s, s, None)
            with act.Fori(1, T // HIST) as g:
                for s in HIST_ACT:
                    sign_tile(s, g * HIST + s, g * HIST + s - (HIST - 1))

            def runs_go_on(layer, j, i, f):
                act.wait_ge(layer["scan"][j], i)
                act.wait_ge(prep_done, 1)
                act.activation(keep[j][:, 0:f, 1:], over_rows(same[:, chunk(i * 2 + j)], f, K),
                               ACT.Copy).then_inc(layer["mask"][j], 1)

            def copy_turns(layer, k, to, used):
                act.wait_ge(layer["turned"], k + 1)
                act.wait_ge(layer["msg"], used)
                act.activation(to[:, :], ps_turn[:, :], ACT.Copy).then_inc(layer["turned_sb"], 1)

            def layer0(j, i):
                k = i * 2 + j
                act.wait_ge(L0["att_in"][j], 16 * (i + 1))
                act.wait_ge(L0["turned"], k)
                act.activation(padded[:, 0:K, 0:FEAT], att[j][:, :, :], ACT.Copy).then_inc(L0["padded"][j], 1)
                copy_turns(L0, k, turned[0], 4 * k)
                runs_go_on(L0, j, i, FEAT)
                act.wait_ge(L0["got"][j], GOT * (i + 1))
                act.wait_ge(prep_done, 1)
                act.activation(x_src[:, chunk(k), :], got0[j][:, :, 0:FEAT], ACT.Copy).then_inc(L0["saved"][j], 1)
                act.activation(last_of_src[:, chunk(k)], got0[j][:, :, FEAT], ACT.Copy).then_inc(L0["saved"][j], 1)

            with act.Fori(0, HALF) as i:
                layer0(0, i)
                layer0(1, i)

            act.wait_ge(L0["scan"][0], HALF)
            act.wait_ge(L0["scan"][1], HALF)
            def x1_ahead(j, i):
                k = i * 2 + j
                act.wait_ge(L1["stat"], 3 * k + 2)
                act.activation(sq[:, :, :], cen[:, :, :], ACT.Square).then_inc(L1["squared"], 1)

            def x1_deviation(j, i):
                k = i * 2 + j
                act.wait_ge(L1["stat"], 3 * k + 3)
                act.activation(stat[:, 2, :], stat[:, 1, :], ACT.Sqrt, bias=eps[:, :], scale=1.0 / FEAT) \
                    .then_inc(L1["std"], 1)
                for g in range(GROUPS):
                    above(act, L1["msg"], 4 * k + g - 1)
                    act.wait_ge(L1["turned"], 4 * k + g + 1)
                    n = group_tiles(g) * P
                    act.activation(turned[g % 2][:, 0:n], ps_turns[g % 2][:, 0:n], ACT.Copy) \
                        .then_inc(L1["turned_sb"], 1)

            def layer1(j, i, ahead):
                k = i * 2 + j
                runs_go_on(L1, j, i, HID)
                if ahead:
                    x1_ahead(1 - j, i + j)
                act.wait_ge(L1["msg"], 4 * k + 4)
                act.wait_ge(L1["reduced"], 2 * k + 1)
                act.wait_ge(prep_done, 1)
                act.activation(u_src[:, chunk(k), :], ps_msg[j][:, 0:K * 2 * HID]
                               .rearrange("p (k f) -> p k f", k=K)[:, :, HID:], ACT.Copy).then_inc(L1["root_saved"], 1)
                if ahead:
                    x1_deviation(1 - j, i + j)

            x1_ahead(0, 0)
            x1_deviation(0, 0)
            with act.Fori(0, HALF - 1) as i:
                layer1(0, i, True)
                layer1(1, i, True)
            layer1(0, HALF - 1, True)
            layer1(1, HALF - 1, False)

            act.wait_ge(L1["scan"][0], HALF)
            act.wait_ge(L1["scan"][1], HALF)
            def layer2(j, i):
                k = i * 2 + j
                runs_go_on(L2, j, i, FEAT)
                act.wait_ge(L2["turned"], k)
                act.wait_ge(L2["sum"][j], i + 1)
                act.activation(padded[:, 0:K, :], hsum[:, :, :], ACT.Relu).then_inc(L2["padded"][j], 1)
                copy_turns(L2, k, turned[0], 4 * k)
                act.wait_ge(L2["att_in"][j], 32 * (i + 1))
                act.wait_ge(L2["stored"][j], GOT * i)
                act.activation(node_rows[j][:, :, 0:FEAT], old0[j][:, :, :], ACT.Copy).then_inc(L2["saved"][j], 1)
                act.activation(node_rows[j][:, :, FEAT:FEAT + HID], old1[j][:, :, :], ACT.Copy) \
                    .then_inc(L2["saved"][j], 1)

            with act.Fori(0, HALF) as i:
                layer2(0, i)
                layer2(1, i)

            def deviation(n, k):
                act.activation(dst_[n + "dev"], dst_[n + "ss"], ACT.Sqrt, bias=eps[0:NPART, :], scale=1.0 / FEAT) \
                    .then_inc(D["std" + n], 1)

            def nodes(k, s, u):
                static = isinstance(k, int)
                first = not static or k < DCHUNKS
                hidden = not static or 2 <= k <= DCHUNKS + 1
                second = not static or 3 <= k < DCHUNKS + 3

                def turned_h(g):
                    a, b = 4 * g * NPART, min(4 * g + 4, T4) * NPART
                    above(act, D["y"], k - 2)
                    above(act, D["ht"], 3 * (k - 2) + g + 1)
                    act.activation(ht[:, a:b], ps_ht[(s + g) % 2][:, 0:b - a], ACT.Relu).then_inc(D["ht_sb"], 1)

                def turned_x1(g):
                    a, b = 4 * g * NPART, min(4 * g + 4, T8) * NPART
                    above(act, D["h_mm"], 3 * k)
                    above(act, D["x1t"], 2 * k + g + 1)
                    act.activation(x1t[:, a:b], ps_turn[:, 0:b - a], ACT.Copy).then_inc(D["x1t_sb"], 1)

                if first:
                    above(act, D["ss1"], k)
                    above(act, D["center1"], k + 1)
                    act.activation(qq[0], cc1[s % 2], ACT.Square).then_inc(D["q1"], 1)
                if hidden:
                    for g in range(3):
                        turned_h(g)
                if first:
                    above(act, D["ss1"], k + 1)
                    deviation("1", k)
                if not static or 4 <= k < DCHUNKS + 4:
                    above(act, D["inv2"], k - 4)
                    above(act, D["ss2"], k - 3)
                    deviation("2", k)
                if first:
                    turned_x1(0)
                    turned_x1(1)
                if second:
                    above(act, D["ss2"], k - 3)
                    above(act, D["center2"], k - 2)
                    act.activation(qq[1], cc2[(s + 1) % 2], ACT.Square).then_inc(D["q2"], 1)

            over_chunks(act, nodes, 4)

        @block.vector
        def _(dve):
            for w in (w0, w2, wr1, wr2):
                dve.memset(w[:, :, :], 0.0).then_inc(zeroed, 1)
            dve.memset(ones_t[:, :], 1.0).then_inc(consts_made, 1)
            dve.memset(eps[:, :], EPS).then_inc(consts_made, 1)
            dve.memset(ones16[:, :], 1.0).then_inc(consts_made, 1)
            dve.memset(tail[:, :], 0.0).then_inc(consts_made, 1)
            dve.memset(carry_out[:, :], 0.0).then_inc(consts_made, 1)
            dve.memset(carry64[:, :], 0.0).then_inc(consts_made, 1)
            dve.memset(padded[:, :, :], 0.0).then_inc(consts_made, 1)
            for j in range(2):
                dve.memset(keep[j][:, :, 0:1], 0.0).then_inc(consts_made, 1)
                dve.memset(scanned[j][:, :, :], 0.0).then_inc(consts_made, 1)
            dve.wait_ge(consts_made, 11)
            dve.memset(padded[:, :, FEAT:FEAT + 1], 1.0).then_inc(consts_made, 1)
            dve.wait_ge(pool_made, 10)
            dve.tensor_copy(iota_lo[:, :], iota_i).then_inc(consts_made, 1)
            dve.tensor_copy(iota_hi[:, :], iota_i[:, 0:P]).then_inc(consts_made, 1)
            dve.tensor_copy(eight[:, :], iota_i[:, 0:REL]).then_inc(consts_made, 1)
            dve.tensor_copy(part[:, :], part_i[:, :]).then_inc(consts_made, 1)
            dve.tensor_copy(dump_row[:, :], edge_i[:, :]).then_inc(consts_made, 1)
            dve.wait_ge(consts_made, 17)
            dve.tensor_scalar(ident[:, :], iota_hi[:, :], part[:, 0:1], None, ALU.is_equal).then_inc(consts_made, 1)
            dve.tensor_scalar(before[:, :], iota_hi[:, :], part[:, 0:1], None, ALU.is_gt).then_inc(consts_made, 1)

            dve.wait_ge(dst0_in, 32)
            dve.tensor_tensor(fix[:, :], dst0_i[:, :], prev_i[:, :], ALU.is_lt).then_inc(digits, 1)
            dve.wait_ge(digits, 1)
            dve.tensor_reduce(small[:, 0:1], fix[:, :], AX.X, ALU.add).then_inc(digits, 1)
            dve.wait_ge(digits, 2)

            dve.tensor_scalar(hi_i[:, :], dst0_i[:, :], 1.0 / NCOL, None, ALU.mult).then_inc(digits, 1)
            dve.wait_ge(digits, 3)
            dve.tensor_copy(hi[:, :], hi_i[:, :]).then_inc(digits, 1)
            dve.wait_ge(digits, 4)
            dve.scalar_tensor_tensor(lo[:, :], hi[:, :], -float(NCOL), dst0_i[:, :], ALU.mult, ALU.add) \
               .then_inc(digits, 1)
            dve.wait_ge(digits, 5)
            dve.tensor_scalar(fix[:, :], lo[:, :], 0.0, None, ALU.is_lt).then_inc(digits, 1)
            dve.wait_ge(digits, 6)
            dve.tensor_tensor(hi[:, :], hi[:, :], fix[:, :], ALU.subtract).then_inc(digits, 1)
            dve.scalar_tensor_tensor(lo[:, :], fix[:, :], float(NCOL), lo[:, :], ALU.mult, ALU.add) \
               .then_inc(digits, 1)
            dve.wait_ge(digits, 8)
            dve.tensor_scalar(fix[:, :], lo[:, :], float(NCOL), None, ALU.is_ge).then_inc(digits, 1)
            dve.wait_ge(digits, 9)
            dve.tensor_tensor(hi[:, :], hi[:, :], fix[:, :], ALU.add).then_inc(digits, 1)
            dve.scalar_tensor_tensor(lo[:, :], fix[:, :], -float(NCOL), lo[:, :], ALU.mult, ALU.add) \
               .then_inc(digits, 1)
            dve.wait_ge(digits, 11)

            dve.wait_ge(disorder_sum, 1)
            dve.tensor_copy(unsorted[:, :], ps_root[0:1, 0:1]).then_inc(flag_ready, 1)

            dve.tensor_scalar(half_lo[:, :], lo[:, :], -1.0, 0.5, ALU.mult, ALU.add).then_inc(digits, 1)

            def count_tiles(a, t, used):
                if used is not None:
                    dve.wait_ge(hot_used, used)
                dve.tensor_tensor(hot[:, a:a + HIST_HOT, :], over_rows(iota_hi[:, :], HIST_HOT, P),
                                  over_last(hi[:, bass.ds(t, HIST_HOT)], P), ALU.is_equal).then_inc(steps_ready, 1)
                for s in range(HIST_HOT):
                    if a + s not in HIST_ACT:
                        dve.tensor_scalar(steps[a + s], iota_lo[:, :], lo[:, bass.ds(t + s, 1)], 2.0,
                                          ALU.is_ge, ALU.mult).then_inc(steps_ready, 1)

            for a in range(0, HIST, HIST_HOT):
                count_tiles(a, a, None)
            with dve.Fori(1, T // HIST) as g:
                for a in range(0, HIST, HIST_HOT):
                    count_tiles(a, g * HIST + a, g * HIST + a - (HIST - HIST_HOT))

            dve.wait_ge(hot_used, T)
            dve.tensor_scalar(halves[0:NPART, :], ps_root[0:NPART, 8:9], 0.5, None, ALU.mult).then_inc(last_step, 1)
            dve.wait_ge(last_step, 1)
            dve.scalar_tensor_tensor(total[0:NPART, :], ps_hist[0:NPART, 512 + NCOL // 2 - 1:512 + NCOL // 2], 0.5,
                                     halves[0:NPART, :], ALU.mult, ALU.add).then_inc(total_ready, 1)
            dve.wait_ge(base_ready, 1)
            dve.tensor_copy(ends[:, 0:1], ps_root[0:NPART, 0:1]).then_inc(last_step, 1)
            dve.wait_ge(last_step, 2)
            dve.tensor_tensor(halves[0:NPART, :], halves[0:NPART, :], ends[:, 0:1], ALU.add).then_inc(last_step, 1)
            dve.wait_ge(last_step, 3)
            dve.wait_ge(x_placed[0], DCHUNKS // 2)
            dve.wait_ge(x_placed[1], DCHUNKS // 2)
            for h in range(2):
                a, b, done = h * NCOL // 2, (h + 1) * NCOL // 2, HALF_STEPS * h + 3
                dve.tensor_scalar(ends[:, 1 + a:1 + b], ps_hist[0:NPART, 512 * h:512 * h + NCOL // 2], 0.5,
                                  halves[0:NPART, 0:1], ALU.mult, ALU.add).then_inc(last_step, 1)
                dve.wait_ge(last_step, done + 1)
                dve.tensor_tensor(count_step[:, a:b], ends[:, 1 + a:1 + b], ends[:, a:b], ALU.subtract) \
                   .then_inc(last_step, 1)
                dve.tensor_scalar(last_edge[:, a:b], ends[:, 1 + a:1 + b], part[0:NPART, 2:3], 1.0,
                                  ALU.subtract, ALU.subtract).then_inc(last_step, 1)
                dve.wait_ge(last_step, done + 3)
                dve.scalar_tensor_tensor(last_edge[:, a:b], count_step[:, a:b], 0.0, last_edge[:, a:b],
                                         ALU.is_gt, ALU.mult).then_inc(last_step, 1)
                dve.wait_ge(last_step, done + 4)
                dve.tensor_scalar(xl[:, a:b, FEAT], last_edge[:, a:b], part[0:NPART, 2:3], None, ALU.add) \
                   .then_inc(last_step, 1)

            with dve.If(dve.value_load(unsorted[0:1, 0:1], min_val=0, max_val=EP)):
                dve.tensor_copy(lo[:, :], dst0_i[:, :]).then_inc(sort_step, 1)
                dve.tensor_scalar(before[:, :], iota_hi[:, :], part[:, 0:1], None, ALU.is_lt).then_inc(sort_step, 1)
                dve.memset(hi[:, :], 0.0).then_inc(sort_step, 1)
                dve.tensor_copy(run_up[:, :], iota_lo[:, 0:T]).then_inc(sort_step, 1)
                dve.wait_ge(sort_step, 4)
                with dve.Fori(0, SORT_CHUNKS) as c:
                    dve.wait_ge(sort_row_in, 16 * (c + 1))
                    dve.scalar_tensor_tensor(sort_low.rearrange("p (q t) -> p q t", t=T),
                                             over_last(before[:, bass.ds(c * SORT_PARTS, SORT_PARTS)], T), -0.5,
                                             sort_row.rearrange("p (q t) -> p q t", t=T), ALU.mult, ALU.add) \
                       .then_inc(sort_read, 1)
                    with dve.Fori(0, T) as t:
                        dve.wait_ge(sort_read, c + 1)
                        dve.tensor_scalar(sort_less, sort_low, lo[:, bass.ds(t, 1)], None, ALU.is_lt) \
                           .then_inc(sort_cmp, 1)
                        dve.wait_ge(sort_cmp, c * (2 * T + 1) + 2 * t + 1)
                        dve.tensor_reduce(fix[:, bass.ds(t, 1)], sort_less, AX.X, ALU.add).then_inc(sort_cmp, 1)
                        dve.wait_ge(sort_cmp, c * (2 * T + 1) + 2 * t + 2)
                    dve.tensor_tensor(hi[:, :], hi[:, :], fix[:, :], ALU.add).then_inc(sort_cmp, 1)
                    dve.wait_ge(sort_cmp, (c + 1) * (2 * T + 1))
                ranked_from = SORT_CHUNKS * (2 * T + 1)
                with dve.Fori(0, T) as t:
                    dve.tensor_scalar(run_down[:, :], lo[:, :], lo[:, bass.ds(t, 1)], None, ALU.is_equal) \
                       .then_inc(sort_cmp, 1)
                    dve.wait_ge(sort_cmp, 3 * t + (ranked_from + 1))
                    dve.scalar_tensor_tensor(first_run[:, :], run_up[:, :], run_up[:, bass.ds(t, 1)], run_down[:, :],
                                             ALU.is_lt, ALU.mult).then_inc(sort_cmp, 1)
                    dve.wait_ge(sort_cmp, 3 * t + (ranked_from + 2))
                    dve.tensor_reduce(fix[:, bass.ds(t, 1)], first_run[:, :], AX.X, ALU.add).then_inc(sort_cmp, 1)
                    dve.wait_ge(sort_cmp, 3 * t + (ranked_from + 3))
                dve.tensor_tensor(cur_i[:, :], hi[:, :], fix[:, :], ALU.add).then_inc(sort_step, 1)
                dve.wait_ge(sort_step, 5)
                dve.tensor_scalar(node_row[:, :], cur_i[:, :], 1.0, None, ALU.add).then_inc(sort_ranked, 1)

            steps_done = 0

            def step(ins):
                nonlocal steps_done
                steps_done += 1
                ins.then_inc(prep, 1)
                return steps_done

            dve.wait_ge(edges_in, 64)
            step(dve.tensor_tensor(same[:, :], cur_i[:, :], prev_i[:, :], ALU.is_equal))
            n = step(dve.tensor_tensor(same_next[:, :], cur_i[:, :], next_i[:, :], ALU.is_equal))
            dve.wait_ge(prep, n)
            step(dve.tensor_tensor_scan(run_up[:, :], same[:, :], ones_t[:, :], 0.0, ALU.mult, ALU.add))
            step(dve.tensor_tensor_scan(back(run_down[:, :]), back(same_next[:, :]), ones_t[:, :], 0.0,
                                        ALU.mult, ALU.add))
            step(dve.tensor_tensor_scan(first_run[:, :], same[:, :], ones_t[:, :], 1.0, ALU.mult, ALU.mult))
            n = step(dve.tensor_tensor_scan(back(last_run[:, :]), back(same_next[:, :]), ones_t[:, :], 1.0,
                                            ALU.mult, ALU.mult))
            dve.wait_ge(prep, n)
            step(dve.tensor_copy(whole[:, 0:1], first_run[:, T - 1:T]))
            n = step(dve.tensor_copy(whole[:, 1:2], last_run[:, 0:1]))
            dve.wait_ge(prep, n)
            dve.tensor_copy(whole32[:, :, :], over_last(whole[:, :], HID)).then_inc(turn_ready, 1)
            dve.wait_ge(turn_done, 1)
            n = step(dve.tensor_copy(whole_rows[:, :, :], ps_turn[0:HID, 0:2 * P].rearrange("p (d q) -> p d q", d=2)))
            dve.wait_ge(prep, n)

            def bring_along(n):
                dve.wait_ge(row_turned, n + 1)
                dve.tensor_copy(tail_row[:, :], ps_root[0:HID, 0:P]).then_inc(row_copied, 1)
                dve.wait_ge(row_copied, n + 1)
                if CARRIES[n] == 0:
                    dve.tensor_tensor_scan(carry_out[:, 1:P + 1], whole_rows[:, 0, :], tail_row[:, :], 0.0,
                                           ALU.mult, ALU.add).then_inc(scan_ready, 1)
                else:
                    dve.tensor_tensor_scan(back(carry_out[:, 0:P]), back(whole_rows[:, 1, :]), back(tail_row[:, :]),
                                           0.0, ALU.mult, ALU.add).then_inc(scan_ready, 1)
                dve.wait_ge(back_done, n + 1)

            def clear_end(n):
                at = 0 if CARRIES[n] == 0 else P
                return dve.memset(carry_out[:, at:at + 1], 0.0)

            for n, (of, at) in enumerate(((run_up, T - 1), (run_down, 0))):
                m = step(clear_end(n))
                dve.wait_ge(prep, m)
                dve.tensor_copy(tail[:, 0:1], of[:, at:at + 1]).then_inc(row_ready, 1)
                bring_along(n)
                m = step(dve.tensor_copy(carry[n][:, :], ps_root[:, 256:256 + HID]))
                dve.wait_ge(prep, m)
            step(dve.tensor_tensor_scan(run_up[:, :], same[:, :], ones_t[:, :], carry[0][:, 0:1], ALU.mult, ALU.add))
            n = step(dve.tensor_tensor_scan(back(run_down[:, :]), back(same_next[:, :]), ones_t[:, :],
                                            carry[1][:, 0:1], ALU.mult, ALU.add))
            dve.wait_ge(prep, n)
            n = step(dve.tensor_tensor(inv_count[:, :], run_up[:, :], run_down[:, :], ALU.add))
            dve.wait_ge(prep, n)
            n = step(dve.tensor_scalar(inv_count[:, :], inv_count[:, :], -1.0, 1.0, ALU.add, ALU.max))
            dve.wait_ge(prep, n)
            n = step(dve.reciprocal(inv_count[:, :], inv_count[:, :]))
            dve.wait_ge(prep, n)

            n = step(dve.tensor_tensor(fix[:, :], dump_row[:, :], cur_i[:, :], ALU.subtract))
            dve.wait_ge(prep, n)
            n = step(dve.tensor_tensor(fix[:, :], fix[:, :], same_next[:, :], ALU.mult))
            dve.wait_ge(prep, n)
            n = step(dve.tensor_tensor(node_row[:, :], fix[:, :], cur_i[:, :], ALU.add))
            step(dve.tensor_reduce(small[:, 0:1], first_run[:, :], AX.X, ALU.add))
            n = step(dve.tensor_copy(small[:, 4:5], cur_i[:, 0:1]))
            dve.wait_ge(prep, n)
            step(dve.tensor_scalar(small[:, 1:2], small[:, 0:1], -1.0, 0.0, ALU.add, ALU.max))
            step(dve.tensor_tensor(small[:, 3:4], whole[:, 0:1], same_next[:, T - 1:T], ALU.mult))
            n = step(dve.tensor_tensor(small[:, 5:6], part[:, 3:4], small[:, 4:5], ALU.subtract))
            dve.wait_ge(prep, n)
            step(dve.tensor_tensor(carry_row[:, :], small[:, 1:2], part[:, 1:2], ALU.add))
            n = step(dve.scalar_tensor_tensor(small[:, 7:8], small[:, 3:4], 1.0, same[:, 0:1], ALU.add, ALU.subtract))
            dve.wait_ge(prep, n)
            n = step(dve.tensor_tensor(small[:, 6:7], small[:, 5:6], small[:, 7:8], ALU.mult))
            dve.wait_ge(prep, n)
            dve.tensor_tensor(carry_node[:, :], small[:, 6:7], small[:, 4:5], ALU.add).then_inc(prep_done, 1)

            PARTS = {id(L0): 5, id(L1): 2, id(L2): 6}

            m = step(dve.tensor_tensor(rel[:, :, :], over_last(typ_i[:, :], REL), over_rows(eight[:, :], T, REL),
                                       ALU.is_equal))
            dve.wait_ge(prep, m)
            m = step(clear_end(2))
            dve.wait_ge(prep, m)
            for r in range(REL):
                m = step(dve.tensor_tensor_scan(run_up[:, :], same[:, :], rel[:, :, r], 0.0, ALU.mult, ALU.add))
                dve.wait_ge(prep, m)
                ins = dve.tensor_copy(tail[:, r:r + 1], run_up[:, T - 1:T])
                if r == REL - 1:
                    ins.then_inc(row_ready, 1)
                else:
                    m = step(ins)
                    dve.wait_ge(prep, m)
            for r in range(REL):
                m = step(dve.tensor_tensor_scan(back(run_down[:, :]), back(same_next[:, :]), back(rel[:, :, r]), 0.0,
                                                ALU.mult, ALU.add))
                dve.wait_ge(prep, m)
                m = step(dve.tensor_copy(heads[:, r:r + 1], run_down[:, 0:1]))
                dve.wait_ge(prep, m)
            bring_along(2)
            m = step(dve.tensor_copy(up8[:, :], ps_root[:, 256:256 + REL]))
            m = step(clear_end(3))
            dve.wait_ge(prep, m)
            dve.tensor_copy(tail[:, 0:REL], heads[:, :]).then_inc(row_ready, 1)
            bring_along(3)
            m = step(dve.tensor_copy(down8[:, :], ps_root[:, 256:256 + REL]))
            dve.wait_ge(prep, m)

            def run_sums(layer, j, i, f):
                k, parts = i * 2 + j, PARTS[id(layer)]
                dve.wait_ge(layer["scan"][1 - j], i + j)
                dve.tensor_copy(part_sum[j][:, 0:f, 0:1], scanned[1 - j][:, 0:f, K:K + 1]).then_inc(layer["reduced"], 1)
                dve.wait_ge(layer["mask"][j], i + 1)
                dve.wait_ge(layer["reduced"], parts * k + parts)
                dve.tensor_tensor_scan(scanned[j][:, 0:f, :].rearrange("p f k -> p (f k)"),
                                       keep[j][:, 0:f, :].rearrange("p f k -> p (f k)"),
                                       part_sum[j][:, 0:f, :].rearrange("p f k -> p (f k)"),
                                       0.0, ALU.mult, ALU.add).then_inc(layer["scan"][j], 1)

            def sums_out(layer, j, i, f, b0):
                dve.wait_ge(layer["scan"][j], i + 1)
                dve.wait_ge(layer["stored"][j], (16 if layer is not L2 else GOT) * i)
                if layer is L2:
                    to = node_rows[j][:, :, FEAT + HID:]
                else:
                    to = rows[j][:, 0:K * f].rearrange("p (k f) -> p k f", k=K)
                dve.tensor_tensor(to, scanned[j][:, 0:f, 1:].rearrange("p f k -> p k f"),
                                  over_rows(bias_row[:, b0:b0 + f], K, f), ALU.add).then_inc(layer["rows"][j], 1)

            def messages(layer, j, i, a, b, scale_of):
                k, parts = i * 2 + j, PARTS[id(layer)]

                def scale(g):
                    n = group_tiles(g)
                    if g >= 2:
                        dve.wait_ge(layer["reduced"], parts * k + g - 1)
                    dve.wait_ge(layer["msg"], 4 * k + g + 1)
                    dve.tensor_tensor(prod[g % 2][:, 0:n * a * b].rearrange("p (t a b) -> p t a b", t=n, a=a),
                                      ps_msg[g % 2][:, 0:n * a * b].rearrange("p (t a b) -> p t a b", t=n, a=a),
                                      over_last(scale_of(g, n), b), ALU.mult).then_inc(layer["mult"][g % 2], 1)

                def add(g):
                    n = group_tiles(g)
                    dve.wait_ge(layer["mult"][g % 2], 2 * k + g // 2 + 1)
                    dve.tensor_reduce(part_sum[j][:, 0:b, 1 + 4 * g:1 + 4 * g + n].rearrange("p b t -> p t b"),
                                      prod[g % 2][:, 0:n * a * b].rearrange("p (t a b) -> p t b a", t=n, a=a),
                                      AX.X, ALU.add).then_inc(layer["reduced"], 1)

                scale(0)
                for g in range(1, GROUPS):
                    scale(g)
                    add(g - 1)
                add(GROUPS - 1)

            def layer0(j, i):
                k = i * 2 + j
                dve.wait_ge(L0["got"][j], GOT * (i + 1))
                dve.tensor_tensor(xc[:, :, :], got0[j][:, :, 0:FEAT], over_last(inv_count[:, chunk(k)], FEAT),
                                  ALU.mult).then_inc(L0["scaled"][j], 1)
                dve.wait_ge(L0["scaled"][j], i + 1)
                messages(L0, j, i, FEAT, FEAT, lambda g, n: xc[:, 4 * g:4 * g + n, :])
                run_sums(L0, j, i, FEAT)
                sums_out(L0, j, i, FEAT, 0)

            def relation_counts(rs):
                for r in rs:
                    step(dve.tensor_tensor_scan(run_up[:, :], same[:, :], rel[:, :, r], up8[:, r:r + 1],
                                                ALU.mult, ALU.add))
                    m = step(dve.tensor_tensor_scan(back(run_down[:, :]), back(same_next[:, :]), back(rel[:, :, r]),
                                                    down8[:, r:r + 1], ALU.mult, ALU.add))
                    dve.wait_ge(prep, m)
                    m = step(dve.tensor_tensor(fix[:, :], run_up[:, :], run_down[:, :], ALU.add))
                    dve.wait_ge(prep, m)
                    to = first_run if r == 0 else last_run
                    m = step(dve.tensor_tensor(to[:, :], fix[:, :], rel[:, :, r], ALU.mult))
                    dve.wait_ge(prep, m)
                    if r:
                        m = step(dve.tensor_tensor(first_run[:, :], first_run[:, :], last_run[:, :], ALU.add))
                        dve.wait_ge(prep, m)

            ends_of = [HALF * n // 5 for n in range(6)]
            for n in range(5):
                with dve.Fori(ends_of[n], ends_of[n + 1]) as i:
                    layer0(0, i)
                    layer0(1, i)
                if n < 4:
                    relation_counts((2 * n, 2 * n + 1))
                if n == 3:
                    m = step(dve.tensor_scalar(first_run[:, :], first_run[:, :], -1.0, 1.0, ALU.add, ALU.max))
                    dve.wait_ge(prep, m)
                    m = step(dve.reciprocal(inv_rel[:, :], first_run[:, :]))
                    dve.wait_ge(prep, m)

            def sum_carry(n, layer, f, to):
                dve.wait_ge(layer["scan"][1], HALF)
                m = step(clear_end(n))
                dve.wait_ge(prep, m)
                dve.tensor_copy(tail[:, 0:f], scanned[1][:, 0:f, K]).then_inc(row_ready, 1)
                bring_along(n)
                dve.tensor_scalar(to, ps_root[:, 256:256 + f], same[:, 0:1], None, ALU.mult).then_inc(carry_ready, 1)

            sum_carry(4, L0, FEAT, carry[0][:, 0:FEAT])

            dve.wait_ge(L0["scan"][1], HALF)
            m = step(dve.memset(scanned[1][:, :, :], 0.0))
            dve.wait_ge(prep, m)

            def x1_sums(j, i):
                k = i * 2 + j
                above(dve, L1["x1"], k)
                dve.wait_ge(L1["got"][j], GOT * (i + 1))
                dve.tensor_tensor(cen[:, :, :], x_src[:, chunk(k), :], got1[j][:, :, :], ALU.add) \
                   .then_inc(L1["sum"][j], 1)
                dve.wait_ge(L1["sum"][j], i + 1)
                dve.tensor_reduce(stat[:, 0, :], cen[:, :, :], AX.X, ALU.add).then_inc(L1["stat"], 1)
                dve.wait_ge(L1["stat"], 3 * k + 1)
                dve.scalar_tensor_tensor(cen[:, :, :], over_last(stat[:, 0, :], FEAT), -1.0 / FEAT, cen[:, :, :],
                                         ALU.mult, ALU.add).then_inc(L1["stat"], 1)

            def x1_squares(j, i):
                k = i * 2 + j
                dve.wait_ge(L1["squared"], k + 1)
                dve.tensor_reduce(stat[:, 1, :], sq[:, :, :], AX.X, ALU.add).then_inc(L1["stat"], 1)

            def x1_rows(j, i):
                k = i * 2 + j
                dve.wait_ge(L1["std"], k + 1)
                dve.reciprocal(stat[:, 3, :], stat[:, 2, :]).then_inc(L1["inv"], 1)
                dve.wait_ge(L1["inv"], k + 1)
                dve.tensor_tensor(xc[:, :, :], cen[:, :, :], over_last(stat[:, 3, :], FEAT), ALU.mult) \
                   .then_inc(L1["x1"], 1)
                dve.wait_ge(L1["x1"], k + 1)
                above(dve, L1["turned"], 4 * k)
                for g in range(GROUPS):
                    a, n = 4 * g, group_tiles(g)
                    dve.tensor_tensor(outer[:, a:a + n, :, :], over_last(rel[:, bass.ds(k * K + a, n), :], FEAT),
                                      xc[:, a:a + n, :].unsqueeze(2).to_broadcast([P, n, REL, FEAT]), ALU.mult) \
                       .then_inc(L1["outer"], 1)

            def layer1(j, i, ahead):
                k, nxt = i * 2 + j, (1 - j, i + j)
                if ahead:
                    x1_sums(*nxt)
                dve.wait_ge(L1["msg"], 4 * k + 4)
                dve.tensor_tensor(part_sum[j][:, :, 1:].rearrange("p f k -> p k f"),
                                  ps_msg[j][:, 0:K * 2 * HID].rearrange("p (k f) -> p k f", k=K)[:, :, 0:HID],
                                  over_last(inv_rel[:, chunk(k)], HID), ALU.mult).then_inc(L1["reduced"], 1)
                if ahead:
                    x1_squares(*nxt)
                run_sums(L1, j, i, HID)
                if ahead:
                    x1_rows(*nxt)
                sums_out(L1, j, i, HID, FEAT)

            x1_sums(0, 0)
            x1_squares(0, 0)
            x1_rows(0, 0)
            dve.wait_ge(L0["stored"][0], 16 * HALF)
            dve.wait_ge(L0["stored"][1], 16 * HALF)
            with dve.Fori(0, HALF - 1) as i:
                layer1(0, i, True)
                layer1(1, i, True)
            layer1(0, HALF - 1, True)
            layer1(1, HALF - 1, False)
            dve.wait_ge(carry_added, 16)
            sum_carry(5, L1, HID, carry[0][:, :])
            m = step(dve.memset(scanned[1][:, :, :], 0.0))
            dve.wait_ge(prep, m)

            def layer2(j, i):
                k = i * 2 + j
                dve.wait_ge(L2["padded"][1 - j], i + j)
                dve.wait_ge(L2["got"][j], GOT * (i + 1))
                dve.tensor_tensor(hsum[:, :, :], u_src[:, chunk(k), :], got2[j][:, :, :], ALU.add) \
                   .then_inc(L2["sum"][j], 1)
                messages(L2, j, i, REL, FEAT, lambda g, n: rel[:, bass.ds(k * K + 4 * g, n), :])
                sums = part_sum[j][:, 0:FEAT, 1:].rearrange("p f k -> p k f")
                dve.wait_ge(L2["reduced"], 6 * k + 4)
                dve.tensor_tensor(sums, sums, over_last(inv_rel[:, chunk(k)], FEAT), ALU.mult).then_inc(L2["reduced"], 1)
                run_sums(L2, j, i, FEAT)
                sums_out(L2, j, i, FEAT, FEAT + HID)

            with dve.Fori(0, HALF) as i:
                layer2(0, i)
                layer2(1, i)
            sum_carry(6, L2, FEAT, carry64[:, FEAT + HID:])

            def hidden(k, s, g):
                if not isinstance(k, int) or 1 <= k <= DCHUNKS:
                    n = min(16, DC - 16 * g)
                    above(dve, D["h_mm"], 3 * (k - 1) + g + 1)
                    above(dve, D["ht"], 3 * (k - 2) + g + 1)
                    dve.tensor_tensor(hn[:, 16 * g:16 * g + n, :],
                                      ps_h[g][0:NPART, 0:n * HID].rearrange("p (c f) -> p c f", f=HID),
                                      nr[(s + 3) % 4][:, 16 * g:16 * g + n, FEAT:FEAT + HID],
                                      ALU.add).then_inc(D["h"], 1)

            def nodes(k, s, u):
                static = isinstance(k, int)
                first = not static or k < DCHUNKS
                second = not static or 3 <= k < DCHUNKS + 3
                third = not static or 4 <= k < DCHUNKS + 4
                if first:
                    above(dve, D["v"], k + 1)
                    dve.tensor_reduce(dst_["1sum"], vv[s % 2], AX.X, ALU.add).then_inc(D["stat1"], 1)
                if first:
                    above(dve, D["q1"], k - 1)
                    above(dve, D["stat1"], 2 * k + 1)
                    dve.scalar_tensor_tensor(cc1[s % 2], over_last(dst_["1sum"], FEAT), -1.0 / FEAT, vv[s % 2],
                                             ALU.mult, ALU.add).then_inc(D["center1"], 1)
                if second:
                    above(dve, D["z"], k - 2)
                    above(dve, D["y"], k - 2)
                    above(dve, D["center2"], k - 3)
                    dve.tensor_tensor(ww, ps_y.rearrange("p (c f) -> p c f", f=FEAT),
                                      zz[(s + 1) % 2], ALU.add).then_inc(D["w"], 1)
                if third:
                    above(dve, D["q2"], k - 3)
                    dve.tensor_reduce(dst_["2ss"], qq[1], AX.X, ALU.add).then_inc(D["ss2"], 1)
                if first:
                    above(dve, D["q1"], k + 1)
                    dve.tensor_reduce(dst_["1ss"], qq[0], AX.X, ALU.add).then_inc(D["ss1"], 1)
                if second:
                    above(dve, D["w"], k - 2)
                    dve.tensor_reduce(dst_["2sum"], ww, AX.X, ALU.add).then_inc(D["sum2"], 1)
                if third:
                    above(dve, D["std2"], k - 3)
                    above(dve, D["result"], k - 4)
                    dve.reciprocal(inv2[s % 2], dst_["2dev"]).then_inc(D["inv2"], 1)
                if first:
                    above(dve, D["std1"], k + 1)
                    dve.reciprocal(dst_["1inv"], dst_["1dev"]).then_inc(D["stat1"], 1)
                    above(dve, D["stat1"], 2 * k + 2)
                    above(dve, D["x1t"], 2 * (k - 1))
                    above(dve, D["z"], k - 1)
                    dve.tensor_tensor(x1n[s % 2], cc1[s % 2], over_last(dst_["1inv"], FEAT), ALU.mult) \
                       .then_inc(D["x1"], 1)
                hidden(k, s, 0)
                hidden(k, s, 1)
                if second:
                    above(dve, D["sum2"], k - 2)
                    above(dve, D["result"], k - 4)
                    dve.scalar_tensor_tensor(cc2[(s + 1) % 2], over_last(dst_["2sum"], FEAT), -1.0 / FEAT, ww,
                                             ALU.mult, ALU.add).then_inc(D["center2"], 1)
                hidden(k, s, 2)

            over_chunks(dve, nodes, 4)


_INS = ["x", "src", "dst", "edge_attr_16", "edge_type_8", "L0_gnn_W_e", "L0_gnn_b_e", "L0_gnn_bias",
        "L1_gnn_W1", "L1_gnn_root1", "L1_gnn_b1", "L1_gnn_W2", "L1_gnn_root2", "L1_gnn_b2"]


def kernel(**inputs):
    import concourse.bacc as bacc
    from concourse.bass_utils import run_bass_kernel_spmd

    nc = bacc.Bacc("TRN2", target_bir_lowering=False, num_devices=1)
    arrays, args = {}, []
    for name in _INS:
        a = np.ascontiguousarray(inputs[name])
        arrays[f"in_{name}"] = a
        args.append(nc.dram_tensor(f"in_{name}", a.shape, mybir.dt.from_np(a.dtype), kind="ExternalInput").ap())
    out = nc.dram_tensor("out", inputs["x"].shape, F32, kind="ExternalOutput").ap()
    bass_gnn_resnorm(nc, *args, out)
    r = run_bass_kernel_spmd(nc, [arrays], core_ids=[0])
    return r.results[0]["out"]
```
